# Optimizing a Trainium2 kernel written in Bass

```python
import numpy as np
import jax
import jax.numpy as jnp

def _softmax(x, axis=-1):
    return jax.nn.softmax(x, axis=axis)
def _gelu(x):
    return jax.nn.gelu(x, approximate=True)
def _silu(x):
    return jax.nn.silu(x)
def _sigmoid(x):
    return jax.nn.sigmoid(x)
def _layernorm(x, axis=-1, eps=1e-5):
    m = jnp.mean(x, axis=axis, keepdims=True)
    v = jnp.var(x, axis=axis, keepdims=True)
    return (x - m) / jnp.sqrt(v + eps)
def _scatter_add(tgt, idx, src, axis=0):
    return tgt.at[idx].add(src)
def _segment_sum(src, seg, n):
    return jax.ops.segment_sum(src, seg, n)

kernel_name = 'mk_dlrm_tower_d1_rec_b734ad'

def setup_inputs(seed: int = 0):
    np.random.seed(seed)
    _w = jnp.asarray
    def _rec_inputs():
        import jax
        import jax.numpy as jnp
        _tk = jax.random.key(seed)
        ids = jnp.stack([jax.random.randint(jax.random.fold_in(_tk, 200 + f), (1024,), 0, v, jnp.int32) for f, v in enumerate([10000, 10000, 1000000, 1000])], axis=1)
        tbl_0 = 0.05 * jax.random.normal(jax.random.fold_in(_tk, 500 + 0), (10000, 4), jnp.float32)
        tbl_1 = 0.05 * jax.random.normal(jax.random.fold_in(_tk, 500 + 1), (10000, 4), jnp.float32)
        tbl_2 = 0.05 * jax.random.normal(jax.random.fold_in(_tk, 500 + 2), (1000000, 4), jnp.float32)
        tbl_3 = 0.05 * jax.random.normal(jax.random.fold_in(_tk, 500 + 3), (1000, 4), jnp.float32)
        _rk = jax.random.fold_in(_tk, 7)
        r_x = 7.22013e-05 + 1.00017 * jax.random.normal(jax.random.fold_in(_rk, 101), (1024, 2048), jnp.float32)
        W_top1 = 0.0197642 * jax.random.normal(jax.random.fold_in(_tk, 801), (2560, 512), jnp.float32)
        W_top2 = 0.0441942 * jax.random.normal(jax.random.fold_in(_tk, 802), (512, 256), jnp.float32)
        W_top3 = 0.0625 * jax.random.normal(jax.random.fold_in(_tk, 803), (256, 1), jnp.float32)
        b_top1 = jnp.zeros((512,), jnp.float32)
        b_top2 = jnp.zeros((256,), jnp.float32)
        return r_x, ids, tbl_0, tbl_1, tbl_2, tbl_3, W_top1, b_top1, W_top2, b_top2, W_top3
    r_x, ids, tbl_0, tbl_1, tbl_2, tbl_3, W_top1, b_top1, W_top2, b_top2, W_top3 = _rec_inputs()
    def _L0_rec_setup():
        import jax, jax.numpy as jnp
        import numpy as np
        B, IN, HID, D, N, OUT = (4096, 2048, 2048, 512, 4, 512)
        H = 8
        HD = D // H

        def _ln(x, g, b):
            m = x.mean(-1, keepdims=True)
            v = ((x - m) ** 2).mean(-1, keepdims=True)
            return (x - m) / jnp.sqrt(v + 1e-05) * g + b
        key = jax.random.key(seed)
        ks = jax.random.split(key, 32)

        def nrm(k, shape, scale=0.02):
            return jax.random.normal(k, shape, jnp.float32) * scale
        inp = {}
        inp['x'] = jax.random.normal(ks[0], (B, IN), jnp.float32)
        inp['strength'] = jax.random.uniform(ks[1], (B, N, N), jnp.float32)
        for t, i in (('er', 2), ('ei', 4)):
            inp[t + '_W1'] = nrm(ks[i], (HID, IN))
            inp[t + '_b1'] = jnp.zeros((HID,), jnp.float32)
            inp[t + '_g1'] = jnp.ones((HID,), jnp.float32)
            inp[t + '_be1'] = jnp.zeros((HID,), jnp.float32)
            inp[t + '_W2'] = nrm(ks[i + 1], (N * D, HID))
            inp[t + '_b2'] = jnp.zeros((N * D,), jnp.float32)
        names = ['Wq_r', 'Wq_i', 'Wk_r', 'Wk_i', 'Wv_r', 'Wv_i', 'Wo_r', 'Wo_i']
        for j, nm in enumerate(names):
            inp[nm] = nrm(ks[6 + j], (D, D))
            inp['b' + nm[1:]] = jnp.zeros((D,), jnp.float32)
        inp['int_Wr'] = jnp.tile(jnp.eye(D, dtype=jnp.float32)[None], (N, 1, 1))
        inp['int_Wi'] = jnp.zeros((N, D, D), jnp.float32)
        inp['meas_Mr'] = nrm(ks[20], (OUT, D), 1.0 / np.sqrt(D))
        inp['meas_Mi'] = nrm(ks[21], (OUT, D), 1.0 / np.sqrt(D))
        inp['post_W'] = nrm(ks[22], (OUT, OUT))
        inp['post_b'] = jnp.zeros((OUT,), jnp.float32)
        inp['post_g'] = jnp.ones((OUT,), jnp.float32)
        inp['post_be'] = jnp.zeros((OUT,), jnp.float32)
        return inp
    _L0_rec_all = _L0_rec_setup()
    _L0_rec_in = {k: v for k, v in _L0_rec_all.items() if k in ('er_W1', 'er_b1', 'er_g1', 'er_be1', 'er_W2', 'er_b2', 'ei_W1', 'ei_b1', 'ei_g1', 'ei_be1', 'ei_W2', 'ei_b2', 'Wq_r', 'bq_r', 'Wq_i', 'bq_i', 'Wk_r', 'bk_r', 'Wk_i', 'bk_i', 'Wv_r', 'bv_r', 'Wv_i', 'bv_i', 'Wo_r', 'bo_r', 'Wo_i', 'bo_i', 'int_Wr', 'int_Wi', 'meas_Mr', 'meas_Mi', 'post_W', 'post_b', 'post_g', 'post_be', )}
    del _L0_rec_all

    return {
        "r_x": r_x,
        "ids": ids,
        "tbl_0": tbl_0,
        "tbl_1": tbl_1,
        "tbl_2": tbl_2,
        "tbl_3": tbl_3,
        "W_top1": W_top1,
        "b_top1": b_top1,
        "W_top2": W_top2,
        "b_top2": b_top2,
        "W_top3": W_top3,
        "L0_rec_er_W1": _L0_rec_in["er_W1"],
        "L0_rec_er_b1": _L0_rec_in["er_b1"],
        "L0_rec_er_g1": _L0_rec_in["er_g1"],
        "L0_rec_er_be1": _L0_rec_in["er_be1"],
        "L0_rec_er_W2": _L0_rec_in["er_W2"],
        "L0_rec_er_b2": _L0_rec_in["er_b2"],
        "L0_rec_ei_W1": _L0_rec_in["ei_W1"],
        "L0_rec_ei_b1": _L0_rec_in["ei_b1"],
        "L0_rec_ei_g1": _L0_rec_in["ei_g1"],
        "L0_rec_ei_be1": _L0_rec_in["ei_be1"],
        "L0_rec_ei_W2": _L0_rec_in["ei_W2"],
        "L0_rec_ei_b2": _L0_rec_in["ei_b2"],
        "L0_rec_Wq_r": _L0_rec_in["Wq_r"],
        "L0_rec_bq_r": _L0_rec_in["bq_r"],
        "L0_rec_Wq_i": _L0_rec_in["Wq_i"],
        "L0_rec_bq_i": _L0_rec_in["bq_i"],
        "L0_rec_Wk_r": _L0_rec_in["Wk_r"],
        "L0_rec_bk_r": _L0_rec_in["bk_r"],
        "L0_rec_Wk_i": _L0_rec_in["Wk_i"],
        "L0_rec_bk_i": _L0_rec_in["bk_i"],
        "L0_rec_Wv_r": _L0_rec_in["Wv_r"],
        "L0_rec_bv_r": _L0_rec_in["bv_r"],
        "L0_rec_Wv_i": _L0_rec_in["Wv_i"],
        "L0_rec_bv_i": _L0_rec_in["bv_i"],
        "L0_rec_Wo_r": _L0_rec_in["Wo_r"],
        "L0_rec_bo_r": _L0_rec_in["bo_r"],
        "L0_rec_Wo_i": _L0_rec_in["Wo_i"],
        "L0_rec_bo_i": _L0_rec_in["bo_i"],
        "L0_rec_int_Wr": _L0_rec_in["int_Wr"],
        "L0_rec_int_Wi": _L0_rec_in["int_Wi"],
        "L0_rec_meas_Mr": _L0_rec_in["meas_Mr"],
        "L0_rec_meas_Mi": _L0_rec_in["meas_Mi"],
        "L0_rec_post_W": _L0_rec_in["post_W"],
        "L0_rec_post_b": _L0_rec_in["post_b"],
        "L0_rec_post_g": _L0_rec_in["post_g"],
        "L0_rec_post_be": _L0_rec_in["post_be"],
    }

def reference(r_x, ids, tbl_0, tbl_1, tbl_2, tbl_3, W_top1, b_top1, W_top2, b_top2, W_top3, L0_rec_er_W1, L0_rec_er_b1, L0_rec_er_g1, L0_rec_er_be1, L0_rec_er_W2, L0_rec_er_b2, L0_rec_ei_W1, L0_rec_ei_b1, L0_rec_ei_g1, L0_rec_ei_be1, L0_rec_ei_W2, L0_rec_ei_b2, L0_rec_Wq_r, L0_rec_bq_r, L0_rec_Wq_i, L0_rec_bq_i, L0_rec_Wk_r, L0_rec_bk_r, L0_rec_Wk_i, L0_rec_bk_i, L0_rec_Wv_r, L0_rec_bv_r, L0_rec_Wv_i, L0_rec_bv_i, L0_rec_Wo_r, L0_rec_bo_r, L0_rec_Wo_i, L0_rec_bo_i, L0_rec_int_Wr, L0_rec_int_Wi, L0_rec_meas_Mr, L0_rec_meas_Mi, L0_rec_post_W, L0_rec_post_b, L0_rec_post_g, L0_rec_post_be):
    import jax
    import jax.numpy as jnp
    def _L0_rec_ref(x, strength, er_W1, er_b1, er_g1, er_be1, er_W2, er_b2, ei_W1, ei_b1, ei_g1, ei_be1, ei_W2, ei_b2, Wq_r, bq_r, Wq_i, bq_i, Wk_r, bk_r, Wk_i, bk_i, Wv_r, bv_r, Wv_i, bv_i, Wo_r, bo_r, Wo_i, bo_i, int_Wr, int_Wi, meas_Mr, meas_Mi, post_W, post_b, post_g, post_be):
        import jax, jax.numpy as jnp
        import numpy as np
        B, IN, HID, D, N, OUT = (4096, 2048, 2048, 512, 4, 512)
        H = 8
        HD = D // H

        def _ln(x, g, b):
            m = x.mean(-1, keepdims=True)
            v = ((x - m) ** 2).mean(-1, keepdims=True)
            return (x - m) / jnp.sqrt(v + 1e-05) * g + b
        Bsz = x.shape[0]

        def enc(W1, b1, g, be, W2, b2):
            h = jax.nn.gelu(_ln(x @ W1.T + b1, g, be), approximate=False)
            return (h @ W2.T + b2).reshape(Bsz, N, D)
        sr = enc(er_W1, er_b1, er_g1, er_be1, er_W2, er_b2)
        si = enc(ei_W1, ei_b1, ei_g1, ei_be1, ei_W2, ei_b2)

        def heads(t):
            return t.reshape(Bsz, N, H, HD).transpose(0, 2, 1, 3)
        qr = heads(sr @ Wq_r.T + bq_r)
        qi = heads(si @ Wq_i.T + bq_i)
        kr = heads(sr @ Wk_r.T + bk_r)
        ki = heads(si @ Wk_i.T + bk_i)
        vr = heads(sr @ Wv_r.T + bv_r)
        vi = heads(si @ Wv_i.T + bv_i)
        ar = jnp.einsum('bhnd,bhmd->bhnm', qr, kr) + jnp.einsum('bhnd,bhmd->bhnm', qi, ki)
        ai = jnp.einsum('bhnd,bhmd->bhnm', qi, kr) - jnp.einsum('bhnd,bhmd->bhnm', qr, ki)
        mag = jnp.sqrt(ar ** 2 + ai ** 2 + 1e-08) * HD ** (-0.5)
        w = jax.nn.softmax(mag, axis=-1)
        out_r = jnp.einsum('bhnm,bhmd->bhnd', w, vr).transpose(0, 2, 1, 3).reshape(Bsz, N, D)
        out_i = jnp.einsum('bhnm,bhmd->bhnd', w, vi).transpose(0, 2, 1, 3).reshape(Bsz, N, D)
        attn_r = out_r @ Wo_r.T + bo_r
        attn_i = out_i @ Wo_i.T + bo_i
        R = jnp.einsum('bnd,ned->bne', attn_r, int_Wr) - jnp.einsum('bnd,ned->bne', attn_i, int_Wi)
        I = jnp.einsum('bnd,ned->bne', attn_r, int_Wi) + jnp.einsum('bnd,ned->bne', attn_i, int_Wr)
        Ri, Ii = (R[:, :, None, :], I[:, :, None, :])
        Rj, Ij = (R[:, None, :, :], I[:, None, :, :])
        phase = jnp.arctan2(Ii * Rj - Ri * Ij, Ri * Rj + Ii * Ij)
        f = jnp.cos(phase) * strength[..., None]
        sup_r = jnp.einsum('bijd,bjd->bd', f, R)
        sup_i = jnp.einsum('bijd,bjd->bd', f, I)
        norm = jnp.sqrt(jnp.sum(sup_r ** 2 + sup_i ** 2, axis=-1, keepdims=True) + 1e-08)
        sup_r = sup_r / norm
        sup_i = sup_i / norm
        mr = sup_r @ meas_Mr.T - sup_i @ meas_Mi.T
        mi = sup_r @ meas_Mi.T + sup_i @ meas_Mr.T
        amp = jnp.sqrt(mr ** 2 + mi ** 2)
        out = jax.nn.gelu(_ln(amp @ post_W.T + post_b, post_g, post_be), approximate=False)
        return out

    e = jnp.stack([tbl_0[ids[:, 0]], tbl_1[ids[:, 1]], tbl_2[ids[:, 2]], tbl_3[ids[:, 3]]], axis=1)
    z = _L0_rec_ref(r_x, e, L0_rec_er_W1, L0_rec_er_b1, L0_rec_er_g1, L0_rec_er_be1, L0_rec_er_W2, L0_rec_er_b2, L0_rec_ei_W1, L0_rec_ei_b1, L0_rec_ei_g1, L0_rec_ei_be1, L0_rec_ei_W2, L0_rec_ei_b2, L0_rec_Wq_r, L0_rec_bq_r, L0_rec_Wq_i, L0_rec_bq_i, L0_rec_Wk_r, L0_rec_bk_r, L0_rec_Wk_i, L0_rec_bk_i, L0_rec_Wv_r, L0_rec_bv_r, L0_rec_Wv_i, L0_rec_bv_i, L0_rec_Wo_r, L0_rec_bo_r, L0_rec_Wo_i, L0_rec_bo_i, L0_rec_int_Wr, L0_rec_int_Wi, L0_rec_meas_Mr, L0_rec_meas_Mi, L0_rec_post_W, L0_rec_post_b, L0_rec_post_g, L0_rec_post_be)
    z = z.reshape(z.shape[0], -1)
    h = jnp.concatenate([z, r_x], axis=1)
    h = jnp.maximum(h @ W_top1 + b_top1, 0.0)
    h = jnp.maximum(h @ W_top2 + b_top2, 0.0)
    y = h @ W_top3
    return y


_drawn_inputs = setup_inputs


def setup_inputs(seed=0):
    import zlib

    import numpy as np

    out = dict(_drawn_inputs(seed))
    spreads = {'b_top1': (0.0, 0.1),
     'b_top2': (0.0, 0.1),
     'L0_rec_er_b1': (0.0, 0.8),
     'L0_rec_er_g1': (1.0, 0.6),
     'L0_rec_er_be1': (0.0, 0.8),
     'L0_rec_er_b2': (0.0, 0.8),
     'L0_rec_ei_b1': (0.0, 0.8),
     'L0_rec_ei_g1': (1.0, 0.6),
     'L0_rec_ei_be1': (0.0, 0.8),
     'L0_rec_ei_b2': (0.0, 0.8),
     'L0_rec_bq_r': (0.0, 0.8),
     'L0_rec_bq_i': (0.0, 0.8),
     'L0_rec_bk_r': (0.0, 0.8),
     'L0_rec_bk_i': (0.0, 0.8),
     'L0_rec_bv_r': (0.0, 0.1),
     'L0_rec_bv_i': (0.0, 0.1),
     'L0_rec_bo_r': (0.0, 0.1),
     'L0_rec_bo_i': (0.0, 0.1),
     'L0_rec_int_Wi': (0.0, 0.1),
     'L0_rec_post_b': (0.0, 0.1),
     'L0_rec_post_g': (1.0, 0.2),
     'L0_rec_post_be': (0.0, 0.1)}
    factors = {'L0_rec_Wq_r': 8.0, 'L0_rec_Wq_i': 8.0, 'L0_rec_Wk_r': 8.0, 'L0_rec_Wk_i': 8.0}
    for name, (base, spread) in spreads.items():
        noise = np.random.default_rng([zlib.crc32(name.encode()), seed]).standard_normal(out[name].shape)
        drawn = base * np.exp(spread * noise) if base else spread * noise
        out[name] = jnp.asarray(drawn.astype(out[name].dtype))
    for name, factor in factors.items():
        out[name] = (out[name] * factor).astype(out[name].dtype)
    return out
```

```python
from contextlib import ExitStack

import numpy as np

import concourse.bass as bass
from concourse import mybir

F32 = mybir.dt.float32
F32R = mybir.dt.float32r
I32 = mybir.dt.int32
ALU = mybir.AluOpType
ACT = mybir.ActivationFunctionType
AX = mybir.AxisListType

P = 128
B = 1024
HID = 2048
D = 512
N = 4
HEADS = 8
HD = D // HEADS
KT = HID // P
KQ = 4
PIECES = KT // KQ
HALF = 512
LN_EPS = 1e-5
ENC_TILES = HID // P
TOP_TILES = D // P
L1_TILES = 2 * ENC_TILES + TOP_TILES
ALL_TILES = L1_TILES + 2 * ENC_TILES
JOBS = 4
PARTS = ((0, 0), (0, 1), (1, 0))


def encoders_phase(nc, t, scr):
    with ExitStack() as ctx:
        def sb(name, shape, dt=F32):
            return ctx.enter_context(nc.sbuf_tensor(name, shape, dt))

        def sem(name):
            return ctx.enter_context(nc.semaphore(name))

        mov = [sb("mov_hi", [P, KT, B], F32R), sb("mov_lo", [P, KT, B], F32R)]
        w_stage = sb("w_stage", [P, PIECES, KQ * P])
        w = [sb("w_hi", [P, PIECES, KQ * P], F32R), sb("w_lo", [P, PIECES, KQ * P], F32R)]
        out_sb = sb("out_sb", [P, 2, B])
        load_sb = sb("load_sb", [P, 2, B])
        gelu_sb = sb("gelu_sb", [P, 2, B])
        shift = sb("shift", [P, B])
        dev = sb("dev", [P, B])
        dev_sum = sb("dev_sum", [P, B])
        dev_sq = sb("dev_sq", [P, B])
        mean_bc = sb("mean_bc", [P, B])
        rstd_bc = sb("rstd_bc", [P, B])
        bias = sb("bias_cols", [P, ALL_TILES])
        ln_g = sb("ln_g", [P, 2 * ENC_TILES])
        ln_b = sb("ln_b", [P, 2 * ENC_TILES])
        averager = sb("averager", [P, P])
        eps = sb("eps", [P, 1])
        zeros = sb("zeros", [P, KQ * P])
        ps = ctx.enter_context(nc.psum_tensor("ps", [P, 2, B], F32))
        ps_mean = ctx.enter_context(nc.psum_tensor("ps_mean", [P, B], F32))
        ps_var = ctx.enter_context(nc.psum_tensor("ps_var", [P, B], F32))

        consts_loaded = sem("consts_loaded")
        consts_set = sem("consts_set")
        w_loaded = [sem(f"w_loaded{q}") for q in range(PIECES)]
        w_rounded = sem("w_rounded")
        w_split = sem("w_split")
        piece_used = sem("piece_used")
        loaded = [sem(f"loaded{j}") for j in range(2)]
        load_used = [sem(f"load_used{j}") for j in range(2)]
        hi_filled = sem("hi_filled")
        tile_out = sem("tile_out")
        stored = [sem(f"stored{j}") for j in range(2)]
        centred = sem("centred")
        squared = sem("squared")
        tile_summed = sem("tile_summed")
        ln_step = sem("ln_step")
        part_means = sem("part_means")
        mean_done = sem("mean_done")
        part_vars = sem("part_vars")
        var_done = sem("var_done")
        std_done = sem("std_done")
        z_centred = sem("z_centred")
        z_done = sem("z_done")
        gelu_stored = [sem(f"gelu_stored{j}") for j in range(2)]

        block = ctx.enter_context(nc.Block())

        FILLS = (0, 2 * KT, 4 * KT)
        NORMS = (KT, 3 * KT)
        ER1, EI1, TOP, ER2, EI2, END = 0, 8, 16, 18, 26, 34
        FILL_PAIRS = (ER1, ER2, EI2)
        NORM_PAIRS = (EI1 + 1, ER2 + 1)
        NORM_LEN = KT // JOBS

        @block.sync
        def _(sp):
            sp.dma_start(bias[:], t["enc_bias"]).then_inc(consts_loaded, 16)
            sp.dma_start(ln_g[:], t["ln_g"]).then_inc(consts_loaded, 16)
            sp.dma_start(ln_b[:], t["ln_b"]).then_inc(consts_loaded, 16)

            def weights(tile, first=False):
                for q in range(PIECES):
                    if not first:
                        sp.wait_ge(w_split, PIECES * (tile - 1) + q + 1)
                    sp.dma_start(w_stage[:, q, :], t["w_enc"][tile, :, q * KQ * P:(q + 1) * KQ * P]) \
                        .then_inc(w_loaded[q], 16)

            def load(source, number, half_number, first=False):
                j = number % 2
                if not first:
                    sp.wait_ge(load_used[j], half_number)
                sp.dma_start(load_sb[:, j, :], source).then_inc(loaded[j], 16)

            def fill(f, pair):
                weights(2 * pair, first=pair == 0)
                for k in range(KT):
                    if f > 0 and k == 0:
                        for j in range(2):
                            sp.wait_ge(gelu_stored[j], 16 * (KT // 2) * f)
                    source = t["x_t"][k] if f == 0 else scr["h"][KT * (f - 1) + k]
                    load(source, FILLS[f] + k, FILLS[f] // 2 + k // 2, first=f == 0 and k < 2)
                weights(2 * pair + 1)

            def norm(enc, start):
                for j in range(2):
                    sp.wait_ge(stored[j], 16 * (ENC_TILES // 2) * (enc + 1))
                with sp.Fori(start, start + NORM_LEN) as i:
                    weights(2 * i)
                    weights(2 * i + 1)
                    for c in range(JOBS):
                        load(scr["u"][ENC_TILES * enc + JOBS * (i - start) + c], c,
                             NORMS[enc] // 2 + JOBS // 2 * (i - start) + c // 2)

            def plain(start, end):
                with sp.Fori(start, end) as i:
                    weights(2 * i)
                    weights(2 * i + 1)

            fill(0, ER1)
            plain(ER1 + 1, NORM_PAIRS[0])
            norm(0, NORM_PAIRS[0])
            plain(NORM_PAIRS[0] + NORM_LEN, ER2)
            fill(1, ER2)
            norm(1, NORM_PAIRS[1])
            plain(NORM_PAIRS[1] + NORM_LEN, EI2)
            fill(2, EI2)
            plain(EI2 + 1, END)

        @block.gpsimd
        def _(pool):
            pool.memset(averager[:], 1.0 / P).then_inc(consts_set, 1)
            pool.memset(eps[:], LN_EPS).then_inc(consts_set, 1)
            pool.memset(zeros[:], 0.0).then_inc(consts_set, 1)
            pool.wait_ge(consts_set, 3)

            def split(tile, first=False):
                for q in range(PIECES):
                    pool.wait_ge(w_loaded[q], 16 * (tile + 1))
                    if not first:
                        pool.wait_ge(piece_used, PIECES * (tile - 1) + q + 1)
                    pool.tensor_tensor(w[0][:, q, :], w_stage[:, q, :], zeros[:], ALU.add) \
                        .then_inc(w_rounded, 1)
                    pool.wait_ge(w_rounded, PIECES * tile + q + 1)
                    pool.tensor_tensor(w[1][:, q, :], w_stage[:, q, :], w[0][:, q, :].bitcast(F32),
                                       ALU.subtract).then_inc(w_split, 1)

            split(0, first=True)
            with pool.Fori(1, ALL_TILES) as tile:
                split(tile)

        @block.tensor
        def _(pe):
            def tile_products(j, tile, fill=None):
                if not (isinstance(tile, int) and tile < 2):
                    pe.wait_ge(tile_out, tile - 1)
                for q in range(PIECES):
                    pe.wait_ge(w_split, PIECES * tile + q + 1)
                    for kk in range(KQ):
                        k = KQ * q + kk
                        if fill is not None:
                            pe.wait_ge(load_used[k % 2], (FILLS[fill] + k) // 2 + 1)
                        for wp, mp in PARTS:
                            for half in range(2):
                                last = pe.matmul(ps[:, j, half * HALF:(half + 1) * HALF],
                                                 w[wp][:, q, kk * P:(kk + 1) * P],
                                                 mov[mp][:, k, half * HALF:(half + 1) * HALF],
                                                 start=(k == 0 and (wp, mp) == PARTS[0]),
                                                 stop=(k == KT - 1 and (wp, mp) == PARTS[-1]))
                    last.then_inc(piece_used, 1)

            def pairs(start, end):
                with pe.Fori(start, end) as i:
                    for j in range(2):
                        tile_products(j, 2 * i + j)

            def average(enc, out, source, ready, done):
                pe.wait_ge(ready, enc + 1)
                for half in range(2):
                    cols = slice(half * HALF, (half + 1) * HALF)
                    last = pe.matmul(out[:, cols], averager[:], source[:, cols], start=True, stop=True)
                last.then_inc(done, 1)

            def pair_and_statistics(enc, pair):
                tile_products(0, 2 * pair)
                average(enc, ps_mean, mean_bc, part_means, mean_done)
                tile_products(1, 2 * pair + 1)
                average(enc, ps_var, rstd_bc, part_vars, var_done)

            def pair_filling(fill, pair):
                for j in range(2):
                    tile_products(j, 2 * pair + j, fill if j == 0 else None)

            pe.wait_ge(consts_set, 3)
            pair_filling(0, ER1)
            pairs(ER1 + 1, EI1)
            pair_and_statistics(0, EI1)
            pairs(EI1 + 1, TOP)
            pair_and_statistics(1, TOP)
            pairs(TOP + 1, ER2)
            pair_filling(1, ER2)
            pairs(ER2 + 1, EI2)
            pair_filling(2, EI2)
            pairs(EI2 + 1, END)

        @block.scalar
        def _(act):
            def out(j, tile, pair, first=False, summed=True):
                act.wait_ge(piece_used, PIECES * (tile + 1))
                if not first:
                    act.wait_ge(stored[j], 16 * pair)
                    if summed:
                        act.wait_ge(tile_summed, tile - 1)
                act.activation(out_sb[:, j, :], ps[:, j, :], ACT.Identity,
                               bias=bias[:, bass.ds(tile, 1)]).then_inc(tile_out, 1)
                act.wait_ge(tile_out, tile + 1)
                act.dma_start(scr["u"][tile], out_sb[:, j, :]).then_inc(stored[j], 16)

            def gelu(enc, job, number, half_number, half_job, first=False):
                j = number % 2
                act.wait_ge(z_done, KT * enc + job + 1)
                if not first:
                    act.wait_ge(gelu_stored[j], 16 * (KT // 2 * enc + half_job))
                act.activation(gelu_sb[:, j, :], load_sb[:, j, :], ACT.Gelu,
                               scale=ln_g[:, bass.ds(KT * enc + job, 1)],
                               bias=ln_b[:, bass.ds(KT * enc + job, 1)]).then_inc(load_used[j], 1)
                act.wait_ge(load_used[j], half_number + 1)
                act.dma_start(scr["h"][KT * enc + job], gelu_sb[:, j, :]).then_inc(gelu_stored[j], 16)

            def pairs(start, end, summed=False):
                with act.Fori(start, end) as i:
                    for j in range(2):
                        out(j, 2 * i + j, i, summed=summed)

            def pair_with_jobs(enc, i, start, first=False, summed=False):
                for j in range(2):
                    out(j, 2 * i + j, i, summed=summed)
                    for c in range(j * JOBS // 2, (j + 1) * JOBS // 2):
                        gelu(enc, JOBS * (i - start) + c, c,
                             NORMS[enc] // 2 + JOBS // 2 * (i - start) + c // 2,
                             JOBS // 2 * (i - start) + c // 2, first=first and c < 2)

            def fill(f, pair):
                for k in range(KT):
                    L = FILLS[f] + k
                    act.wait_ge(loaded[k % 2], 16 * (L // 2 + 1))
                    if f > 0:
                        act.wait_ge(piece_used, PIECES * (2 * pair - 1) + k // KQ + 1)
                    act.activation(mov[0][:, k, :], load_sb[:, k % 2, :], ACT.Copy).then_inc(hi_filled, 1)
                for j in range(2):
                    out(j, 2 * pair + j, pair, first=pair == 0, summed=False)

            def std(enc):
                act.wait_ge(var_done, enc + 1)
                act.activation(rstd_bc[:], ps_var[:], ACT.Sqrt, scale=1.0 / ENC_TILES,
                               bias=eps[:]).then_inc(std_done, 1)

            act.wait_ge(consts_loaded, 48)
            act.wait_ge(consts_set, 3)
            fill(0, ER1)
            pairs(ER1 + 1, EI1, summed=True)
            for j in range(2):
                out(j, 2 * EI1 + j, EI1)
            std(0)
            pair_with_jobs(0, NORM_PAIRS[0], NORM_PAIRS[0], first=True, summed=True)
            with act.Fori(NORM_PAIRS[0] + 1, NORM_PAIRS[0] + NORM_LEN) as i:
                pair_with_jobs(0, i, NORM_PAIRS[0], summed=True)
            pairs(NORM_PAIRS[0] + NORM_LEN, TOP, summed=True)
            for j in range(2):
                out(j, 2 * TOP + j, TOP)
            std(1)
            pairs(TOP + 1, ER2)
            fill(1, ER2)
            with act.Fori(NORM_PAIRS[1], NORM_PAIRS[1] + NORM_LEN) as i:
                pair_with_jobs(1, i, NORM_PAIRS[1])
            pairs(NORM_PAIRS[1] + NORM_LEN, EI2)
            fill(2, EI2)
            pairs(EI2 + 1, END)
            for j in range(2):
                act.wait_ge(stored[j], 16 * (ALL_TILES // 2))
                act.wait_ge(gelu_stored[j], 16 * KT)

        @block.vector
        def _(dve):
            def fill(f):
                for k in range(KT):
                    dve.wait_ge(hi_filled, KT * f + k + 1)
                    dve.tensor_tensor(mov[1][:, k, :], load_sb[:, k % 2, :],
                                      mov[0][:, k, :].bitcast(F32), ALU.subtract) \
                        .then_inc(load_used[k % 2], 1)

            def first_sum(tile, j):
                dve.wait_ge(tile_out, tile + 1)
                dve.tensor_copy(shift[:], out_sb[:, j, :]).then_inc(centred, 1)
                dve.memset(dev_sum[:], 0.0).then_inc(squared, 1)
                dve.memset(dev_sq[:], 0.0).then_inc(tile_summed, 1)

            def add_sum(tile, j):
                dve.wait_ge(tile_out, tile + 1)
                dve.wait_ge(tile_summed, tile)
                dve.tensor_tensor(dev[:], out_sb[:, j, :], shift[:], ALU.subtract).then_inc(centred, 1)
                dve.wait_ge(centred, tile + 1)
                dve.tensor_tensor(dev_sum[:], dev_sum[:], dev[:], ALU.add)
                dve.tensor_tensor(dev[:], dev[:], dev[:], ALU.mult).then_inc(squared, 1)
                dve.wait_ge(squared, tile + 1)
                dve.tensor_tensor(dev_sq[:], dev_sq[:], dev[:], ALU.add).then_inc(tile_summed, 1)

            def pairs(start, end):
                with dve.Fori(start, end) as i:
                    for j in range(2):
                        add_sum(2 * i + j, j)

            steps = [0]

            def step(instruction):
                steps[0] += 1
                instruction.then_inc(ln_step, 1)
                dve.wait_ge(ln_step, steps[0])

            def parts(enc):
                dve.wait_ge(tile_summed, ENC_TILES * (enc + 1))
                step(dve.tensor_scalar(rstd_bc[:], dev_sum[:], 1.0 / ENC_TILES, None, ALU.mult))
                dve.tensor_tensor(mean_bc[:], rstd_bc[:], shift[:], ALU.add).then_inc(part_means, 1)
                step(dve.tensor_tensor(rstd_bc[:], rstd_bc[:], dev_sum[:], ALU.mult))
                step(dve.tensor_tensor(rstd_bc[:], dev_sq[:], rstd_bc[:], ALU.subtract))

            def combine(enc):
                dve.wait_ge(mean_done, enc + 1)
                step(dve.tensor_tensor(dev[:], mean_bc[:], ps_mean[:], ALU.subtract))
                step(dve.tensor_tensor(dev[:], dev[:], dev[:], ALU.mult))
                dve.tensor_copy(mean_bc[:], ps_mean[:])
                dve.scalar_tensor_tensor(rstd_bc[:], dev[:], float(ENC_TILES), rstd_bc[:],
                                         ALU.mult, ALU.add).then_inc(part_vars, 1)

            def rstd(enc):
                dve.wait_ge(std_done, enc + 1)
                step(dve.reciprocal(rstd_bc[:], rstd_bc[:]))

            def normalise(enc, job, number, half_number):
                j = number % 2
                dve.wait_ge(loaded[j], 16 * (half_number + 1))
                dve.tensor_tensor(load_sb[:, j, :], load_sb[:, j, :], mean_bc[:], ALU.subtract) \
                    .then_inc(z_centred, 1)
                dve.wait_ge(z_centred, KT * enc + job + 1)
                dve.tensor_tensor(load_sb[:, j, :], load_sb[:, j, :], rstd_bc[:], ALU.mult) \
                    .then_inc(z_done, 1)

            def jobs(enc, i, start, js, sums):
                for j in js:
                    if sums:
                        add_sum(2 * i + j, j)
                    for c in range(j * JOBS // 2, (j + 1) * JOBS // 2):
                        normalise(enc, JOBS * (i - start) + c, c,
                                  NORMS[enc] // 2 + JOBS // 2 * (i - start) + c // 2)

            fill(0)
            first_sum(0, 0)
            add_sum(1, 1)
            pairs(ER1 + 1, EI1)
            parts(0)
            combine(0)
            first_sum(2 * EI1, 0)
            add_sum(2 * EI1 + 1, 1)
            rstd(0)
            with dve.Fori(NORM_PAIRS[0], NORM_PAIRS[0] + NORM_LEN) as i:
                jobs(0, i, NORM_PAIRS[0], (0, 1), True)
            pairs(NORM_PAIRS[0] + NORM_LEN, TOP)
            parts(1)
            combine(1)
            rstd(1)
            fill(1)
            with dve.Fori(NORM_PAIRS[1], NORM_PAIRS[1] + NORM_LEN) as i:
                jobs(1, i, NORM_PAIRS[1], (0, 1), False)
            fill(2)


GROUPS = 4
GR = P // GROUPS
NB = N * P
ROW_TILES = B // P
SCALE = float(HD) ** -0.5
MAG_EPS = 1e-8
DK = D // P


def attention_phase(nc, t, scr, strength):
    with ExitStack() as ctx:
        def sb(name, shape, dt=F32):
            return ctx.enter_context(nc.sbuf_tensor(name, shape, dt))

        def sem(name):
            return ctx.enter_context(nc.semaphore(name))

        wts = [sb("qkv_hi", [P, 6, DK, D], F32R), sb("qkv_lo", [P, 6, DK, D], F32R)]
        s_stage = [sb(f"s{c}_stage", [P, DK, N, P]) for c in "ri"]
        s = [[sb(f"s{c}_{part}", [P, DK, GROUPS, P], F32R) for part in ("hi", "lo")] for c in "ri"]
        q_cat = sb("q_cat", [P, 2, 2, GROUPS, P])
        k_both = sb("k_both", [P, 2, 2, 2, GROUPS, P])
        v_sb = sb("v_sb", [P, GROUPS, HEADS, 2, HD])
        masked = sb("masked", [P, GROUPS, 2 * N, GR])
        scores = sb("scores", [P, HEADS, GROUPS, 2, N])
        mag = sb("mag", [P, HEADS * GROUPS, N])
        top = sb("top", [P, HEADS * GROUPS])
        total = sb("total", [P, HEADS * GROUPS])
        spread = sb("spread", [P, 2, GROUPS, N, GR])
        spread_t = sb("spread_t", [P, 2, GROUPS, P])
        o_sb = sb("o_sb", [P, 2, N, P])
        same_row = sb("same_row", [P, GR])
        ident = sb("ident", [P, P])
        qk_bias = sb("qk_bias", [P, 5, DK])
        v_bias = sb("v_bias", [P, HEADS])
        mag_eps = sb("mag_eps", [P, 1])
        ids = sb("ids", [P, ROW_TILES, N], I32)
        banks = ctx.enter_context(nc.psum_tensor("banks", [P, 4, HALF], F32))
        ps_x = ctx.enter_context(nc.psum_tensor("ps_x", [P, 4, HALF], F32))
        ps_scores = ps_x[:, 0:2, :]
        ps_pt = [ps_x[:, 2, :], ps_x[:, 0, :]]
        ps_o = [ps_x[:, 3, :], ps_x[:, 1, :]]

        consts_loaded = sem("a_consts_loaded")
        consts_set = sem("a_consts_set")
        bias_negated = sem("bias_negated")
        ids_loaded = sem("ids_loaded")
        gathered = sem("gathered")
        mat_loaded = [sem(f"mat_loaded{m}") for m in range(6)]
        mat_rounded = sem("mat_rounded")
        mat_split = sem("mat_split")
        s_loaded = [sem(f"s_{c}_loaded") for c in "ri"]
        s_rounded = sem("s_rounded")
        s_split = sem("s_split")
        bank_full = sem("bank_full")
        bank_read = sem("bank_read")
        scores_done = sem("scores_done")
        scores_masked = sem("scores_masked")
        scores_kept = sem("scores_kept")
        soft = sem("soft")
        mag2_done = sem("mag2_done")
        mag_done = sem("mag_done")
        mag_less = sem("mag_less")
        exp_done = sem("exp_done")
        weights_done = sem("weights_done")
        spread_done = sem("spread_done")
        turned = sem("turned")
        turned_out = sem("turned_out")
        o_done = sem("o_done")
        o_out = sem("o_out")
        o_stored = [sem(f"o_stored{j}") for j in range(2)]

        block = ctx.enter_context(nc.Block())

        BANKS = 4
        QK_PLACES = 2 * 2
        FILLS = 4 * DK + 2 * GROUPS
        mat_stage = [x.rearrange(pattern)[:, j * DK * D:(j + 1) * DK * D] for x, pattern in
                     ((k_both[:], "p e a k g x -> p (e a k g x)"), (v_sb[:], "p g h c d -> p (g h c d)"))
                     for j in range(2)]
        mat_stage += mat_stage[2:]
        s_src = [scr["u"][L1_TILES + ENC_TILES * c:L1_TILES + ENC_TILES * (c + 1)]
                 .rearrange("(n k) p (t b) -> t p k n b", k=DK, b=P) for c in range(2)]

        @block.sync
        def _(sp):
            sp.dma_start(qk_bias[:, 0:4, :], t["qk_bias"]).then_inc(consts_loaded, 16)
            sp.dma_start(v_bias[:], t["v_bias"]).then_inc(consts_loaded, 16)

            def load_s(tile, c):
                for k in range(DK):
                    sp.dma_start(s_stage[c][:, k, :, :], s_src[c][tile, :, k, :, :]) \
                        .then_inc(s_loaded[c], 16)

            for j in range(2):
                sp.sem_inc(o_stored[j], 16)
            for m in range(6):
                if m == 0:
                    load_s(0, 0)
                if m == 2:
                    load_s(0, 1)
                if m >= 4:
                    sp.wait_ge(mat_split, m - 1)
                sp.dma_start(mat_stage[m], t["qkv"][m]).then_inc(mat_loaded[m], 16)
            sp.dma_start(ids[:], t["ids"]).then_inc(ids_loaded, 16)

            def store_o(tile):
                for h in range(HEADS):
                    sp.wait_ge(o_out, 2 + HEADS * tile + h + 1)
                    sp.dma_start(scr["o"][tile, h], o_sb[:, h % 2, :, :].rearrange("p n b -> p (n b)")) \
                        .then_inc(o_stored[h % 2], 16)

            with sp.Fori(0, ROW_TILES - 1) as tile:
                for c in range(2):
                    sp.wait_ge(s_split, 2 * tile + c + 1)
                    load_s(tile + 1, c)
                store_o(tile)
            store_o(ROW_TILES - 1)
            for j in range(2):
                sp.wait_ge(o_stored[j], 16 * (HEADS // 2 * ROW_TILES + 1))

        @block.gpsimd
        def _(pool):
            pool.memset(mag_eps[:], MAG_EPS).then_inc(consts_set, 1)
            pool.memset(ident[:], 0.0).then_inc(consts_set, 1)
            pool.memset(same_row[:], 0.0).then_inc(consts_set, 1)
            pool.wait_ge(consts_set, 3)
            pool.affine_select(out=ident[:], in_=ident[:], compare_op=ALU.not_equal, fill=1.0,
                               base=0, pattern=[[-1, P]], channel_multiplier=1).then_inc(consts_set, 1)
            for n in range(N):
                pool.wait_ge(consts_set, 4 + n)
                pool.affine_select(out=same_row[:], in_=same_row[:], compare_op=ALU.not_equal,
                                   fill=1.0, base=-GR * n, pattern=[[-1, GR]],
                                   channel_multiplier=1).then_inc(consts_set, 1)
            pool.wait_ge(ids_loaded, 16)
            for tile in range(ROW_TILES):
                for n in range(N):
                    pool.indirect_dma_start(
                        out=strength[:, tile, n, :], out_offset=None, in_=t[f"tbl_{n}"],
                        in_offset=bass.IndirectOffsetOnAxis(ap=ids[:, tile, n:n + 1], axis=0)) \
                        .then_inc(gathered, 16)
            pool.wait_ge(gathered, 16 * N * ROW_TILES)

        CONSTS = 4 + N

        @block.tensor
        def _(pe):
            def fill_bank(tile, x, products):
                pe.wait_ge(bank_read, FILLS * tile + x + 1)
                for n, (lhs, rhs) in enumerate(products):
                    last = pe.matmul(banks[:, x % BANKS, :], lhs, rhs, start=n == 0,
                                     stop=n == len(products) - 1)
                last.then_inc(bank_full, 1)

            def project(tile, et, m):
                c = m // 2
                fill_bank(tile, 4 * et + m,
                          [(wts[wp][:, m, k, et * P:(et + 1) * P], s[c][sp_][:, k, :, :])
                           for k in range(DK) for wp, sp_ in PARTS])

            def values(tile, c, g):
                fill_bank(tile, 4 * DK + GROUPS * c + g,
                          [(s[c][sp_][:, k, g, :], wts[wp][:, 4 + c, k, :])
                           for k in range(DK) for wp, sp_ in PARTS])

            def score(tile, h):
                et, a = h // 2, h % 2
                pe.wait_ge(bank_read, BANKS + FILLS * tile + 4 * (et + 1))
                pe.wait_ge(scores_masked, HEADS * tile + h + 1)
                if h == 0:
                    pe.wait_ge(turned_out, 2 + HEADS * tile)
                    pe.wait_ge(o_out, 2 + HEADS * tile)
                for g in range(GROUPS):
                    last = pe.matmul(ps_scores[:, g // 2, (g % 2) * 2 * P:(g % 2 + 1) * 2 * P],
                                     q_cat[:, et % 2, a, g, :], k_both[:, et % 2, a, :, g, :],
                                     start=True, stop=True)
                last.then_inc(scores_done, 1)

            def turn(tile, h):
                pe.wait_ge(spread_done, HEADS * tile + h + 1)
                pe.wait_ge(turned_out, HEADS * tile + h + 1)
                for g in range(GROUPS):
                    last = pe.transpose(ps_pt[h % 2][:, g * P:(g + 1) * P],
                                        spread[:, h % 2, g, :, :].rearrange("p m b -> p (m b)"),
                                        ident[:])
                last.then_inc(turned, 1)

            def weigh(tile, h):
                if h == 0:
                    pe.wait_ge(bank_read, BANKS + FILLS * (tile + 1))
                pe.wait_ge(turned_out, 2 + HEADS * tile + h + 1)
                pe.wait_ge(o_out, HEADS * tile + h + 1)
                for g in range(GROUPS):
                    last = pe.matmul(ps_o[h % 2][:, g * P:(g + 1) * P],
                                     v_sb[:, g, h, :, :].rearrange("p c d -> p (c d)"),
                                     spread_t[:, h % 2, g, :], start=True, stop=True)
                last.then_inc(o_done, 1)

            pe.sem_inc(scores_done, QK_PLACES)
            pe.sem_inc(bank_full, FILLS)
            pe.sem_inc(turned, 2)
            pe.wait_ge(consts_set, CONSTS)
            with pe.Fori(0, ROW_TILES) as tile:
                for et in range(DK):
                    for m in range(4):
                        if et == 0 and m % 2 == 0:
                            pe.wait_ge(s_split, 2 * tile + m // 2 + 1)
                        if et == 0:
                            pe.wait_ge(mat_split, m + 1)
                        project(tile, et, m)
                        if et and m % 2:
                            score(tile, 2 * (et - 1) + m // 2)
                pe.wait_ge(mat_split, 6)
                for c in range(2):
                    for g in range(GROUPS):
                        values(tile, c, g)
                        if c == 0 and g < 2:
                            score(tile, 2 * (DK - 1) + g)
                turn(tile, 0)
                for h in range(HEADS):
                    if h + 1 < HEADS:
                        turn(tile, h + 1)
                    weigh(tile, h)

        @block.scalar
        def _(act):
            act.sem_inc(bank_read, BANKS)
            act.sem_inc(turned_out, 2)
            act.sem_inc(o_out, 2)
            act.wait_ge(consts_loaded, 32)
            act.mul(qk_bias[:, 4, :], qk_bias[:, 3, :], -1.0).then_inc(bias_negated, 1)
            act.wait_ge(bias_negated, 1)
            act.wait_ge(consts_set, CONSTS)
            for m in range(6):
                act.wait_ge(mat_loaded[m], 16)
                act.activation(wts[0][:, m, :, :].rearrange("p k e -> p (k e)"), mat_stage[m],
                               ACT.Copy).then_inc(mat_rounded, 1)

            def read_qk(tile, et, m):
                act.wait_ge(bank_full, FILLS * (tile + 1) + 4 * et + m + 1)
                if m == 0:
                    act.wait_ge(scores_done, HEADS * tile + 2 * et + 2)
                imag, par = m // 2, et % 2
                here = slice(imag * HD, (imag + 1) * HD)
                there = slice((1 - imag) * HD, (2 - imag) * HD)
                for a in range(2):
                    src = slice(a * HD, (a + 1) * HD)

                    def put(dst, scale, col):
                        return act.activation(dst.rearrange("p g x -> p (g x)"),
                                              banks[src, (4 * et + m) % BANKS, :], ACT.Identity,
                                              scale=scale, bias=qk_bias[src, col, et:et + 1])
                    if m % 2 == 0:
                        last = put(q_cat[here, par, a, :, :], 1.0, m)
                    else:
                        put(k_both[here, par, a, 0, :, :], 1.0, m)
                        last = put(k_both[there, par, a, 1, :, :], -1.0 if imag else 1.0,
                                   4 if imag else m)
                last.then_inc(bank_read, 1)

            def read_v(tile, c, g):
                x = 4 * DK + GROUPS * c + g
                act.wait_ge(bank_full, FILLS * (tile + 1) + x + 1)
                act.activation(v_sb[:, g, :, c, :],
                               banks[:, x % BANKS, :].rearrange("p (h d) -> p h d", d=HD), ACT.Copy) \
                    .then_inc(bank_read, 1)

            def read_turned(tile, h):
                act.wait_ge(turned, 2 + HEADS * tile + h + 1)
                act.activation(spread_t[:, h % 2, :, :].rearrange("p g q -> p (g q)"), ps_pt[h % 2],
                               ACT.Copy).then_inc(turned_out, 1)

            def read_o(tile, h):
                act.wait_ge(o_done, HEADS * tile + h + 1)
                act.wait_ge(o_stored[h % 2], 16 * (HEADS // 2 * tile + h // 2 + 1))
                act.activation(o_sb[:, h % 2, :, :].rearrange("p n (g b) -> p g n b", b=GR),
                               ps_o[h % 2].rearrange("p (g n b) -> p g n b", n=N, b=GR), ACT.Identity,
                               bias=v_bias[:, h:h + 1]).then_inc(o_out, 1)

            with act.Fori(0, ROW_TILES) as tile:
                for et in range(DK):
                    for m in range(4):
                        read_qk(tile, et, m)
                for g in range(GROUPS):
                    read_v(tile, 0, g)
                act.wait_ge(mag2_done, tile + 1)
                act.activation(mag[:], mag[:], ACT.Sqrt, bias=mag_eps[:]).then_inc(mag_done, 1)
                read_v(tile, 1, 0)
                act.wait_ge(mag_less, tile + 1)
                act.activation(mag[:], mag[:], ACT.Exp, scale=SCALE).then_inc(exp_done, 1)
                for g in range(1, GROUPS):
                    read_v(tile, 1, g)
                read_turned(tile, 0)
                for h in range(HEADS):
                    if h + 1 < HEADS:
                        read_turned(tile, h + 1)
                    read_o(tile, h)

        @block.vector
        def _(dve):
            dve.sem_inc(scores_masked, 1)
            dve.wait_ge(consts_set, CONSTS)

            def low_mat(m):
                dve.wait_ge(mat_rounded, m + 1)
                dve.tensor_tensor(wts[1][:, m, :, :].rearrange("p k e -> p (k e)"), mat_stage[m],
                                  wts[0][:, m, :, :].bitcast(F32).rearrange("p k e -> p (k e)"),
                                  ALU.subtract).then_inc(mat_split, 1)

            def split_s(tile, c):
                dve.wait_ge(s_loaded[c], 16 * DK * (tile + 1))
                dve.wait_ge(bank_full, FILLS * tile + 4 * DK + GROUPS * (c + 1))
                for k in range(DK):
                    stage_k = s_stage[c][:, k, :, :].rearrange("p n (g b) -> p g n b", b=GR)
                    hi_k = s[c][0][:, k, :, :].rearrange("p g (n b) -> p g n b", b=GR)
                    dve.tensor_copy(hi_k, stage_k).then_inc(s_rounded, 1)
                for k in range(DK):
                    stage_k = s_stage[c][:, k, :, :].rearrange("p n (g b) -> p g n b", b=GR)
                    hi_k = s[c][0][:, k, :, :].rearrange("p g (n b) -> p g n b", b=GR)
                    lo_k = s[c][1][:, k, :, :].rearrange("p g (n b) -> p g n b", b=GR)
                    dve.wait_ge(s_rounded, DK * (2 * tile + c) + k + 1)
                    last = dve.tensor_tensor(lo_k, stage_k, hi_k.bitcast(F32), ALU.subtract)
                last.then_inc(s_split, 1)

            def keep_own_row(tile, h):
                dve.wait_ge(scores_done, QK_PLACES + HEADS * tile + h + 1)
                if h > 0:
                    dve.wait_ge(scores_kept, HEADS * tile + h)
                dve.tensor_tensor(masked[:].rearrange("p g m b -> p (g m) b"),
                                  ps_scores.rearrange("p k (x b) -> p (k x) b", b=GR),
                                  same_row[:].unsqueeze(1).broadcast_to([P, GROUPS * 2 * N, GR]),
                                  ALU.mult).then_inc(scores_masked, 1)
                dve.wait_ge(scores_masked, 1 + HEADS * tile + h + 1)
                dve.tensor_reduce(scores[:, h, :, :, :].rearrange("p g c m -> p (g c m)"),
                                  masked[:].rearrange("p g m b -> p (g m) b"), AX.X, ALU.add) \
                    .then_inc(scores_kept, 1)

            HG = HEADS * GROUPS
            SOFT_STEPS = 4

            def softmax(tile):
                def step(n, instruction):
                    instruction.then_inc(soft, 1)
                    dve.wait_ge(soft, SOFT_STEPS * tile + n)

                sc = scores[:].rearrange("p h g c m -> p (h g) c m")
                dve.wait_ge(scores_kept, HEADS * (tile + 1))
                step(1, dve.tensor_tensor(scores[:], scores[:], scores[:], ALU.mult))
                dve.tensor_tensor(mag[:], sc[:, :, 0, :], sc[:, :, 1, :], ALU.add).then_inc(mag2_done, 1)
                dve.wait_ge(mag_done, tile + 1)
                step(2, dve.tensor_reduce(top[:], mag[:], AX.X, ALU.max))
                dve.tensor_tensor(mag[:], mag[:], top[:].unsqueeze(2).broadcast_to([P, HG, N]),
                                  ALU.subtract).then_inc(mag_less, 1)
                dve.wait_ge(exp_done, tile + 1)
                step(3, dve.tensor_reduce(total[:], mag[:], AX.X, ALU.add))
                step(4, dve.reciprocal(total[:], total[:]))
                dve.tensor_tensor(mag[:], mag[:], total[:].unsqueeze(2).broadcast_to([P, HG, N]),
                                  ALU.mult).then_inc(weights_done, 1)

            def spread_weights(tile, h):
                if h == 0:
                    dve.wait_ge(weights_done, tile + 1)
                dve.wait_ge(turned, HEADS * tile + h + 1)
                dve.tensor_tensor(
                    spread[:, h % 2, :, :, :].rearrange("p g m b -> p (g m) b"),
                    mag[:, h * GROUPS:(h + 1) * GROUPS, :].rearrange("p g m -> p (g m)")
                    .unsqueeze(2).broadcast_to([P, GROUPS * N, GR]),
                    same_row[:].unsqueeze(1).broadcast_to([P, GROUPS * N, GR]),
                    ALU.mult).then_inc(spread_done, 1)

            def attend(tile):
                for h in range(HEADS):
                    keep_own_row(tile, h)
                softmax(tile)
                for h in range(HEADS):
                    spread_weights(tile, h)

            split_s(0, 0)
            for m in range(2):
                low_mat(m)
            split_s(0, 1)
            for m in range(2, 6):
                low_mat(m)
            with dve.Fori(0, ROW_TILES - 1) as tile:
                attend(tile)
                for c in range(2):
                    split_s(tile + 1, c)
            attend(ROW_TILES - 1)



def output_projection_phase(nc, t, scr):
    with ExitStack() as ctx:
        def sb(name, shape, dt=F32):
            return ctx.enter_context(nc.sbuf_tensor(name, shape, dt))

        def sem(name):
            return ctx.enter_context(nc.semaphore(name))

        wts = [sb("wo_hi", [P, 2, DK, D], F32R), sb("wo_lo", [P, 2, DK, D], F32R)]
        wo_stage = sb("wo_stage", [P, 2, DK, D])
        o_stage = sb("o_stage", [P, 2, DK, NB])
        o = [sb("o_hi", [P, 2, DK, NB], F32R), sb("o_lo", [P, 2, DK, NB], F32R)]
        attn_sb = sb("attn_sb", [P, 2 * DK, NB])
        wo_bias = sb("wo_bias", [P, 2, DK])
        banks = ctx.enter_context(nc.psum_tensor("wo_banks", [P, 2 * DK, NB], F32))

        bias_loaded = sem("wo_bias_loaded")
        wo_loaded = [sem(f"wo_loaded{c}") for c in range(2)]
        wo_rounded = sem("wo_rounded")
        wo_split = sem("wo_split")
        o_loaded = [sem(f"o_loaded{c}") for c in range(2)]
        o_rounded = sem("o_rounded")
        o_split = sem("o_split")
        bank_full = sem("wo_bank_full")
        bank_read = sem("wo_bank_read")
        attn_stored = [sem(f"attn_stored{c}") for c in range(2)]

        block = ctx.enter_context(nc.Block())
        FILLS = 2 * DK

        @block.sync
        def _(sp):
            sp.dma_start(wo_bias[:], t["wo_bias"]).then_inc(bias_loaded, 16)

            def load(tile, c, first=False):
                if not first:
                    sp.wait_ge(o_split, 2 * (tile - 1) + c + 1)
                for a in range(2):
                    sp.dma_start(o_stage[a * HD:(a + 1) * HD, c, :, :],
                                 scr["o"][tile, a::2, c * HD:(c + 1) * HD, :].rearrange("k d x -> d k x")) \
                        .then_inc(o_loaded[c], 16)

            for c in range(2):
                sp.dma_start(wo_stage[:, c, :, :].rearrange("p k e -> p (k e)"), t["wo"][c]) \
                    .then_inc(wo_loaded[c], 16)
                load(0, c, first=True)
            with sp.Fori(1, ROW_TILES) as tile:
                for c in range(2):
                    load(tile, c)

        @block.vector
        def _(dve):
            def split(stage, parts, rounded, done, count):
                dve.tensor_copy(parts[0], stage).then_inc(rounded, 1)
                dve.wait_ge(rounded, count)
                dve.tensor_tensor(parts[1], stage, parts[0].bitcast(F32), ALU.subtract).then_inc(done, 1)

            dve.sem_inc(bank_full, FILLS)
            def split_o(tile, c):
                dve.wait_ge(o_loaded[c], 32 * (tile + 1))
                dve.wait_ge(bank_full, FILLS * tile + DK * (c + 1))
                split(o_stage[:, c, :, :], [x[:, c, :, :] for x in o], o_rounded, o_split,
                      2 * tile + c + 1)

            for c in range(2):
                dve.wait_ge(wo_loaded[c], 16)
                split(wo_stage[:, c, :, :], [w[:, c, :, :] for w in wts], wo_rounded, wo_split, c + 1)
                split_o(0, c)
            with dve.Fori(1, ROW_TILES) as tile:
                for c in range(2):
                    split_o(tile, c)

        @block.tensor
        def _(pe):
            with pe.Fori(0, ROW_TILES) as tile:
                for c in range(2):
                    pe.wait_ge(wo_split, c + 1)
                    pe.wait_ge(o_split, 2 * tile + c + 1)
                    for et in range(DK):
                        pe.wait_ge(bank_read, FILLS * tile + DK * c + et + 1)
                        n = 0
                        for k in range(DK):
                            for wp, op in PARTS:
                                last = pe.matmul(banks[:, DK * c + et, :],
                                                 wts[wp][:, c, k, et * P:(et + 1) * P], o[op][:, c, k, :],
                                                 start=n == 0, stop=n == 3 * DK - 1)
                                n += 1
                        last.then_inc(bank_full, 1)

        @block.scalar
        def _(act):
            act.sem_inc(bank_read, FILLS)
            for c in range(2):
                act.sem_inc(attn_stored[c], 16)
            act.wait_ge(bias_loaded, 16)
            with act.Fori(0, ROW_TILES) as tile:
                for c in range(2):
                    act.wait_ge(attn_stored[c], 16 * (tile + 1))
                    for et in range(DK):
                        x = DK * c + et
                        act.wait_ge(bank_full, FILLS * (tile + 1) + x + 1)
                        act.activation(attn_sb[:, x, :], banks[:, x, :], ACT.Identity,
                                       bias=wo_bias[:, c, et:et + 1]).then_inc(bank_read, 1)
                    act.wait_ge(bank_read, FILLS * (tile + 1) + DK * (c + 1))
                    act.dma_start(scr["attn"][tile, c].rearrange("k p x -> p k x"),
                                  attn_sb[:, DK * c:DK * (c + 1), :]).then_inc(attn_stored[c], 16)
            for c in range(2):
                act.wait_ge(attn_stored[c], 16 * (ROW_TILES + 1))


EH = D // 2
PAIRS = ((0, 1), (0, 2), (0, 3), (1, 2), (1, 3), (2, 3))


def interference_phase(nc, t, scr, strength):
    with ExitStack() as ctx:
        def sb(name, shape, dt=F32):
            return ctx.enter_context(nc.sbuf_tensor(name, shape, dt))

        def sem(name):
            return ctx.enter_context(nc.semaphore(name))

        KH = DK // 2
        wts = [sb("int_hi", [P, N, DK, 3, EH], F32R), sb("int_lo", [P, N, DK, 3, EH], F32R)]
        w_stage = sb("int_stage", [P, 2, KH, 2, EH])
        a_stage = sb("a_stage", [P, 2, KH, NB])
        a = [sb("a_hi", [P, 2, DK, NB], F32R), sb("a_lo", [P, 2, DK, NB], F32R)]
        ri = sb("ri", [P, 2, N, 2, EH])
        unit = sb("unit", [P, N, 2, EH])
        sq = sb("ri_squares", [P, N, 2, EH])
        root = sq[:].rearrange("p n c e -> p (n c e)")[:, 0:N * EH]
        newton = sq[:].rearrange("p n c e -> p (n c e)")[:, N * EH:]
        zero = newton.rearrange("p (n e) -> p n e", n=N)
        mag2 = sb("mag2", [P, N, EH])
        mag2_flat = mag2[:].rearrange("p n e -> p (n e)")
        prod = sb("prod", [P, len(PAIRS), 2, EH])
        cos = prod[:, :, 0, :]
        zeros = sb("pair_zeros", [P, len(PAIRS), EH])
        f = zeros[:, 0:N, :]
        sup = sb("sup", [P, 2, 2, EH])
        s_tile = sb("s_tile", [P, 2, N, N])
        tiny = sb("tiny", [P, 1])
        one = sb("one", [P, 1])
        banks = ctx.enter_context(nc.psum_tensor("ri_banks", [P, 2, N, 2, EH], F32))

        w_loaded = [sem(f"int_loaded{kh}") for kh in range(2)]
        w_rounded = sem("int_rounded")
        w_split = [sem(f"int_split{kh}") for kh in range(2)]
        a_loaded = [sem(f"a_loaded{kh}") for kh in range(2)]
        a_rounded = sem("a_rounded")
        a_split = sem("a_split")
        part_done = sem("part_done")
        ri_out = sem("ri_out")
        mag2_done = sem("mag2_done")
        root_done = sem("root_done")
        root2_done = sem("root2_done")
        t_done = sem("t_done")
        factor_done = sem("factor_done")
        zero_done = sem("zero_done")
        inverse_done = sem("inverse_done")
        zeros_done = sem("zeros_done")
        tiny_set = sem("tiny_set")
        step_done = sem("step_done")
        by_factor = sem("by_factor")
        sup_done = sem("sup_done")
        sup_stored = [sem(f"sup_stored{j}") for j in range(2)]

        block = ctx.enter_context(nc.Block())

        ROOT_SCALE = float(2 ** 15)
        TINY = 1e-26
        UNITS = 2 * ROW_TILES
        PARTS_DONE = 2 * N

        def units(eng, body, half, end=ROW_TILES):
            with eng.Fori(0, end // 2) as i:
                for j in range(2):
                    body(2 * i + (j + ROW_TILES * half), 2 * i + j, j, half)

        @block.sync
        def _(sp):
            def load_w(half, n):
                for kh in range(2):
                    if half or n:
                        sp.wait_ge(w_split[kh], N * half + n)
                    sp.dma_start(w_stage[:, kh, :, :, :].rearrange("p k m e -> p (k m e)"),
                                 t["int_w"][half, n, :, kh * KH * D:(kh + 1) * KH * D]) \
                        .then_inc(w_loaded[kh], 16)

            def load_a(unit_no, tile, c, first=False):
                for kh in range(2):
                    if not first:
                        sp.wait_ge(a_split, 4 * unit_no + 2 * c + kh - 1)
                    sp.dma_start(a_stage[:, kh, :, :],
                                 scr["attn"][tile, c, KH * kh:KH * (kh + 1)].rearrange("k p x -> p k x")) \
                        .then_inc(a_loaded[kh], 16)

            def store(unit_no, tile, j, half):
                sp.wait_ge(sup_done, unit_no + 3)
                sp.dma_start(scr["sup"][tile, :, :, half * EH:(half + 1) * EH].rearrange("c p e -> p c e"),
                             sup[:, j, :, :]).then_inc(sup_stored[j], 16)

            def load_and_store(half):
                with sp.Fori(0, ROW_TILES // 2 - 2) as i:
                    for j in range(2):
                        tile = 2 * i + j
                        for c in range(2):
                            load_a(tile + (3 + ROW_TILES * half), tile + 3, c)
                        store(tile + ROW_TILES * half, tile, j, half)
                for c in range(2):
                    load_a(ROW_TILES - 1 + ROW_TILES * half, ROW_TILES - 1, c)
                store(ROW_TILES - 4 + ROW_TILES * half, ROW_TILES - 4, 0, half)

            for j in range(2):
                sp.sem_inc(sup_stored[j], 16)
            load_w(0, 0)
            load_a(0, 0, 0, first=True)
            for n in range(1, N):
                load_w(0, n)
            load_a(0, 0, 1)
            for tile in (1, 2):
                for c in range(2):
                    load_a(tile, tile, c)
            load_and_store(0)
            load_a(ROW_TILES, 0, 0)
            for n in range(N):
                load_w(1, n)
            load_a(ROW_TILES, 0, 1)
            for tile in range(3):
                if tile:
                    for c in range(2):
                        load_a(ROW_TILES + tile, tile, c)
                store(ROW_TILES - 3 + tile, ROW_TILES - 3 + tile, (1 + tile) % 2, 0)
            load_and_store(1)
            for tile in range(ROW_TILES - 3, ROW_TILES):
                store(ROW_TILES + tile, tile, tile % 2, 1)
            for j in range(2):
                sp.wait_ge(sup_stored[j], 16 * (UNITS // 2 + 1))

        def low_w(eng, half, kh):
            ks = slice(KH * kh, KH * (kh + 1))
            for n in range(N):
                eng.wait_ge(w_rounded, 2 * (N * half + n) + kh + 1)
                eng.tensor_tensor(wts[1][:, n, ks, 1:3, :], w_stage[:, kh, :, :, :],
                                  wts[0][:, n, ks, 1:3, :].bitcast(F32), ALU.subtract)
                eng.tensor_tensor(wts[1][:, n, ks, 0, :], wts[0][:, n, ks, 2, :].bitcast(F32),
                                  w_stage[:, kh, :, 1, :], ALU.subtract).then_inc(w_split[kh], 1)

        @block.gpsimd
        def _(pool):
            def low_a(unit_no, c):
                for kh in range(2):
                    hi, lo = (x[:, c, KH * kh:KH * (kh + 1), :] for x in a)
                    pool.wait_ge(a_rounded, 4 * unit_no + 2 * c + kh + 1)
                    pool.tensor_tensor(lo, a_stage[:, kh, :, :], hi.bitcast(F32), ALU.subtract) \
                        .then_inc(a_split, 1)

            def pair_zeros(unit_no):
                pool.wait_ge(zero_done, unit_no + 1)
                pool.wait_ge(sup_done, unit_no + 2)
                at = 0
                for i in range(N - 1):
                    n = N - 1 - i
                    last = pool.tensor_tensor(zeros[:, at:at + n, :], zero[:, i + 1:N, :],
                                              zero[:, i, :].unsqueeze(1).broadcast_to([P, n, EH]),
                                              ALU.add)
                    at += n
                last.then_inc(zeros_done, 1)

            pool.memset(tiny[:], TINY).then_inc(tiny_set, 1)
            pool.memset(one[:], 1.0).then_inc(tiny_set, 1)
            pool.sem_inc(zeros_done, 1)
            low_a(0, 0)
            low_w(pool, 0, 0)
            low_a(0, 1)
            with pool.Fori(1, ROW_TILES) as unit_no:
                for c in range(2):
                    low_a(unit_no, c)
                pair_zeros(unit_no - 1)
            low_a(ROW_TILES, 0)
            low_w(pool, 1, 0)
            low_a(ROW_TILES, 1)
            pair_zeros(ROW_TILES - 1)
            with pool.Fori(ROW_TILES + 1, UNITS) as unit_no:
                for c in range(2):
                    low_a(unit_no, c)
                pair_zeros(unit_no - 1)
            pair_zeros(UNITS - 1)

        @block.tensor
        def _(pe):
            pe.sem_inc(part_done, PARTS_DONE)

            def products(unit_no, tile, j, half):
                pe.wait_ge(ri_out, 2 * unit_no + 2)
                for c in range(2):
                    for n in range(N):
                        for k in range(DK):
                            if k % KH == 0:
                                pe.wait_ge(w_split[k // KH], N * half + n + 1)
                            if n == 0 and k % KH == 0:
                                pe.wait_ge(a_split, 4 * unit_no + 2 * c + k // KH + 1)
                            for ap, wp in PARTS:
                                cols = slice(1, 3) if c == 0 else slice(0, 2)
                                last = pe.matmul(banks[:, j, n, :, :].rearrange("p c e -> p (c e)"),
                                                 a[ap][:, c, k, n * P:(n + 1) * P],
                                                 wts[wp][:, n, k, cols, :].rearrange("p m e -> p (m e)"),
                                                 start=c == 0 and k == 0 and (ap, wp) == PARTS[0],
                                                 stop=c == 1 and k == DK - 1 and (ap, wp) == PARTS[-1])
                        last.then_inc(part_done, 1)

            for half in range(2):
                units(pe, products, half)

        @block.scalar
        def _(act):
            act.sem_inc(ri_out, 4)

            def round_w(half, n):
                if half:
                    act.wait_ge(part_done, PARTS_DONE * (ROW_TILES + 1) - N + n + 1)
                for kh in range(2):
                    ks = slice(KH * kh, KH * (kh + 1))
                    act.wait_ge(w_loaded[kh], 16 * (N * half + n + 1))
                    act.activation(wts[0][:, n, ks, 1:3, :], w_stage[:, kh, :, :, :], ACT.Copy)
                    act.activation(wts[0][:, n, ks, 0, :], w_stage[:, kh, :, 1, :], ACT.Copy,
                                   scale=-1.0).then_inc(w_rounded, 1)

            def round_a(unit_no, c):
                act.wait_ge(part_done, PARTS_DONE * unit_no + N * (c + 1))
                for kh in range(2):
                    act.wait_ge(a_loaded[kh], 16 * (2 * unit_no + c + 1))
                    act.activation(a[0][:, c, KH * kh:KH * (kh + 1), :], a_stage[:, kh, :, :],
                                   ACT.Copy).then_inc(a_rounded, 1)

            def read(unit_no, tile, j, half, ahead=True):
                act.wait_ge(sup_done, unit_no + 1)
                act.activation(s_tile[:, j, :, :].rearrange("p i j -> p (i j)"),
                               strength[:, bass.ds(tile, 1), :, :].rearrange("p t i j -> p (t i j)"),
                               ACT.Copy)
                for pair in range(2):
                    states = slice(2 * pair, 2 * pair + 2)
                    act.wait_ge(part_done, PARTS_DONE * (unit_no + 1) + N + 2 * (pair + 1))
                    act.activation(ri[:, j, states, :, :], banks[:, j, states, :, :], ACT.Copy)
                    if pair == 0:
                        act.wait_ge(inverse_done, unit_no + 1)
                        act.wait_ge(zeros_done, unit_no + 1)
                    act.activation(sq[:, states, :, :], banks[:, j, states, :, :], ACT.Square) \
                        .then_inc(ri_out, 1)
                if ahead:
                    round_a(unit_no + 1, 1)
                act.wait_ge(mag2_done, unit_no + 1)
                act.activation(root, mag2_flat, ACT.Abs_reciprocal_sqrt, scale=ROOT_SCALE ** 2,
                               bias=tiny[:]).then_inc(root_done, 1)
                act.wait_ge(root_done, unit_no + 1)
                act.activation(newton, root, ACT.Square, scale=ROOT_SCALE).then_inc(root2_done, 1)
                act.wait_ge(t_done, unit_no + 1)
                act.activation(mag2_flat, newton, ACT.Copy, scale=-0.5 * ROOT_SCALE,
                               bias=1.5 * ROOT_SCALE).then_inc(factor_done, 1)
                act.wait_ge(factor_done, unit_no + 1)
                act.activation(newton, newton, ACT.Relu, scale=-2.0, bias=one[:]) \
                    .then_inc(zero_done, 1)

            def unit_and_next(unit_no, tile, j, half):
                read(unit_no, tile, j, half)
                round_a(unit_no + 2, 0)

            act.wait_ge(tiny_set, 2)
            round_w(0, 0)
            round_a(0, 0)
            for n in range(1, N):
                round_w(0, n)
            round_a(0, 1)
            round_a(1, 0)
            units(act, unit_and_next, 0, ROW_TILES - 2)
            unit_and_next(ROW_TILES - 2, ROW_TILES - 2, 0, 0)
            for n in range(N):
                round_w(1, n)
            unit_and_next(ROW_TILES - 1, ROW_TILES - 1, 1, 0)
            units(act, unit_and_next, 1, ROW_TILES - 2)
            read(UNITS - 2, ROW_TILES - 2, 0, 1)
            read(UNITS - 1, ROW_TILES - 1, 1, 1, ahead=False)

        @block.vector
        def _(dve):
            dve.sem_inc(sup_done, 2)
            dve.sem_inc(inverse_done, 1)
            low_w(dve, 0, 1)

            def add_squares(unit_no):
                dve.wait_ge(ri_out, 2 * unit_no + 6)
                dve.tensor_tensor(mag2[:], sq[:, :, 0, :], sq[:, :, 1, :], ALU.add) \
                    .then_inc(mag2_done, 1)

            def newton_t(unit_no):
                dve.wait_ge(root2_done, unit_no + 1)
                dve.tensor_tensor(newton, newton, mag2_flat, ALU.mult).then_inc(t_done, 1)

            def superpose(unit_no, tile, j, half, ahead=True):
                STEPS = 8
                count = [0]

                def step(*instructions):
                    instructions[-1].then_inc(step_done, 1)
                    count[0] += 1
                    dve.wait_ge(step_done, STEPS * unit_no + count[0])

                def by_part(x, n):
                    return x.unsqueeze(2).broadcast_to([P, n, 2, EH])

                z = ri[:, j, :, :, :]
                dve.wait_ge(factor_done, unit_no + 1)
                dve.tensor_tensor(mag2_flat, root, mag2_flat, ALU.mult).then_inc(inverse_done, 1)
                dve.wait_ge(inverse_done, unit_no + 2)
                dve.wait_ge(sup_done, unit_no + 2)
                step(dve.tensor_tensor(unit[:], z, by_part(mag2[:], N), ALU.mult))
                at, made = 0, []
                for i in range(N - 1):
                    n = N - 1 - i
                    made.append(dve.tensor_tensor(
                        prod[:, at:at + n, :, :], unit[:, i + 1:N, :, :],
                        unit[:, i, :, :].unsqueeze(1).broadcast_to([P, n, 2, EH]), ALU.mult))
                    at += n
                step(*made)
                step(dve.tensor_tensor(cos, cos, prod[:, :, 1, :], ALU.add))
                dve.wait_ge(zeros_done, unit_no + 2)
                step(dve.tensor_tensor(cos, cos, zeros[:], ALU.add))
                others = [[i for i in range(N) if i != m] for m in range(N)]

                def cosine(i, m):
                    return prod[:, PAIRS.index((min(i, m), max(i, m))), 0, :]

                step(*[dve.tensor_scalar(f[:, m, :], cosine(others[m][0], m),
                                         s_tile[:, j, others[m][0], m:m + 1],
                                         s_tile[:, j, m, m:m + 1],
                                         ALU.mult, ALU.add) for m in range(N)])
                for o in (1, 2):
                    made = [dve.scalar_tensor_tensor(f[:, m, :], cosine(others[m][o], m),
                                                     s_tile[:, j, others[m][o], m:m + 1], f[:, m, :],
                                                     ALU.mult, ALU.add) for m in range(N)]
                    if o == 2 and ahead:
                        add_squares(unit_no + 1)
                    step(*made)
                dve.tensor_tensor(unit[:], z, by_part(f, N), ALU.mult).then_inc(by_factor, 1)
                if ahead:
                    newton_t(unit_no + 1)
                dve.wait_ge(by_factor, unit_no + 1)
                step(dve.tensor_tensor(unit[:, 0:2, :, :], unit[:, 0:2, :, :], unit[:, 2:4, :, :],
                                       ALU.add))
                assert count[0] == STEPS
                dve.wait_ge(sup_stored[j], 8 * unit_no + 16 - 8 * j)
                dve.tensor_tensor(sup[:, j, :, :], unit[:, 0, :, :], unit[:, 1, :, :], ALU.add) \
                    .then_inc(sup_done, 1)

            add_squares(0)
            newton_t(0)
            units(dve, superpose, 0, ROW_TILES - 2)
            superpose(ROW_TILES - 2, ROW_TILES - 2, 0, 0, ahead=False)
            low_w(dve, 1, 1)
            add_squares(ROW_TILES - 1)
            newton_t(ROW_TILES - 1)
            superpose(ROW_TILES - 1, ROW_TILES - 1, 1, 0)
            units(dve, superpose, 1, ROW_TILES - 2)
            superpose(UNITS - 2, ROW_TILES - 2, 0, 1)
            superpose(UNITS - 1, ROW_TILES - 1, 1, 1, ahead=False)


def top_phase(nc, t, scr, out):
    with ExitStack() as ctx:
        def sb(name, shape, dt=F32):
            return ctx.enter_context(nc.sbuf_tensor(name, shape, dt))

        def sem(name):
            return ctx.enter_context(nc.semaphore(name))

        TILES_HALF = ROW_TILES // 2
        EPS_NORM, EPS_LN = range(2)
        MR, MI, NEG_MI, POST = range(4)
        LOADS = ("Mr", "Mi", "post", "top1", "top2")
        PLACES = (MR, MI, POST, MR, MI)
        wts = [sb(f"top_w_{part}", [P, 4, DK, D], F32R) for part in ("hi", "lo")]
        w_stage = sb("top_w_stage", [P, DK, D])
        w3 = sb("w3", [P, 2])
        sup = sb("top_sup", [P, 2, 2, D])
        norm = sb("norm", [P, ROW_TILES])
        unread = sb("unread", [P, 2 * D])
        sup_t = [[sb(f"sup_t{h}_{part}", [P, 2, DK, HALF], F32R) for part in ("hi", "lo")]
                 for h in range(2)]
        amp_0 = [sb(f"amp_0_{part}", [P, DK, HALF], F32R) for part in ("hi", "lo")]
        amp_t = [[x[:] for x in amp_0], [x[:, 0, :, :] for x in sup_t[0]]]
        z_t = [[x[:, 1, :, :] for x in sup_t[0]], [x[:, 0, :, :] for x in sup_t[1]]]
        h1_t = [[x[:, 1, :, :] for x in sup_t[1]], [x[:] for x in amp_0]]
        sq = sb("top_sq", [P, 2, 2, HALF])
        amp = sb("amp", [P, 2, HALF])
        y = sb("y", [P, DK, B])
        y_sum = sb("y_sum", [P, B])
        x_part = sb("x_part", [P, 2, HALF])
        h2 = y[:, 0:2, :]
        y_out = y_sum[0:1, :]
        cols = sb("top_cols", [P, 3 * DK + 2])
        consts = sb("top_consts", [P, 2])
        averager = sb("top_averager", [P, P])
        ident = sb("top_ident", [P, P])
        ps_turn = ctx.enter_context(nc.psum_tensor("ps_turn", [P, 2, DK, P], F32))
        banks = ctx.enter_context(nc.psum_tensor("top_banks", [P, 4, HALF], F32))
        ps_sum = ctx.enter_context(nc.psum_tensor("ps_sum", [P, 2, HALF], F32))

        cols_loaded = sem("cols_loaded")
        consts_set = sem("t_consts_set")
        tw_loaded = sem("tw_loaded")
        tw_rounded = sem("tw_rounded")
        tw_split = sem("tw_split")
        sup_loaded = [sem(f"sup_loaded{j}") for j in range(2)]
        norm2_done = sem("norm2_done")
        norm_done = sem("norm_done")
        norm_inverted = sem("norm_inverted")
        scaled = sem("scaled")
        turned = sem("sup_turned")
        sup_rounded = sem("sup_rounded")
        sup_split = sem("sup_split")
        filled = sem("bank_filled")
        act_read = sem("act_read")
        dve_read = sem("dve_read")
        amp2_done = sem("amp2_done")
        amp_done = sem("amp_done")
        amp_rounded = sem("amp_rounded")
        amp_split = sem("amp_split")
        ln_step = sem("t_ln_step")
        summed = sem("summed")
        averaged = sem("averaged")
        less_mean = sem("less_mean")
        squared = sem("t_squared")
        std_done = sem("t_std_done")
        z_done = sem("t_z_done")
        gelu_done = sem("t_gelu_done")
        z_rounded = sem("z_rounded")
        z_split = sem("z_split")
        x_loaded = [sem(f"x_loaded{j}") for j in range(2)]
        h1_rounded = sem("h1_rounded")
        h1_split = sem("h1_split")
        y_done = sem("y_done")
        y_read = sem("y_read")
        y_stored = sem("y_stored")

        block = ctx.enter_context(nc.Block())

        MEAS_FILLS, POST_FILLS, TOP1_FILLS = 4 * DK, 2 * DK, 2 * DK
        AT_POST = MEAS_FILLS
        AT_TOP1 = AT_POST + POST_FILLS
        AT_TOP2 = AT_TOP1 + TOP1_FILLS

        def rows(h):
            return slice(h * HALF, (h + 1) * HALF)

        @block.sync
        def _(sp):
            sp.dma_start(cols[:], t["top_cols"]).then_inc(cols_loaded, 16)
            sp.dma_start(w3[:], t["w_top3"]).then_inc(cols_loaded, 16)

            def load_sup(tile):
                if tile >= 2:
                    sp.wait_ge(turned, tile - 1)
                sp.dma_start(sup[:, tile % 2, :, :], scr["sup"][tile].rearrange("c p e -> p c e")) \
                    .then_inc(sup_loaded[tile % 2], 16)

            def load_w(m):
                if m:
                    sp.wait_ge(tw_split, m)
                n = D // 2 if LOADS[m] == "top2" else D
                sp.dma_start(w_stage[:, :, 0:n], t["w_" + LOADS[m]].rearrange("p (k e) -> p k e", k=DK)) \
                    .then_inc(tw_loaded, 16)

            load_sup(0)
            load_sup(1)
            load_w(0)
            load_w(1)
            load_sup(2)
            load_sup(3)
            load_w(2)
            for tile in range(TILES_HALF, ROW_TILES):
                load_sup(tile)
            load_w(3)
            load_w(4)
            for h in range(2):
                for et in range(DK):
                    x = DK * h + et
                    if x >= 2:
                        sp.wait_ge(dve_read, x - 1)
                    sp.dma_start(x_part[:, x % 2, :], scr["u"][2 * ENC_TILES + et, :, rows(h)]) \
                        .then_inc(x_loaded[x % 2], 16)
            sp.wait_ge(y_read, 2)
            sp.dma_start(out.rearrange("b x -> x b"), y_out).then_inc(y_stored, 16)
            sp.wait_ge(y_stored, 16)

        @block.gpsimd
        def _(pool):
            pool.memset(averager[:], 1.0 / P).then_inc(consts_set, 1)
            pool.memset(consts[:, EPS_NORM:EPS_NORM + 1], MAG_EPS).then_inc(consts_set, 1)
            pool.memset(consts[:, EPS_LN:EPS_LN + 1], LN_EPS).then_inc(consts_set, 1)
            pool.memset(ident[:], 0.0).then_inc(consts_set, 1)
            pool.wait_ge(consts_set, 4)
            pool.affine_select(out=ident[:], in_=ident[:], compare_op=ALU.not_equal, fill=1.0,
                               base=0, pattern=[[-1, P]], channel_multiplier=1).then_inc(consts_set, 1)
            for m, place in enumerate(PLACES):
                n = D // 2 if LOADS[m] == "top2" else D
                if m >= 3:
                    pool.wait_ge(filled, MEAS_FILLS)
                pool.wait_ge(tw_loaded, 16 * (m + 1))
                w_in, hi, lo = (x[:, :, 0:n] for x in (w_stage, wts[0][:, place], wts[1][:, place]))
                pool.tensor_copy(hi, w_in).then_inc(tw_rounded, 1)
                pool.wait_ge(tw_rounded, m + 1)
                last = pool.tensor_tensor(lo, w_in, hi.bitcast(F32), ALU.subtract)
                if LOADS[m] == "Mi":
                    pool.tensor_scalar(wts[0][:, NEG_MI], hi.bitcast(F32), -1.0, None, ALU.mult)
                    last = pool.tensor_tensor(wts[1][:, NEG_MI], hi.bitcast(F32), w_in, ALU.subtract)
                last.then_inc(tw_split, 1)

        @block.tensor
        def _(pe):
            def turn(tile):
                pe.wait_ge(scaled, tile + 1)
                if tile:
                    pe.wait_ge(sup_split, tile)
                for c in range(2):
                    for k in range(DK):
                        last = pe.transpose(ps_turn[:, c, k, :], sup[:, tile % 2, c, k * P:(k + 1) * P],
                                            ident[:])
                last.then_inc(turned, 1)

            def fill(x, terms, et):
                before = x - 4
                if before >= AT_TOP2:
                    pe.wait_ge(act_read, AT_TOP1 + before - AT_TOP2 + 1)
                elif before >= AT_TOP1:
                    pe.wait_ge(dve_read, before - AT_TOP1 + 1)
                elif before >= 0:
                    pe.wait_ge(act_read, before + 1)
                all_mm = [(wts[wp][:, place, k, et * P:(et + 1) * P], mov[mp][:, k, :])
                          for place, mov in terms for k in range(DK) for wp, mp in PARTS]
                for n, (lhs, rhs) in enumerate(all_mm):
                    last = pe.matmul(banks[:, x % 4, :], lhs, rhs, start=n == 0,
                                     stop=n == len(all_mm) - 1)
                last.then_inc(filled, 1)

            def average(h, number):
                pe.wait_ge(summed, number + 1)
                pe.matmul(ps_sum[:, h, :], averager[:], y_sum[:, rows(h)], start=True, stop=True) \
                    .then_inc(averaged, 1)

            pe.wait_ge(consts_set, 5)
            for tile in range(TILES_HALF):
                turn(tile)
            pe.wait_ge(tw_split, 2)
            for h in range(2):
                pe.wait_ge(sup_split, TILES_HALF * (h + 1))
                real, imag = ([x[:, c, :, :] for x in sup_t[h]] for c in range(2))
                for et in range(DK):
                    fill(2 * DK * h + 2 * et, [(MR, real), (NEG_MI, imag)], et)
                    fill(2 * DK * h + 2 * et + 1, [(MI, real), (MR, imag)], et)
                    if h == 0:
                        turn(TILES_HALF + et)
            pe.wait_ge(tw_split, 3)
            for h in range(2):
                pe.wait_ge(amp_split, DK * (h + 1))
                for et in range(DK):
                    fill(AT_POST + DK * h + et, [(POST, amp_t[h])], et)
            for number in range(2):
                for h in range(2):
                    average(h, 2 * number + h)
            pe.wait_ge(tw_split, 5)
            for h in range(2):
                pe.wait_ge(z_split, h + 1)
                for et in range(DK):
                    fill(AT_TOP1 + DK * h + et, [(MR, z_t[h])], et)
            for h in range(2):
                pe.wait_ge(h1_split, DK * (h + 1))
                for et in range(2):
                    fill(AT_TOP2 + 2 * h + et, [(MI, h1_t[h])], et)
            pe.wait_ge(cols_loaded, 32)
            for h in range(2):
                pe.wait_ge(act_read, AT_TOP1 + 2 * (h + 1))
                for k in range(2):
                    last = pe.matmul(ps_sum[0:1, h, :], w3[:, k:k + 1], h2[:, k, rows(h)],
                                     start=k == 0, stop=k == 1)
                last.then_inc(y_done, 1)

        @block.scalar
        def _(act):
            def norms(tile):
                act.wait_ge(sup_loaded[tile % 2], 16 * (tile // 2 + 1))
                act.activation(unread[:],
                               sup[:, tile % 2, :, :].rearrange("p c e -> p (c e)"), ACT.Square,
                               accum_out=norm[:, tile:tile + 1]).then_inc(norm2_done, 1)
                act.wait_ge(norm2_done, tile + 1)
                act.activation(norm[:, tile:tile + 1], norm[:, tile:tile + 1], ACT.Sqrt,
                               bias=consts[:, EPS_NORM:EPS_NORM + 1]).then_inc(norm_done, 1)

            def round_sup(tile):
                act.wait_ge(turned, tile + 1)
                h, at = tile // TILES_HALF, tile % TILES_HALF * P
                act.activation(sup_t[h][0][:, :, :, at:at + P], ps_turn[:], ACT.Copy) \
                    .then_inc(sup_rounded, 1)

            def squares(x):
                if x >= 4:
                    act.wait_ge(amp2_done, x // 2 - 1)
                act.wait_ge(filled, x + 1)
                act.activation(sq[:, x // 2 % 2, x % 2, :], banks[:, x % 4, :], ACT.Square) \
                    .then_inc(act_read, 1)

            def root(n):
                act.wait_ge(amp2_done, n + 1)
                act.activation(amp[:, n % 2, :], amp[:, n % 2, :], ACT.Sqrt).then_inc(amp_done, 1)

            act.wait_ge(consts_set, 5)
            act.wait_ge(cols_loaded, 32)
            for tile in range(TILES_HALF):
                norms(tile)
                if tile:
                    round_sup(tile - 1)
            round_sup(TILES_HALF - 1)
            for n in range(2 * DK):
                if n < TILES_HALF:
                    norms(TILES_HALF + n)
                squares(2 * n)
                squares(2 * n + 1)
                if n:
                    root(n - 1)
                if n < TILES_HALF:
                    round_sup(TILES_HALF + n)
            root(2 * DK - 1)

            for h in range(2):
                for et in range(DK):
                    x = AT_POST + DK * h + et
                    act.wait_ge(filled, x + 1)
                    act.activation(y[:, et, rows(h)], banks[:, x % 4, :], ACT.Identity,
                                   bias=cols[:, et:et + 1]).then_inc(act_read, 1)
            for h in range(2):
                act.wait_ge(less_mean, h + 1)
                if h:
                    act.wait_ge(summed, 3)
                act.activation(sq[:].rearrange("p a c x -> p (a c) x"), y[:, :, rows(h)],
                               ACT.Square).then_inc(squared, 1)
            for h in range(2):
                act.wait_ge(averaged, 2 + h + 1)
                act.activation(amp[:, h, :], ps_sum[:, h, :], ACT.Sqrt, scale=1.0 / DK,
                               bias=consts[:, EPS_LN:EPS_LN + 1]).then_inc(std_done, 1)
            for h in range(2):
                act.wait_ge(z_done, h + 1)
                for et in range(DK):
                    last = act.activation(y[:, et, rows(h)], y[:, et, rows(h)], ACT.Gelu,
                                          scale=cols[:, DK + et:DK + et + 1],
                                          bias=cols[:, 2 * DK + et:2 * DK + et + 1])
                last.then_inc(gelu_done, 1)
            for h in range(2):
                for et in range(2):
                    x = AT_TOP2 + 2 * h + et
                    act.wait_ge(filled, x + 1)
                    act.activation(h2[:, et, rows(h)], banks[:, x % 4, :], ACT.Relu,
                                   bias=cols[:, 3 * DK + et:3 * DK + et + 1]).then_inc(act_read, 1)
            for h in range(2):
                act.wait_ge(y_done, h + 1)
                act.activation(y_out[:, rows(h)], ps_sum[0:1, h, :], ACT.Copy).then_inc(y_read, 1)

        @block.vector
        def _(dve):
            def scale(tile):
                dve.wait_ge(norm_done, tile + 1)
                dve.reciprocal(norm[:, tile:tile + 1], norm[:, tile:tile + 1]).then_inc(norm_inverted, 1)
                dve.wait_ge(norm_inverted, tile + 1)
                tile_sup = sup[:, tile % 2, :, :]
                dve.tensor_scalar(tile_sup, tile_sup, norm[:, tile:tile + 1], None, ALU.mult) \
                    .then_inc(scaled, 1)

            def low_sup(tile):
                dve.wait_ge(sup_rounded, tile + 1)
                h, at = tile // TILES_HALF, tile % TILES_HALF * P
                hi, lo = (x[:, :, :, at:at + P] for x in sup_t[h])
                dve.tensor_tensor(lo, ps_turn[:], hi.bitcast(F32), ALU.subtract).then_inc(sup_split, 1)

            def add_squares(n):
                dve.wait_ge(act_read, 2 * n + 2)
                dve.tensor_tensor(amp[:, n % 2, :], sq[:, n % 2, 0, :], sq[:, n % 2, 1, :], ALU.add) \
                    .then_inc(amp2_done, 1)

            def split_amp(n):
                h, et = n // DK, n % DK
                hi, lo = (x[:, et, :] for x in amp_t[h])
                dve.wait_ge(amp_done, n + 1)
                dve.tensor_copy(hi, amp[:, n % 2, :]).then_inc(amp_rounded, 1)
                dve.wait_ge(amp_rounded, n + 1)
                dve.tensor_tensor(lo, amp[:, n % 2, :], hi.bitcast(F32), ALU.subtract) \
                    .then_inc(amp_split, 1)

            for tile in range(TILES_HALF):
                scale(tile)
                if tile:
                    low_sup(tile - 1)
            low_sup(TILES_HALF - 1)
            for n in range(2 * DK):
                if n < TILES_HALF:
                    scale(TILES_HALF + n)
                if n >= 2:
                    dve.wait_ge(amp_split, n - 1)
                add_squares(n)
                if n:
                    split_amp(n - 1)
                if n < TILES_HALF:
                    low_sup(TILES_HALF + n)
            split_amp(2 * DK - 1)

            steps = [0]

            def step(instruction):
                steps[0] += 1
                instruction.then_inc(ln_step, 1)
                dve.wait_ge(ln_step, steps[0])

            def over_tiles(x):
                return x.unsqueeze(1).broadcast_to([P, DK, HALF])

            for h in range(2):
                dve.wait_ge(act_read, AT_POST + DK * (h + 1))
                step(dve.tensor_tensor(sq[:, 0, :, :], y[:, 0:2, rows(h)], y[:, 2:4, rows(h)], ALU.add))
                dve.tensor_tensor(y_sum[:, rows(h)], sq[:, 0, 0, :], sq[:, 0, 1, :], ALU.add) \
                    .then_inc(summed, 1)
                dve.wait_ge(summed, h + 1)
            for h in range(2):
                dve.wait_ge(averaged, h + 1)
                step(dve.tensor_scalar(y_sum[:, rows(h)], ps_sum[:, h, :], 1.0 / DK, None, ALU.mult))
                dve.tensor_tensor(y[:, :, rows(h)], y[:, :, rows(h)], over_tiles(y_sum[:, rows(h)]),
                                  ALU.subtract).then_inc(less_mean, 1)
            for h in range(2):
                dve.wait_ge(less_mean, h + 1)
                dve.wait_ge(squared, h + 1)
                step(dve.tensor_tensor(sq[:, 0, :, :], sq[:, 0, :, :], sq[:, 1, :, :], ALU.add))
                dve.tensor_tensor(y_sum[:, rows(h)], sq[:, 0, 0, :], sq[:, 0, 1, :], ALU.add) \
                    .then_inc(summed, 1)
            for h in range(2):
                dve.wait_ge(std_done, h + 1)
                step(dve.reciprocal(amp[:, h, :], amp[:, h, :]))
                dve.tensor_tensor(y[:, :, rows(h)], y[:, :, rows(h)], over_tiles(amp[:, h, :]),
                                  ALU.mult).then_inc(z_done, 1)
            for h in range(2):
                dve.wait_ge(gelu_done, h + 1)
                dve.tensor_copy(z_t[h][0], y[:, :, rows(h)]).then_inc(z_rounded, 1)
                dve.wait_ge(z_rounded, h + 1)
                dve.tensor_tensor(z_t[h][1], y[:, :, rows(h)], z_t[h][0].bitcast(F32), ALU.subtract) \
                    .then_inc(z_split, 1)
            for h in range(2):
                for et in range(DK):
                    n = DK * h + et
                    x = AT_TOP1 + n
                    hi, lo = (v[:, et, :] for v in h1_t[h])
                    added = sq[:, n % 2, 0, :]
                    dve.wait_ge(filled, x + 1)
                    dve.wait_ge(x_loaded[n % 2], 16 * (n // 2 + 1))
                    if n >= 2:
                        dve.wait_ge(h1_split, n - 1)
                    dve.tensor_tensor(added, banks[:, x % 4, :], x_part[:, n % 2, :], ALU.add) \
                        .then_inc(dve_read, 1)
                    dve.wait_ge(dve_read, n + 1)
                    dve.tensor_scalar(hi, added, 0.0, None, ALU.max).then_inc(h1_rounded, 1)
                    dve.wait_ge(h1_rounded, n + 1)
                    dve.scalar_tensor_tensor(lo, added, 0.0, hi.bitcast(F32), ALU.max, ALU.subtract) \
                        .then_inc(h1_split, 1)


def build(nc, t, out):
    scr = {"u": nc.dram_tensor("u_scratch", [ALL_TILES, P, B], F32, kind="Internal").ap(),
           "h": nc.dram_tensor("h_scratch", [2 * ENC_TILES, P, B], F32, kind="Internal").ap()}
    scr["o"] = nc.dram_tensor("o_scratch", [ROW_TILES, HEADS, P, NB], F32, kind="Internal").ap()
    scr["attn"] = nc.dram_tensor("attn_scratch", [ROW_TILES, 2, DK, P, NB], F32, kind="Internal").ap()
    scr["sup"] = nc.dram_tensor("sup_scratch", [ROW_TILES, 2, P, D], F32, kind="Internal").ap()
    encoders_phase(nc, t, scr)
    with nc.sbuf_tensor("strength", [P, ROW_TILES, N, N], F32) as strength:
        attention_phase(nc, t, scr, strength)
        output_projection_phase(nc, t, scr)
        interference_phase(nc, t, scr, strength)
    top_phase(nc, t, scr, out)


def _layouts(i):
    f = {k: np.asarray(v) for k, v in i.items()}

    def cols(*vectors):
        return np.concatenate([v.reshape(-1, P).T for v in vectors], axis=1)

    def lhs_tiles(*mats):
        m = np.concatenate(mats, axis=1)
        return m.reshape(m.shape[0] // P, P, -1, P).transpose(2, 1, 0, 3).reshape(-1, P, m.shape[0])

    def rhs(w):
        return w.T.reshape(-1, P, w.shape[0]).transpose(1, 0, 2).reshape(P, -1)

    e = "L0_rec_"
    bq_r, bk_r, bq_i, bk_i = (f[e + b].reshape(DK, P).T for b in ("bq_r", "bk_r", "bq_i", "bk_i"))
    return {
        "qkv": np.stack([rhs(f[e + w]) for w in ("Wq_r", "Wk_r", "Wq_i", "Wk_i", "Wv_r", "Wv_i")]),
        "qk_bias": np.stack([bq_r, bk_r, bq_i, bk_i], axis=1),
        "wo": np.stack([rhs(f[e + w]) for w in ("Wo_r", "Wo_i")]),
        "wo_bias": np.stack([f[e + b].reshape(DK, P).T for b in ("bo_r", "bo_i")], axis=1),
        "int_w": np.stack([f[e + w].reshape(N, 2, EH, DK, P) for w in ("int_Wr", "int_Wi")])
        .transpose(2, 1, 5, 4, 0, 3).reshape(2, N, P, -1),
        "ids": f["ids"].reshape(ROW_TILES, P, N).transpose(1, 0, 2),
        **{f"tbl_{n}": f[f"tbl_{n}"] for n in range(N)},
        "w_Mr": rhs(f[e + "meas_Mr"]),
        "w_Mi": rhs(f[e + "meas_Mi"]),
        "w_post": rhs(f[e + "post_W"]),
        "w_top1": rhs(f["W_top1"][:D].T),
        "w_top2": rhs(f["W_top2"].T),
        "w_top3": f["W_top3"].reshape(2, P).T,
        "top_cols": cols(f[e + "post_b"], f[e + "post_g"], f[e + "post_be"], f["b_top2"]),
        "v_bias": np.concatenate([f[e + "bv_r"].reshape(HEADS, HD).T, f[e + "bv_i"].reshape(HEADS, HD).T]),
        "x_t": f["r_x"].T.reshape(KT, P, B),
        "w_enc": lhs_tiles(f[e + "er_W1"].T, f[e + "ei_W1"].T, f["W_top1"][D:],
                           f[e + "er_W2"].T, f[e + "ei_W2"].T),
        "enc_bias": cols(f[e + "er_b1"], f[e + "ei_b1"], f["b_top1"], f[e + "er_b2"], f[e + "ei_b2"]),
        "ln_g": cols(f[e + "er_g1"], f[e + "ei_g1"]),
        "ln_b": cols(f[e + "er_be1"], f[e + "ei_be1"]),
    }


def kernel(**inputs):
    import concourse.bacc as bacc
    from concourse.bass_utils import run_bass_kernel_spmd

    nc = bacc.Bacc("TRN2", target_bir_lowering=False, num_devices=1)
    arrays, t = {}, {}
    for name, a in _layouts(inputs).items():
        a = np.ascontiguousarray(a)
        arrays[f"in_{name}"] = a
        t[name] = nc.dram_tensor(f"in_{name}", a.shape, mybir.dt.from_np(a.dtype),
                                 kind="ExternalInput").ap()
    out = nc.dram_tensor("out_y", (B, 1), F32, kind="ExternalOutput").ap()
    build(nc, t, out)
    r = run_bass_kernel_spmd(nc, [arrays], core_ids=[0])
    return r.results[0]["out_y"]
```

```python
from contextlib import ExitStack

import numpy as np

import concourse.bass as bass
from concourse import mybir

F32 = mybir.dt.float32
F32R = mybir.dt.float32r
I32 = mybir.dt.int32
ALU = mybir.AluOpType
ACT = mybir.ActivationFunctionType
AX = mybir.AxisListType

P = 128
B = 1024
HID = 2048
D = 512
N = 4
HEADS = 8
HD = D // HEADS
KT = HID // P
KQ = 4
PIECES = KT // KQ
HALF = 512
LN_EPS = 1e-5
ENC_TILES = HID // P
TOP_TILES = D // P
L1_TILES = 2 * ENC_TILES + TOP_TILES
ALL_TILES = L1_TILES + 2 * ENC_TILES
JOBS = 4
PARTS = ((0, 0), (0, 1), (1, 0))


def encoders_phase(nc, t, scr):
    with ExitStack() as ctx:
        def sb(name, shape, dt=F32):
            return ctx.enter_context(nc.sbuf_tensor(name, shape, dt))

        def sem(name):
            return ctx.enter_context(nc.semaphore(name))

        PLACES = 4

        mov = [sb("mov_hi", [P, KT, B], F32R), sb("mov_lo", [P, KT, B], F32R)]
        w_stage = sb("w_stage", [P, PIECES, KQ * P])
        w = [sb("w_hi", [P, PIECES, KQ * P], F32R), sb("w_lo", [P, PIECES, KQ * P], F32R)]
        out_sb = sb("out_sb", [P, 2, B])
        load_sb = sb("load_sb", [P, PLACES, B])
        gelu_sb = load_sb[:, 2:4, :]
        shift = sb("shift", [P, B])
        dev = sb("dev", [P, B])
        dev_sum = sb("dev_sum", [P, B])
        dev_sq = sb("dev_sq", [P, B])
        mean_bc = sb("mean_bc", [P, B])
        rstd_bc = sb("rstd_bc", [P, B])
        bias = sb("bias_cols", [P, ALL_TILES])
        ln_g = sb("ln_g", [P, 2 * ENC_TILES])
        ln_b = sb("ln_b", [P, 2 * ENC_TILES])
        averager = sb("averager", [P, P])
        eps = sb("eps", [P, 1])
        zeros = sb("zeros", [P, KQ * P])
        ps = ctx.enter_context(nc.psum_tensor("ps", [P, 2, B], F32))
        ps_mean = ctx.enter_context(nc.psum_tensor("ps_mean", [P, B], F32))
        ps_var = ctx.enter_context(nc.psum_tensor("ps_var", [P, B], F32))

        consts_loaded = sem("consts_loaded")
        consts_set = sem("consts_set")
        w_loaded = [sem(f"w_loaded{q}") for q in range(PIECES)]
        w_rounded = sem("w_rounded")
        w_split = sem("w_split")
        piece_used = sem("piece_used")
        loaded = [sem(f"loaded{j}") for j in range(PLACES)]
        load_used = [sem(f"load_used{j}") for j in range(PLACES)]
        hi_filled = sem("hi_filled")
        tile_out = sem("tile_out")
        stored = [sem(f"stored{j}") for j in range(2)]
        centred = sem("centred")
        squared = sem("squared")
        tile_summed = sem("tile_summed")
        ln_step = sem("ln_step")
        part_means = sem("part_means")
        mean_done = sem("mean_done")
        part_vars = sem("part_vars")
        var_done = sem("var_done")
        std_done = sem("std_done")
        z_centred = sem("z_centred")
        z_done = sem("z_done")
        gelu_stored = [sem(f"gelu_stored{j}") for j in range(2)]

        block = ctx.enter_context(nc.Block())

        NORM_BASE = tuple(KT // PLACES * (enc + 1) + KT // 2 * enc for enc in range(2))

        def filled_before(f, k):
            return KT // PLACES * f + (KT // 2 * f if k % PLACES < 2 else 0) + k // PLACES

        EARLY = KT - KQ

        ER1, EI1, TOP, ER2, EI2, END = 0, 8, 16, 18, 26, 34
        FILL_PAIRS = (ER1, ER2, EI2)
        NORM_PAIRS = (EI1 + 1, ER2 + 1)
        NORM_LEN = KT // JOBS

        @block.sync
        def _(sp):
            def piece(tile, q, first=False):
                if not first:
                    sp.wait_ge(w_split, PIECES * (tile - 1) + q + 1)
                sp.dma_start(w_stage[:, q, :], t["w_enc"][tile, :, q * KQ * P:(q + 1) * KQ * P]) \
                    .then_inc(w_loaded[q], 16)

            def weights(tile):
                for q in range(PIECES):
                    piece(tile, q)

            def load(source, j, before):
                if not (isinstance(before, int) and before == 0):
                    sp.wait_ge(load_used[j], before)
                sp.dma_start(load_sb[:, j, :], source).then_inc(loaded[j], 16)

            def fill(f, pair):
                if f:
                    weights(2 * pair)
                    for j in range(2):
                        sp.wait_ge(gelu_stored[j], 16 * (KT // 2) * f)
                for k in range(KT):
                    if f == 0 and k % KQ == 0:
                        piece(0, k // KQ, first=True)
                    source = t["x_t"][k] if f == 0 else scr["h"][KT * (f - 1) + k]
                    load(source, k % PLACES, filled_before(f, k))
                weights(2 * pair + 1)

            def norm(enc, start):
                for j in range(2):
                    sp.wait_ge(stored[j], 16 * (ENC_TILES // 2) * (enc + 1))
                with sp.Fori(start, start + NORM_LEN) as i:
                    weights(2 * i)
                    weights(2 * i + 1)
                    for c in range(JOBS):
                        load(scr["u"][ENC_TILES * enc + JOBS * (i - start) + c], c % 2,
                             NORM_BASE[enc] + JOBS // 2 * (i - start) + c // 2)

            def plain(start, end):
                with sp.Fori(start, end) as i:
                    weights(2 * i)
                    weights(2 * i + 1)

            fill(0, ER1)
            sp.dma_start(bias[:], t["enc_bias"]).then_inc(consts_loaded, 16)
            sp.dma_start(ln_g[:], t["ln_g"]).then_inc(consts_loaded, 16)
            sp.dma_start(ln_b[:], t["ln_b"]).then_inc(consts_loaded, 16)
            plain(ER1 + 1, NORM_PAIRS[0])
            norm(0, NORM_PAIRS[0])
            plain(NORM_PAIRS[0] + NORM_LEN, ER2)
            fill(1, ER2)
            norm(1, NORM_PAIRS[1])
            plain(NORM_PAIRS[1] + NORM_LEN, EI2)
            fill(2, EI2)
            plain(EI2 + 1, END)

        @block.gpsimd
        def _(pool):
            pool.memset(averager[:], 1.0 / P).then_inc(consts_set, 1)
            pool.memset(eps[:], LN_EPS).then_inc(consts_set, 1)
            pool.memset(zeros[:], 0.0).then_inc(consts_set, 1)
            pool.wait_ge(consts_set, 3)

            def split(tile, first=False):
                for q in range(PIECES):
                    pool.wait_ge(w_loaded[q], 16 * (tile + 1))
                    if not first:
                        pool.wait_ge(piece_used, PIECES * (tile - 1) + q + 1)
                    pool.tensor_tensor(w[0][:, q, :], w_stage[:, q, :], zeros[:], ALU.add) \
                        .then_inc(w_rounded, 1)
                    pool.wait_ge(w_rounded, PIECES * tile + q + 1)
                    pool.tensor_tensor(w[1][:, q, :], w_stage[:, q, :], w[0][:, q, :].bitcast(F32),
                                       ALU.subtract).then_inc(w_split, 1)

            split(0, first=True)
            with pool.Fori(1, ALL_TILES) as tile:
                split(tile)

        @block.tensor
        def _(pe):
            def tile_products(j, tile, fill=None):
                if not (isinstance(tile, int) and tile < 2):
                    pe.wait_ge(tile_out, tile - 1)
                for q in range(PIECES):
                    pe.wait_ge(w_split, PIECES * tile + q + 1)
                    for kk in range(KQ):
                        k = KQ * q + kk
                        if fill is not None:
                            pe.wait_ge(load_used[k % PLACES], filled_before(fill, k) + 1)
                        for wp, mp in PARTS:
                            for half in range(2):
                                last = pe.matmul(ps[:, j, half * HALF:(half + 1) * HALF],
                                                 w[wp][:, q, kk * P:(kk + 1) * P],
                                                 mov[mp][:, k, half * HALF:(half + 1) * HALF],
                                                 start=(k == 0 and (wp, mp) == PARTS[0]),
                                                 stop=(k == KT - 1 and (wp, mp) == PARTS[-1]))
                    last.then_inc(piece_used, 1)

            def pairs(start, end):
                with pe.Fori(start, end) as i:
                    for j in range(2):
                        tile_products(j, 2 * i + j)

            def average(enc, out, source, ready, done):
                pe.wait_ge(ready, enc + 1)
                for half in range(2):
                    cols = slice(half * HALF, (half + 1) * HALF)
                    last = pe.matmul(out[:, cols], averager[:], source[:, cols], start=True, stop=True)
                last.then_inc(done, 1)

            def pair_and_statistics(enc, pair):
                tile_products(0, 2 * pair)
                average(enc, ps_mean, mean_bc, part_means, mean_done)
                tile_products(1, 2 * pair + 1)
                average(enc, ps_var, rstd_bc, part_vars, var_done)

            def pair_filling(fill, pair):
                for j in range(2):
                    tile_products(j, 2 * pair + j, fill if j == 0 else None)

            pe.wait_ge(consts_set, 3)
            pair_filling(0, ER1)
            pairs(ER1 + 1, EI1)
            pair_and_statistics(0, EI1)
            pairs(EI1 + 1, TOP)
            pair_and_statistics(1, TOP)
            pairs(TOP + 1, ER2)
            pair_filling(1, ER2)
            pairs(ER2 + 1, EI2)
            pair_filling(2, EI2)
            pairs(EI2 + 1, END)

        @block.scalar
        def _(act):
            def out(j, tile, pair, first=False, summed=True):
                act.wait_ge(piece_used, PIECES * (tile + 1))
                if not first:
                    act.wait_ge(stored[j], 16 * pair)
                    if summed:
                        act.wait_ge(tile_summed, tile - 1)
                act.activation(out_sb[:, j, :], ps[:, j, :], ACT.Identity,
                               bias=bias[:, bass.ds(tile, 1)]).then_inc(tile_out, 1)
                act.wait_ge(tile_out, tile + 1)
                act.dma_start(scr["u"][tile], out_sb[:, j, :]).then_inc(stored[j], 16)

            def gelu(enc, job, number, half_number, half_job, first=False):
                j = number % 2
                act.wait_ge(z_done, KT * enc + job + 1)
                if not first:
                    act.wait_ge(gelu_stored[j], 16 * (KT // 2 * enc + half_job))
                act.activation(gelu_sb[:, j, :], load_sb[:, j, :], ACT.Gelu,
                               scale=ln_g[:, bass.ds(KT * enc + job, 1)],
                               bias=ln_b[:, bass.ds(KT * enc + job, 1)]).then_inc(load_used[j], 1)
                act.wait_ge(load_used[j], half_number + 1)
                act.dma_start(scr["h"][KT * enc + job], gelu_sb[:, j, :]).then_inc(gelu_stored[j], 16)

            def pairs(start, end, summed=False):
                with act.Fori(start, end) as i:
                    for j in range(2):
                        out(j, 2 * i + j, i, summed=summed)

            def pair_with_jobs(enc, i, start, first=False, summed=False):
                for j in range(2):
                    out(j, 2 * i + j, i, summed=summed)
                    for c in range(j * JOBS // 2, (j + 1) * JOBS // 2):
                        gelu(enc, JOBS * (i - start) + c, c,
                             NORM_BASE[enc] + JOBS // 2 * (i - start) + c // 2,
                             JOBS // 2 * (i - start) + c // 2, first=first and c < 2)

            def fill(f, pair, ks):
                for k in ks:
                    act.wait_ge(loaded[k % PLACES], 16 * (filled_before(f, k) + 1))
                    if f > 0:
                        act.wait_ge(piece_used, PIECES * (2 * pair - 1) + k // KQ + 1)
                    act.activation(mov[0][:, k, :], load_sb[:, k % PLACES, :], ACT.Copy) \
                        .then_inc(hi_filled, 1)

            def refill(f, pair):
                out(0, 2 * pair - 2, pair - 1, summed=False)
                fill(f, pair, range(EARLY))
                out(1, 2 * pair - 1, pair - 1, summed=False)
                fill(f, pair, range(EARLY, KT))
                for j in range(2):
                    out(j, 2 * pair + j, pair, summed=False)

            def std(enc):
                act.wait_ge(var_done, enc + 1)
                act.activation(rstd_bc[:], ps_var[:], ACT.Sqrt, scale=1.0 / ENC_TILES,
                               bias=eps[:]).then_inc(std_done, 1)

            fill(0, ER1, range(KT))
            act.wait_ge(consts_loaded, 48)
            act.wait_ge(consts_set, 3)
            for j in range(2):
                out(j, j, 0, first=True, summed=False)
            pairs(ER1 + 1, EI1, summed=True)
            for j in range(2):
                out(j, 2 * EI1 + j, EI1)
            std(0)
            pair_with_jobs(0, NORM_PAIRS[0], NORM_PAIRS[0], first=True, summed=True)
            with act.Fori(NORM_PAIRS[0] + 1, NORM_PAIRS[0] + NORM_LEN) as i:
                pair_with_jobs(0, i, NORM_PAIRS[0], summed=True)
            pairs(NORM_PAIRS[0] + NORM_LEN, TOP, summed=True)
            for j in range(2):
                out(j, 2 * TOP + j, TOP)
            std(1)
            refill(1, ER2)
            with act.Fori(NORM_PAIRS[1], NORM_PAIRS[1] + NORM_LEN) as i:
                pair_with_jobs(1, i, NORM_PAIRS[1])
            pairs(NORM_PAIRS[1] + NORM_LEN, EI2 - 1)
            refill(2, EI2)
            pairs(EI2 + 1, END)
            for j in range(2):
                act.wait_ge(stored[j], 16 * (ALL_TILES // 2))
                act.wait_ge(gelu_stored[j], 16 * KT)

        @block.vector
        def _(dve):
            def fill(f):
                for k in range(KT):
                    dve.wait_ge(hi_filled, KT * f + k + 1)
                    dve.tensor_tensor(mov[1][:, k, :], load_sb[:, k % PLACES, :],
                                      mov[0][:, k, :].bitcast(F32), ALU.subtract) \
                        .then_inc(load_used[k % PLACES], 1)

            def first_sum(tile, j):
                dve.wait_ge(tile_out, tile + 1)
                dve.tensor_copy(shift[:], out_sb[:, j, :]).then_inc(centred, 1)
                dve.memset(dev_sum[:], 0.0).then_inc(squared, 1)
                dve.memset(dev_sq[:], 0.0).then_inc(tile_summed, 1)

            def add_sum(tile, j):
                dve.wait_ge(tile_out, tile + 1)
                dve.wait_ge(tile_summed, tile)
                dve.tensor_tensor(dev[:], out_sb[:, j, :], shift[:], ALU.subtract).then_inc(centred, 1)
                dve.wait_ge(centred, tile + 1)
                dve.tensor_tensor(dev_sum[:], dev_sum[:], dev[:], ALU.add)
                dve.tensor_tensor(dev[:], dev[:], dev[:], ALU.mult).then_inc(squared, 1)
                dve.wait_ge(squared, tile + 1)
                dve.tensor_tensor(dev_sq[:], dev_sq[:], dev[:], ALU.add).then_inc(tile_summed, 1)

            def pairs(start, end):
                with dve.Fori(start, end) as i:
                    for j in range(2):
                        add_sum(2 * i + j, j)

            steps = [0]

            def step(instruction):
                steps[0] += 1
                instruction.then_inc(ln_step, 1)
                dve.wait_ge(ln_step, steps[0])

            def parts(enc):
                dve.wait_ge(tile_summed, ENC_TILES * (enc + 1))
                step(dve.tensor_scalar(rstd_bc[:], dev_sum[:], 1.0 / ENC_TILES, None, ALU.mult))
                dve.tensor_tensor(mean_bc[:], rstd_bc[:], shift[:], ALU.add).then_inc(part_means, 1)
                step(dve.tensor_tensor(rstd_bc[:], rstd_bc[:], dev_sum[:], ALU.mult))
                step(dve.tensor_tensor(rstd_bc[:], dev_sq[:], rstd_bc[:], ALU.subtract))

            def combine(enc):
                dve.wait_ge(mean_done, enc + 1)
                step(dve.tensor_tensor(dev[:], mean_bc[:], ps_mean[:], ALU.subtract))
                step(dve.tensor_tensor(dev[:], dev[:], dev[:], ALU.mult))
                dve.tensor_copy(mean_bc[:], ps_mean[:])
                dve.scalar_tensor_tensor(rstd_bc[:], dev[:], float(ENC_TILES), rstd_bc[:],
                                         ALU.mult, ALU.add).then_inc(part_vars, 1)

            def rstd(enc):
                dve.wait_ge(std_done, enc + 1)
                step(dve.reciprocal(rstd_bc[:], rstd_bc[:]))

            def normalise(enc, job, number, half_number):
                j = number % 2
                dve.wait_ge(loaded[j], 16 * (half_number + 1))
                dve.tensor_tensor(load_sb[:, j, :], load_sb[:, j, :], mean_bc[:], ALU.subtract) \
                    .then_inc(z_centred, 1)
                dve.wait_ge(z_centred, KT * enc + job + 1)
                dve.tensor_tensor(load_sb[:, j, :], load_sb[:, j, :], rstd_bc[:], ALU.mult) \
                    .then_inc(z_done, 1)

            def jobs(enc, i, start, js, sums):
                for j in js:
                    if sums:
                        add_sum(2 * i + j, j)
                    for c in range(j * JOBS // 2, (j + 1) * JOBS // 2):
                        normalise(enc, JOBS * (i - start) + c, c,
                                  NORM_BASE[enc] + JOBS // 2 * (i - start) + c // 2)

            fill(0)
            first_sum(0, 0)
            add_sum(1, 1)
            pairs(ER1 + 1, EI1)
            parts(0)
            combine(0)
            first_sum(2 * EI1, 0)
            add_sum(2 * EI1 + 1, 1)
            rstd(0)
            with dve.Fori(NORM_PAIRS[0], NORM_PAIRS[0] + NORM_LEN) as i:
                jobs(0, i, NORM_PAIRS[0], (0, 1), True)
            pairs(NORM_PAIRS[0] + NORM_LEN, TOP)
            parts(1)
            combine(1)
            rstd(1)
            fill(1)
            with dve.Fori(NORM_PAIRS[1], NORM_PAIRS[1] + NORM_LEN) as i:
                jobs(1, i, NORM_PAIRS[1], (0, 1), False)
            fill(2)


GROUPS = 4
GR = P // GROUPS
NB = N * P
ROW_TILES = B // P
SCALE = float(HD) ** -0.5
MAG_EPS = 1e-8
DK = D // P


def attention_phase(nc, t, scr, strength):
    with ExitStack() as ctx:
        def sb(name, shape, dt=F32):
            return ctx.enter_context(nc.sbuf_tensor(name, shape, dt))

        def sem(name):
            return ctx.enter_context(nc.semaphore(name))

        wts = [sb("qkv_hi", [P, 6, DK, D], F32R), sb("qkv_lo", [P, 6, DK, D], F32R)]
        s_stage = [sb(f"s{c}_stage", [P, DK, N, P]) for c in "ri"]
        s = [[sb(f"s{c}_{part}", [P, DK, GROUPS, P], F32R) for part in ("hi", "lo")] for c in "ri"]
        q_cat = sb("q_cat", [P, 2, 2, GROUPS, P])
        k_both = sb("k_both", [P, 2, 2, 2, GROUPS, P])
        v_sb = sb("v_sb", [P, GROUPS, HEADS, 2, HD])
        masked = sb("masked", [P, GROUPS, 2 * N, GR])
        scores = sb("scores", [P, HEADS, GROUPS, 2, N])
        mag = sb("mag", [P, HEADS * GROUPS, N])
        top = sb("top", [P, HEADS * GROUPS])
        total = sb("total", [P, HEADS * GROUPS])
        spread = sb("spread", [P, 2, GROUPS, N, GR])
        spread_t = sb("spread_t", [P, 2, GROUPS, P])
        o_sb = sb("o_sb", [P, 2, N, P])
        same_row = sb("same_row", [P, GR])
        ident = sb("ident", [P, P])
        qk_bias = sb("qk_bias", [P, 5, DK])
        v_bias = sb("v_bias", [P, HEADS])
        mag_eps = sb("mag_eps", [P, 1])
        ids = sb("ids", [P, ROW_TILES, N], I32)
        banks = ctx.enter_context(nc.psum_tensor("banks", [P, 4, HALF], F32))
        ps_x = ctx.enter_context(nc.psum_tensor("ps_x", [P, 4, HALF], F32))
        ps_scores = ps_x[:, 0:2, :]
        ps_pt = [ps_x[:, 2, :], ps_x[:, 0, :]]
        ps_o = [ps_x[:, 3, :], ps_x[:, 1, :]]

        consts_loaded = sem("a_consts_loaded")
        consts_set = sem("a_consts_set")
        bias_negated = sem("bias_negated")
        gathered = sem("gathered")
        mat_loaded = [sem(f"mat_loaded{j}") for j in range(4)]
        mat_rounded = sem("mat_rounded")
        mat_split = sem("mat_split")
        s_loaded = [sem(f"s_{c}_loaded") for c in "ri"]
        s_rounded = sem("s_rounded")
        s_split = sem("s_split")
        bank_full = sem("bank_full")
        bank_read = sem("bank_read")
        scores_done = sem("scores_done")
        scores_masked = sem("scores_masked")
        scores_kept = sem("scores_kept")
        soft = sem("soft")
        mag2_done = sem("mag2_done")
        mag_done = sem("mag_done")
        mag_less = sem("mag_less")
        exp_done = sem("exp_done")
        weights_done = sem("weights_done")
        spread_done = sem("spread_done")
        turned = sem("turned")
        turned_out = sem("turned_out")
        o_done = sem("o_done")
        o_out = sem("o_out")
        o_stored = [sem(f"o_stored{j}") for j in range(2)]

        block = ctx.enter_context(nc.Block())

        BANKS = 4
        QK_PLACES = 2 * 2
        FILLS = 4 * DK + 2 * GROUPS
        mat_stage = [x.rearrange(pattern)[:, j * DK * D:(j + 1) * DK * D] for x, pattern in
                     ((k_both[:], "p e a k g x -> p (e a k g x)"), (v_sb[:], "p g h c d -> p (g h c d)"))
                     for j in range(2)]
        mat_stage += mat_stage[2:]
        s_src = [scr["u"][L1_TILES + ENC_TILES * c:L1_TILES + ENC_TILES * (c + 1)]
                 .rearrange("(n k) p (t b) -> t p k n b", k=DK, b=P) for c in range(2)]

        @block.sync
        def _(sp):
            sp.dma_start(qk_bias[:, 0:4, :], t["qk_bias"]).then_inc(consts_loaded, 16)
            sp.dma_start(v_bias[:], t["v_bias"]).then_inc(consts_loaded, 16)
            sp.dma_start(ids[:], t["ids"]).then_inc(consts_loaded, 16)

            def load_s(tile, c):
                for k in range(DK):
                    sp.dma_start(s_stage[c][:, k, :, :], s_src[c][tile, :, k, :, :]) \
                        .then_inc(s_loaded[c], 16)

            for j in range(2):
                sp.sem_inc(o_stored[j], 16)
            for m in range(6):
                if m == 0:
                    load_s(0, 0)
                if m == 2:
                    load_s(0, 1)
                if m >= 4:
                    sp.wait_ge(mat_split, m - 1)
                sp.dma_start(mat_stage[m], t["qkv"][m]).then_inc(mat_loaded[m % 4], 16)

            def store_o(tile):
                for h in range(HEADS):
                    sp.wait_ge(o_out, 2 + HEADS * tile + h + 1)
                    sp.dma_start(scr["o"][tile, h], o_sb[:, h % 2, :, :].rearrange("p n b -> p (n b)")) \
                        .then_inc(o_stored[h % 2], 16)

            with sp.Fori(0, ROW_TILES - 1) as tile:
                for c in range(2):
                    sp.wait_ge(s_split, 2 * tile + c + 1)
                    load_s(tile + 1, c)
                store_o(tile)
            store_o(ROW_TILES - 1)
            for j in range(2):
                sp.wait_ge(o_stored[j], 16 * (HEADS // 2 * ROW_TILES + 1))

        @block.gpsimd
        def _(pool):
            pool.memset(mag_eps[:], MAG_EPS).then_inc(consts_set, 1)
            pool.memset(ident[:], 0.0).then_inc(consts_set, 1)
            pool.memset(same_row[:], 0.0).then_inc(consts_set, 1)
            pool.wait_ge(consts_set, 3)
            pool.affine_select(out=ident[:], in_=ident[:], compare_op=ALU.not_equal, fill=1.0,
                               base=0, pattern=[[-1, P]], channel_multiplier=1).then_inc(consts_set, 1)
            for n in range(N):
                pool.wait_ge(consts_set, 4 + n)
                pool.affine_select(out=same_row[:], in_=same_row[:], compare_op=ALU.not_equal,
                                   fill=1.0, base=-GR * n, pattern=[[-1, GR]],
                                   channel_multiplier=1).then_inc(consts_set, 1)
            pool.wait_ge(consts_loaded, 48)
            for tile in range(ROW_TILES):
                for n in range(N):
                    pool.indirect_dma_start(
                        out=strength[:, tile, n, :], out_offset=None, in_=t[f"tbl_{n}"],
                        in_offset=bass.IndirectOffsetOnAxis(ap=ids[:, tile, n:n + 1], axis=0)) \
                        .then_inc(gathered, 16)
            pool.wait_ge(gathered, 16 * N * ROW_TILES)

        CONSTS = 4 + N

        @block.tensor
        def _(pe):
            def fill_bank(tile, x, products):
                pe.wait_ge(bank_read, FILLS * tile + x + 1)
                for n, (lhs, rhs) in enumerate(products):
                    last = pe.matmul(banks[:, x % BANKS, :], lhs, rhs, start=n == 0,
                                     stop=n == len(products) - 1)
                last.then_inc(bank_full, 1)

            def project(tile, et, m):
                c = m // 2
                fill_bank(tile, 4 * et + m,
                          [(wts[wp][:, m, k, et * P:(et + 1) * P], s[c][sp_][:, k, :, :])
                           for k in range(DK) for wp, sp_ in PARTS])

            def values(tile, c, g):
                fill_bank(tile, 4 * DK + GROUPS * c + g,
                          [(s[c][sp_][:, k, g, :], wts[wp][:, 4 + c, k, :])
                           for k in range(DK) for wp, sp_ in PARTS])

            def score(tile, h):
                et, a = h // 2, h % 2
                pe.wait_ge(bank_read, BANKS + FILLS * tile + 4 * (et + 1))
                pe.wait_ge(scores_masked, HEADS * tile + h + 1)
                if h == 0:
                    pe.wait_ge(turned_out, 2 + HEADS * tile)
                    pe.wait_ge(o_out, 2 + HEADS * tile)
                for g in range(GROUPS):
                    last = pe.matmul(ps_scores[:, g // 2, (g % 2) * 2 * P:(g % 2 + 1) * 2 * P],
                                     q_cat[:, et % 2, a, g, :], k_both[:, et % 2, a, :, g, :],
                                     start=True, stop=True)
                last.then_inc(scores_done, 1)

            def turn(tile, h):
                pe.wait_ge(spread_done, HEADS * tile + h + 1)
                pe.wait_ge(turned_out, HEADS * tile + h + 1)
                for g in range(GROUPS):
                    last = pe.transpose(ps_pt[h % 2][:, g * P:(g + 1) * P],
                                        spread[:, h % 2, g, :, :].rearrange("p m b -> p (m b)"),
                                        ident[:])
                last.then_inc(turned, 1)

            def weigh(tile, h):
                if h == 0:
                    pe.wait_ge(bank_read, BANKS + FILLS * (tile + 1))
                pe.wait_ge(turned_out, 2 + HEADS * tile + h + 1)
                pe.wait_ge(o_out, HEADS * tile + h + 1)
                for g in range(GROUPS):
                    last = pe.matmul(ps_o[h % 2][:, g * P:(g + 1) * P],
                                     v_sb[:, g, h, :, :].rearrange("p c d -> p (c d)"),
                                     spread_t[:, h % 2, g, :], start=True, stop=True)
                last.then_inc(o_done, 1)

            pe.sem_inc(scores_done, QK_PLACES)
            pe.sem_inc(bank_full, FILLS)
            pe.sem_inc(turned, 2)
            pe.wait_ge(consts_set, CONSTS)
            with pe.Fori(0, ROW_TILES) as tile:
                for et in range(DK):
                    for m in range(4):
                        if et == 0 and m % 2 == 0:
                            pe.wait_ge(s_split, 2 * tile + m // 2 + 1)
                        if et == 0:
                            pe.wait_ge(mat_split, m + 1)
                        project(tile, et, m)
                        if et and m % 2:
                            score(tile, 2 * (et - 1) + m // 2)
                pe.wait_ge(mat_split, 6)
                for c in range(2):
                    for g in range(GROUPS):
                        values(tile, c, g)
                        if c == 0 and g < 2:
                            score(tile, 2 * (DK - 1) + g)
                turn(tile, 0)
                for h in range(HEADS):
                    if h + 1 < HEADS:
                        turn(tile, h + 1)
                    weigh(tile, h)

        @block.scalar
        def _(act):
            act.sem_inc(bank_read, BANKS)
            act.sem_inc(turned_out, 2)
            act.sem_inc(o_out, 2)
            act.wait_ge(consts_loaded, 48)
            act.mul(qk_bias[:, 4, :], qk_bias[:, 3, :], -1.0).then_inc(bias_negated, 1)
            act.wait_ge(bias_negated, 1)
            act.wait_ge(consts_set, CONSTS)
            for m in range(6):
                act.wait_ge(mat_loaded[m % 4], 16 * (m // 4 + 1))
                act.activation(wts[0][:, m, :, :].rearrange("p k e -> p (k e)"), mat_stage[m],
                               ACT.Copy).then_inc(mat_rounded, 1)

            def read_qk(tile, et, m):
                act.wait_ge(bank_full, FILLS * (tile + 1) + 4 * et + m + 1)
                if m == 0:
                    act.wait_ge(scores_done, HEADS * tile + 2 * et + 2)
                imag, par = m // 2, et % 2
                here = slice(imag * HD, (imag + 1) * HD)
                there = slice((1 - imag) * HD, (2 - imag) * HD)
                for a in range(2):
                    src = slice(a * HD, (a + 1) * HD)

                    def put(dst, scale, col):
                        return act.activation(dst.rearrange("p g x -> p (g x)"),
                                              banks[src, (4 * et + m) % BANKS, :], ACT.Identity,
                                              scale=scale, bias=qk_bias[src, col, et:et + 1])
                    if m % 2 == 0:
                        last = put(q_cat[here, par, a, :, :], 1.0, m)
                    else:
                        put(k_both[here, par, a, 0, :, :], 1.0, m)
                        last = put(k_both[there, par, a, 1, :, :], -1.0 if imag else 1.0,
                                   4 if imag else m)
                last.then_inc(bank_read, 1)

            def read_v(tile, c, g):
                x = 4 * DK + GROUPS * c + g
                act.wait_ge(bank_full, FILLS * (tile + 1) + x + 1)
                act.activation(v_sb[:, g, :, c, :],
                               banks[:, x % BANKS, :].rearrange("p (h d) -> p h d", d=HD), ACT.Copy) \
                    .then_inc(bank_read, 1)

            def read_turned(tile, h):
                act.wait_ge(turned, 2 + HEADS * tile + h + 1)
                act.activation(spread_t[:, h % 2, :, :].rearrange("p g q -> p (g q)"), ps_pt[h % 2],
                               ACT.Copy).then_inc(turned_out, 1)

            def read_o(tile, h):
                act.wait_ge(o_done, HEADS * tile + h + 1)
                act.wait_ge(o_stored[h % 2], 16 * (HEADS // 2 * tile + h // 2 + 1))
                act.activation(o_sb[:, h % 2, :, :].rearrange("p n (g b) -> p g n b", b=GR),
                               ps_o[h % 2].rearrange("p (g n b) -> p g n b", n=N, b=GR), ACT.Identity,
                               bias=v_bias[:, h:h + 1]).then_inc(o_out, 1)

            with act.Fori(0, ROW_TILES) as tile:
                for et in range(DK):
                    for m in range(4):
                        read_qk(tile, et, m)
                for g in range(GROUPS):
                    read_v(tile, 0, g)
                act.wait_ge(mag2_done, tile + 1)
                act.activation(mag[:], mag[:], ACT.Sqrt, bias=mag_eps[:]).then_inc(mag_done, 1)
                read_v(tile, 1, 0)
                act.wait_ge(mag_less, tile + 1)
                act.activation(mag[:], mag[:], ACT.Exp, scale=SCALE).then_inc(exp_done, 1)
                for g in range(1, GROUPS):
                    read_v(tile, 1, g)
                read_turned(tile, 0)
                for h in range(HEADS):
                    if h + 1 < HEADS:
                        read_turned(tile, h + 1)
                    read_o(tile, h)

        @block.vector
        def _(dve):
            dve.sem_inc(scores_masked, 1)
            dve.wait_ge(consts_set, CONSTS)

            def low_mat(m):
                dve.wait_ge(mat_rounded, m + 1)
                dve.tensor_tensor(wts[1][:, m, :, :].rearrange("p k e -> p (k e)"), mat_stage[m],
                                  wts[0][:, m, :, :].bitcast(F32).rearrange("p k e -> p (k e)"),
                                  ALU.subtract).then_inc(mat_split, 1)

            def split_s(tile, c):
                dve.wait_ge(s_loaded[c], 16 * DK * (tile + 1))
                dve.wait_ge(bank_full, FILLS * tile + 4 * DK + GROUPS * (c + 1))
                for k in range(DK):
                    stage_k = s_stage[c][:, k, :, :].rearrange("p n (g b) -> p g n b", b=GR)
                    hi_k = s[c][0][:, k, :, :].rearrange("p g (n b) -> p g n b", b=GR)
                    dve.tensor_copy(hi_k, stage_k).then_inc(s_rounded, 1)
                for k in range(DK):
                    stage_k = s_stage[c][:, k, :, :].rearrange("p n (g b) -> p g n b", b=GR)
                    hi_k = s[c][0][:, k, :, :].rearrange("p g (n b) -> p g n b", b=GR)
                    lo_k = s[c][1][:, k, :, :].rearrange("p g (n b) -> p g n b", b=GR)
                    dve.wait_ge(s_rounded, DK * (2 * tile + c) + k + 1)
                    last = dve.tensor_tensor(lo_k, stage_k, hi_k.bitcast(F32), ALU.subtract)
                last.then_inc(s_split, 1)

            def keep_own_row(tile, h):
                dve.wait_ge(scores_done, QK_PLACES + HEADS * tile + h + 1)
                if h > 0:
                    dve.wait_ge(scores_kept, HEADS * tile + h)
                dve.tensor_tensor(masked[:].rearrange("p g m b -> p (g m) b"),
                                  ps_scores.rearrange("p k (x b) -> p (k x) b", b=GR),
                                  same_row[:].unsqueeze(1).broadcast_to([P, GROUPS * 2 * N, GR]),
                                  ALU.mult).then_inc(scores_masked, 1)
                dve.wait_ge(scores_masked, 1 + HEADS * tile + h + 1)
                dve.tensor_reduce(scores[:, h, :, :, :].rearrange("p g c m -> p (g c m)"),
                                  masked[:].rearrange("p g m b -> p (g m) b"), AX.X, ALU.add) \
                    .then_inc(scores_kept, 1)

            HG = HEADS * GROUPS
            SOFT_STEPS = 4

            def softmax(tile):
                def step(n, instruction):
                    instruction.then_inc(soft, 1)
                    dve.wait_ge(soft, SOFT_STEPS * tile + n)

                sc = scores[:].rearrange("p h g c m -> p (h g) c m")
                dve.wait_ge(scores_kept, HEADS * (tile + 1))
                step(1, dve.tensor_tensor(scores[:], scores[:], scores[:], ALU.mult))
                dve.tensor_tensor(mag[:], sc[:, :, 0, :], sc[:, :, 1, :], ALU.add).then_inc(mag2_done, 1)
                dve.wait_ge(mag_done, tile + 1)
                step(2, dve.tensor_reduce(top[:], mag[:], AX.X, ALU.max))
                dve.tensor_tensor(mag[:], mag[:], top[:].unsqueeze(2).broadcast_to([P, HG, N]),
                                  ALU.subtract).then_inc(mag_less, 1)
                dve.wait_ge(exp_done, tile + 1)
                step(3, dve.tensor_reduce(total[:], mag[:], AX.X, ALU.add))
                step(4, dve.reciprocal(total[:], total[:]))
                dve.tensor_tensor(mag[:], mag[:], total[:].unsqueeze(2).broadcast_to([P, HG, N]),
                                  ALU.mult).then_inc(weights_done, 1)

            def spread_weights(tile, h):
                if h == 0:
                    dve.wait_ge(weights_done, tile + 1)
                dve.wait_ge(turned, HEADS * tile + h + 1)
                dve.tensor_tensor(
                    spread[:, h % 2, :, :, :].rearrange("p g m b -> p (g m) b"),
                    mag[:, h * GROUPS:(h + 1) * GROUPS, :].rearrange("p g m -> p (g m)")
                    .unsqueeze(2).broadcast_to([P, GROUPS * N, GR]),
                    same_row[:].unsqueeze(1).broadcast_to([P, GROUPS * N, GR]),
                    ALU.mult).then_inc(spread_done, 1)

            def attend(tile):
                for h in range(HEADS):
                    keep_own_row(tile, h)
                softmax(tile)
                for h in range(HEADS):
                    spread_weights(tile, h)

            split_s(0, 0)
            for m in range(2):
                low_mat(m)
            split_s(0, 1)
            for m in range(2, 6):
                low_mat(m)
            with dve.Fori(0, ROW_TILES - 1) as tile:
                attend(tile)
                for c in range(2):
                    split_s(tile + 1, c)
            attend(ROW_TILES - 1)



EH = D // 2
KH = DK // 2


def round_int_w(act, int_w, w_stage, n, kh):
    hi = int_w[0][:, n, KH * kh:KH * (kh + 1), :, :]
    act.activation(hi[:, :, 1:3, :], w_stage[:, kh, :, :, :], ACT.Copy)
    return act.activation(hi[:, :, 0, :], w_stage[:, kh, :, 1, :], ACT.Copy, scale=-1.0)


def low_int_w(eng, int_w, w_stage, n, kh):
    hi, lo = (x[:, n, KH * kh:KH * (kh + 1), :, :] for x in int_w)
    eng.tensor_tensor(lo[:, :, 1:3, :], w_stage[:, kh, :, :, :], hi[:, :, 1:3, :].bitcast(F32),
                      ALU.subtract)
    return eng.tensor_tensor(lo[:, :, 0, :], hi[:, :, 2, :].bitcast(F32), w_stage[:, kh, :, 1, :],
                             ALU.subtract)


def output_projection_phase(nc, t, scr, int_w, w_stage):
    with ExitStack() as ctx:
        def sb(name, shape, dt=F32):
            return ctx.enter_context(nc.sbuf_tensor(name, shape, dt))

        def sem(name):
            return ctx.enter_context(nc.semaphore(name))

        wts = [sb("wo_hi", [P, 2, DK, D], F32R), sb("wo_lo", [P, 2, DK, D], F32R)]
        o_stage = sb("o_stage", [P, 2, DK, NB])
        o = [sb("o_hi", [P, 2, DK, NB], F32R), sb("o_lo", [P, 2, DK, NB], F32R)]
        attn_sb = sb("attn_sb", [P, 2 * DK, NB])
        wo_stage = attn_sb[:].rearrange("p (c k) x -> p c k x", c=2)
        wo_bias = sb("wo_bias", [P, 2, DK])
        banks = ctx.enter_context(nc.psum_tensor("wo_banks", [P, 2 * DK, NB], F32))

        bias_loaded = sem("wo_bias_loaded")
        wo_loaded = [sem(f"wo_loaded{c}") for c in range(2)]
        wo_rounded = sem("wo_rounded")
        wo_split = sem("wo_split")
        o_loaded = [sem(f"o_loaded{c}") for c in range(2)]
        o_rounded = sem("o_rounded")
        o_split = sem("o_split")
        bank_full = sem("wo_bank_full")
        bank_read = sem("wo_bank_read")
        attn_stored = [sem(f"attn_stored{c}") for c in range(2)]
        w_loaded = [sem(f"int_loaded_early{kh}") for kh in range(2)]
        w_rounded = sem("int_rounded_early")
        w_split = sem("int_split_early")

        block = ctx.enter_context(nc.Block())
        FILLS = 2 * DK

        @block.sync
        def _(sp):
            sp.dma_start(wo_bias[:], t["wo_bias"]).then_inc(bias_loaded, 16)

            def load(tile, c, first=False):
                if not first:
                    sp.wait_ge(o_split, 2 * (tile - 1) + c + 1)
                for a in range(2):
                    sp.dma_start(o_stage[a * HD:(a + 1) * HD, c, :, :],
                                 scr["o"][tile, a::2, c * HD:(c + 1) * HD, :].rearrange("k d x -> d k x")) \
                        .then_inc(o_loaded[c], 16)

            for c in range(2):
                sp.dma_start(wo_stage[:, c, :, :].rearrange("p k e -> p (k e)"), t["wo"][c]) \
                    .then_inc(wo_loaded[c], 16)
                load(0, c, first=True)
            with sp.Fori(1, ROW_TILES) as tile:
                for c in range(2):
                    load(tile, c)

        @block.gpsimd
        def _(pool):
            def load_w(n, kh):
                pool.dma_start(w_stage[:, kh, :, :, :].rearrange("p k m e -> p (k m e)"),
                               t["int_w"][0, n, :, kh * KH * D:(kh + 1) * KH * D]) \
                    .then_inc(w_loaded[kh], 16)

            for kh in range(2):
                load_w(0, kh)
            for n in range(N):
                for kh in range(2):
                    pool.wait_ge(w_rounded, 2 * n + kh + 1)
                    low_int_w(pool, int_w, w_stage, n, kh).then_inc(w_split, 1)
                    if n + 1 < N:
                        pool.wait_ge(w_split, 2 * n + kh + 1)
                        load_w(n + 1, kh)

        @block.vector
        def _(dve):
            def split(stage, parts, rounded, done, count):
                dve.tensor_copy(parts[0], stage).then_inc(rounded, 1)
                dve.wait_ge(rounded, count)
                dve.tensor_tensor(parts[1], stage, parts[0].bitcast(F32), ALU.subtract).then_inc(done, 1)

            dve.sem_inc(bank_full, FILLS)
            def split_o(tile, c):
                dve.wait_ge(o_loaded[c], 32 * (tile + 1))
                dve.wait_ge(bank_full, FILLS * tile + DK * (c + 1))
                split(o_stage[:, c, :, :], [x[:, c, :, :] for x in o], o_rounded, o_split,
                      2 * tile + c + 1)

            for c in range(2):
                dve.wait_ge(wo_loaded[c], 16)
                split(wo_stage[:, c, :, :], [w[:, c, :, :] for w in wts], wo_rounded, wo_split, c + 1)
                split_o(0, c)
            with dve.Fori(1, ROW_TILES) as tile:
                for c in range(2):
                    split_o(tile, c)

        @block.tensor
        def _(pe):
            with pe.Fori(0, ROW_TILES) as tile:
                for c in range(2):
                    pe.wait_ge(wo_split, c + 1)
                    pe.wait_ge(o_split, 2 * tile + c + 1)
                    for et in range(DK):
                        pe.wait_ge(bank_read, FILLS * tile + DK * c + et + 1)
                        n = 0
                        for k in range(DK):
                            for wp, op in PARTS:
                                last = pe.matmul(banks[:, DK * c + et, :],
                                                 wts[wp][:, c, k, et * P:(et + 1) * P], o[op][:, c, k, :],
                                                 start=n == 0, stop=n == 3 * DK - 1)
                                n += 1
                        last.then_inc(bank_full, 1)

        @block.scalar
        def _(act):
            act.sem_inc(bank_read, FILLS)
            for c in range(2):
                act.sem_inc(attn_stored[c], 16)
            act.wait_ge(bias_loaded, 16)

            def project(tile, c):
                act.wait_ge(attn_stored[c], 16 * (tile + 1))
                for et in range(DK):
                    x = DK * c + et
                    act.wait_ge(bank_full, FILLS * (tile + 1) + x + 1)
                    act.activation(attn_sb[:, x, :], banks[:, x, :], ACT.Identity,
                                   bias=wo_bias[:, c, et:et + 1]).then_inc(bank_read, 1)
                act.wait_ge(bank_read, FILLS * (tile + 1) + DK * (c + 1))
                act.dma_start(scr["attn"][tile, c].rearrange("k p x -> p k x"),
                              attn_sb[:, DK * c:DK * (c + 1), :]).then_inc(attn_stored[c], 16)

            for n in range(N):
                for kh in range(2):
                    for c in range(2):
                        project(2 * n + kh, c)
                    act.wait_ge(w_loaded[kh], 16 * (n + 1))
                    round_int_w(act, int_w, w_stage, n, kh).then_inc(w_rounded, 1)
            for c in range(2):
                act.wait_ge(attn_stored[c], 16 * (ROW_TILES + 1))


PAIRS = ((0, 1), (0, 2), (0, 3), (1, 2), (1, 3), (2, 3))


def interference_phase(nc, t, scr, strength, int_w, w_stage):
    with ExitStack() as ctx:
        def sb(name, shape, dt=F32):
            return ctx.enter_context(nc.sbuf_tensor(name, shape, dt))

        def sem(name):
            return ctx.enter_context(nc.semaphore(name))

        a_stage = sb("a_stage", [P, 2, KH, NB])
        a = [sb("a_hi", [P, 2, DK, NB], F32R), sb("a_lo", [P, 2, DK, NB], F32R)]
        ri = sb("ri", [P, 2, N, 2, EH])
        unit = sb("unit", [P, N, 2, EH])
        sq = sb("ri_squares", [P, N, 2, EH])
        root = sq[:].rearrange("p n c e -> p (n c e)")[:, 0:N * EH]
        newton = sq[:].rearrange("p n c e -> p (n c e)")[:, N * EH:]
        zero = newton.rearrange("p (n e) -> p n e", n=N)
        mag2 = sb("mag2", [P, N, EH])
        mag2_flat = mag2[:].rearrange("p n e -> p (n e)")
        prod = sb("prod", [P, len(PAIRS), 2, EH])
        cos = prod[:, :, 0, :]
        zeros = sb("pair_zeros", [P, len(PAIRS), EH])
        f = zeros[:, 0:N, :]
        sup = sb("sup", [P, 2, 2, EH])
        s_tile = sb("s_tile", [P, 2, N, N])
        tiny = sb("tiny", [P, 1])
        one = sb("one", [P, 1])
        banks = ctx.enter_context(nc.psum_tensor("ri_banks", [P, 2, N, 2, EH], F32))

        w_loaded = [sem(f"int_loaded{kh}") for kh in range(2)]
        w_rounded = sem("int_rounded")
        w_split = [sem(f"int_split{kh}") for kh in range(2)]
        a_loaded = [sem(f"a_loaded{kh}") for kh in range(2)]
        a_rounded = sem("a_rounded")
        a_split = sem("a_split")
        part_done = sem("part_done")
        ri_out = sem("ri_out")
        mag2_done = sem("mag2_done")
        root_done = sem("root_done")
        root2_done = sem("root2_done")
        t_done = sem("t_done")
        factor_done = sem("factor_done")
        zero_done = sem("zero_done")
        inverse_done = sem("inverse_done")
        unit_done = sem("unit_done")
        zeros_done = sem("zeros_done")
        tiny_set = sem("tiny_set")
        step_done = sem("step_done")
        by_factor = sem("by_factor")
        sup_done = sem("sup_done")
        sup_stored = [sem(f"sup_stored{j}") for j in range(2)]

        block = ctx.enter_context(nc.Block())

        ROOT_SCALE = float(2 ** 15)
        TINY = 1e-26
        UNITS = 2 * ROW_TILES
        PARTS_DONE = 2 * N

        def units(eng, body, half, end=ROW_TILES):
            with eng.Fori(0, end // 2) as i:
                for j in range(2):
                    body(2 * i + (j + ROW_TILES * half), 2 * i + j, j, half)

        @block.sync
        def _(sp):
            def load_w(n):
                for kh in range(2):
                    if n:
                        sp.wait_ge(w_split[kh], n)
                    sp.dma_start(w_stage[:, kh, :, :, :].rearrange("p k m e -> p (k m e)"),
                                 t["int_w"][1, n, :, kh * KH * D:(kh + 1) * KH * D]) \
                        .then_inc(w_loaded[kh], 16)

            def load_a(unit_no, tile, c, first=False):
                for kh in range(2):
                    if not first:
                        sp.wait_ge(a_split, 4 * unit_no + 2 * c + kh - 1)
                    sp.dma_start(a_stage[:, kh, :, :],
                                 scr["attn"][tile, c, KH * kh:KH * (kh + 1)].rearrange("k p x -> p k x")) \
                        .then_inc(a_loaded[kh], 16)

            def store(unit_no, tile, j, half):
                sp.wait_ge(sup_done, unit_no + 3)
                sp.dma_start(scr["sup"][tile, :, :, half * EH:(half + 1) * EH].rearrange("c p e -> p c e"),
                             sup[:, j, :, :]).then_inc(sup_stored[j], 16)

            def load_and_store(half):
                with sp.Fori(0, ROW_TILES // 2 - 2) as i:
                    for j in range(2):
                        tile = 2 * i + j
                        for c in range(2):
                            load_a(tile + (3 + ROW_TILES * half), tile + 3, c)
                        store(tile + ROW_TILES * half, tile, j, half)
                for c in range(2):
                    load_a(ROW_TILES - 1 + ROW_TILES * half, ROW_TILES - 1, c)
                store(ROW_TILES - 4 + ROW_TILES * half, ROW_TILES - 4, 0, half)

            for j in range(2):
                sp.sem_inc(sup_stored[j], 16)
            load_a(0, 0, 0, first=True)
            load_a(0, 0, 1)
            for tile in (1, 2):
                for c in range(2):
                    load_a(tile, tile, c)
            load_and_store(0)
            load_a(ROW_TILES, 0, 0)
            for n in range(N):
                load_w(n)
            load_a(ROW_TILES, 0, 1)
            for tile in range(3):
                if tile:
                    for c in range(2):
                        load_a(ROW_TILES + tile, tile, c)
                store(ROW_TILES - 3 + tile, ROW_TILES - 3 + tile, (1 + tile) % 2, 0)
            load_and_store(1)
            for tile in range(ROW_TILES - 3, ROW_TILES):
                store(ROW_TILES + tile, tile, tile % 2, 1)
            for j in range(2):
                sp.wait_ge(sup_stored[j], 16 * (UNITS // 2 + 1))

        def low_w(eng, kh):
            for n in range(N):
                eng.wait_ge(w_rounded, 2 * n + kh + 1)
                low_int_w(eng, int_w, w_stage, n, kh).then_inc(w_split[kh], 1)

        @block.gpsimd
        def _(pool):
            def low_a(unit_no, c):
                for kh in range(2):
                    hi, lo = (x[:, c, KH * kh:KH * (kh + 1), :] for x in a)
                    pool.wait_ge(a_rounded, 4 * unit_no + 2 * c + kh + 1)
                    pool.tensor_tensor(lo, a_stage[:, kh, :, :], hi.bitcast(F32), ALU.subtract) \
                        .then_inc(a_split, 1)

            def add_squares(unit_no):
                pool.wait_ge(ri_out, 2 * unit_no + 6)
                pool.wait_ge(unit_done, unit_no + 1)
                pool.tensor_tensor(mag2[:], sq[:, :, 0, :], sq[:, :, 1, :], ALU.add) \
                    .then_inc(mag2_done, 1)

            def pair_zeros(unit_no):
                pool.wait_ge(zero_done, unit_no + 1)
                pool.wait_ge(sup_done, unit_no + 2)
                at = 0
                for i in range(N - 1):
                    n = N - 1 - i
                    last = pool.tensor_tensor(zeros[:, at:at + n, :], zero[:, i + 1:N, :],
                                              zero[:, i, :].unsqueeze(1).broadcast_to([P, n, EH]),
                                              ALU.add)
                    at += n
                last.then_inc(zeros_done, 1)

            pool.memset(tiny[:], TINY).then_inc(tiny_set, 1)
            pool.memset(one[:], 1.0).then_inc(tiny_set, 1)
            pool.sem_inc(zeros_done, 1)
            for c in range(2):
                low_a(0, c)
            with pool.Fori(1, ROW_TILES) as unit_no:
                low_a(unit_no, 0)
                add_squares(unit_no - 1)
                low_a(unit_no, 1)
                pair_zeros(unit_no - 1)
            low_a(ROW_TILES, 0)
            low_w(pool, 0)
            add_squares(ROW_TILES - 1)
            low_a(ROW_TILES, 1)
            pair_zeros(ROW_TILES - 1)
            with pool.Fori(ROW_TILES + 1, UNITS) as unit_no:
                low_a(unit_no, 0)
                add_squares(unit_no - 1)
                low_a(unit_no, 1)
                pair_zeros(unit_no - 1)
            add_squares(UNITS - 1)
            pair_zeros(UNITS - 1)

        @block.tensor
        def _(pe):
            pe.sem_inc(part_done, PARTS_DONE)

            def products(unit_no, tile, j, half):
                pe.wait_ge(ri_out, 2 * unit_no + 2)
                for c in range(2):
                    for n in range(N):
                        for k in range(DK):
                            if half and k % KH == 0:
                                pe.wait_ge(w_split[k // KH], n + 1)
                            if n == 0 and k % KH == 0:
                                pe.wait_ge(a_split, 4 * unit_no + 2 * c + k // KH + 1)
                            for ap, wp in PARTS:
                                cols = slice(1, 3) if c == 0 else slice(0, 2)
                                last = pe.matmul(banks[:, j, n, :, :].rearrange("p c e -> p (c e)"),
                                                 a[ap][:, c, k, n * P:(n + 1) * P],
                                                 int_w[wp][:, n, k, cols, :].rearrange("p m e -> p (m e)"),
                                                 start=c == 0 and k == 0 and (ap, wp) == PARTS[0],
                                                 stop=c == 1 and k == DK - 1 and (ap, wp) == PARTS[-1])
                        last.then_inc(part_done, 1)

            for half in range(2):
                units(pe, products, half)

        @block.scalar
        def _(act):
            act.sem_inc(ri_out, 4)

            def round_w(n):
                act.wait_ge(part_done, PARTS_DONE * (ROW_TILES + 1) - N + n + 1)
                for kh in range(2):
                    act.wait_ge(w_loaded[kh], 16 * (n + 1))
                    round_int_w(act, int_w, w_stage, n, kh).then_inc(w_rounded, 1)

            def round_a(unit_no, c):
                act.wait_ge(part_done, PARTS_DONE * unit_no + N * (c + 1))
                for kh in range(2):
                    act.wait_ge(a_loaded[kh], 16 * (2 * unit_no + c + 1))
                    act.activation(a[0][:, c, KH * kh:KH * (kh + 1), :], a_stage[:, kh, :, :],
                                   ACT.Copy).then_inc(a_rounded, 1)

            def read(unit_no, tile, j, half, ahead=True):
                act.wait_ge(sup_done, unit_no + 1)
                act.activation(s_tile[:, j, :, :].rearrange("p i j -> p (i j)"),
                               strength[:, bass.ds(tile, 1), :, :].rearrange("p t i j -> p (t i j)"),
                               ACT.Copy)
                for pair in range(2):
                    states = slice(2 * pair, 2 * pair + 2)
                    act.wait_ge(part_done, PARTS_DONE * (unit_no + 1) + N + 2 * (pair + 1))
                    act.activation(ri[:, j, states, :, :], banks[:, j, states, :, :], ACT.Copy)
                    if pair == 0:
                        act.wait_ge(inverse_done, unit_no + 1)
                        act.wait_ge(zeros_done, unit_no + 1)
                    act.activation(sq[:, states, :, :], banks[:, j, states, :, :], ACT.Square) \
                        .then_inc(ri_out, 1)
                if ahead:
                    round_a(unit_no + 1, 1)
                act.wait_ge(mag2_done, unit_no + 1)
                act.activation(root, mag2_flat, ACT.Abs_reciprocal_sqrt, scale=ROOT_SCALE ** 2,
                               bias=tiny[:]).then_inc(root_done, 1)
                act.wait_ge(root_done, unit_no + 1)
                act.activation(newton, root, ACT.Square, scale=ROOT_SCALE).then_inc(root2_done, 1)
                act.wait_ge(t_done, unit_no + 1)
                act.activation(mag2_flat, newton, ACT.Copy, scale=-0.5 * ROOT_SCALE,
                               bias=1.5 * ROOT_SCALE).then_inc(factor_done, 1)
                act.wait_ge(factor_done, unit_no + 1)
                act.activation(newton, newton, ACT.Relu, scale=-2.0, bias=one[:]) \
                    .then_inc(zero_done, 1)

            def unit_and_next(unit_no, tile, j, half):
                read(unit_no, tile, j, half)
                round_a(unit_no + 2, 0)

            act.wait_ge(tiny_set, 2)
            round_a(0, 0)
            round_a(0, 1)
            round_a(1, 0)
            units(act, unit_and_next, 0, ROW_TILES - 2)
            unit_and_next(ROW_TILES - 2, ROW_TILES - 2, 0, 0)
            for n in range(N):
                round_w(n)
            unit_and_next(ROW_TILES - 1, ROW_TILES - 1, 1, 0)
            units(act, unit_and_next, 1, ROW_TILES - 2)
            read(UNITS - 2, ROW_TILES - 2, 0, 1)
            read(UNITS - 1, ROW_TILES - 1, 1, 1, ahead=False)

        @block.vector
        def _(dve):
            dve.sem_inc(sup_done, 2)
            dve.sem_inc(inverse_done, 1)
            dve.sem_inc(unit_done, 1)

            def newton_t(unit_no):
                dve.wait_ge(root2_done, unit_no + 1)
                dve.tensor_tensor(newton, newton, mag2_flat, ALU.mult).then_inc(t_done, 1)

            def superpose(unit_no, tile, j, half, ahead=True):
                STEPS = 7
                count = [0]

                def step(*instructions):
                    instructions[-1].then_inc(step_done, 1)
                    count[0] += 1
                    dve.wait_ge(step_done, STEPS * unit_no + count[0])

                def by_part(x, n):
                    return x.unsqueeze(2).broadcast_to([P, n, 2, EH])

                z = ri[:, j, :, :, :]
                dve.wait_ge(factor_done, unit_no + 1)
                dve.tensor_tensor(mag2_flat, root, mag2_flat, ALU.mult).then_inc(inverse_done, 1)
                dve.wait_ge(inverse_done, unit_no + 2)
                dve.wait_ge(sup_done, unit_no + 2)
                dve.tensor_tensor(unit[:], z, by_part(mag2[:], N), ALU.mult).then_inc(unit_done, 1)
                dve.wait_ge(unit_done, unit_no + 2)
                at, made = 0, []
                for i in range(N - 1):
                    n = N - 1 - i
                    made.append(dve.tensor_tensor(
                        prod[:, at:at + n, :, :], unit[:, i + 1:N, :, :],
                        unit[:, i, :, :].unsqueeze(1).broadcast_to([P, n, 2, EH]), ALU.mult))
                    at += n
                step(*made)
                step(dve.tensor_tensor(cos, cos, prod[:, :, 1, :], ALU.add))
                dve.wait_ge(zeros_done, unit_no + 2)
                step(dve.tensor_tensor(cos, cos, zeros[:], ALU.add))
                others = [[i for i in range(N) if i != m] for m in range(N)]

                def cosine(i, m):
                    return prod[:, PAIRS.index((min(i, m), max(i, m))), 0, :]

                step(*[dve.tensor_scalar(f[:, m, :], cosine(others[m][0], m),
                                         s_tile[:, j, others[m][0], m:m + 1],
                                         s_tile[:, j, m, m:m + 1],
                                         ALU.mult, ALU.add) for m in range(N)])
                for o in (1, 2):
                    step(*[dve.scalar_tensor_tensor(f[:, m, :], cosine(others[m][o], m),
                                                    s_tile[:, j, others[m][o], m:m + 1], f[:, m, :],
                                                    ALU.mult, ALU.add) for m in range(N)])
                dve.tensor_tensor(unit[:], z, by_part(f, N), ALU.mult).then_inc(by_factor, 1)
                if ahead:
                    newton_t(unit_no + 1)
                dve.wait_ge(by_factor, unit_no + 1)
                step(dve.tensor_tensor(unit[:, 0:2, :, :], unit[:, 0:2, :, :], unit[:, 2:4, :, :],
                                       ALU.add))
                assert count[0] == STEPS
                dve.wait_ge(sup_stored[j], 8 * unit_no + 16 - 8 * j)
                dve.tensor_tensor(sup[:, j, :, :], unit[:, 0, :, :], unit[:, 1, :, :], ALU.add) \
                    .then_inc(sup_done, 1)

            newton_t(0)
            units(dve, superpose, 0, ROW_TILES - 2)
            superpose(ROW_TILES - 2, ROW_TILES - 2, 0, 0, ahead=False)
            low_w(dve, 1)
            newton_t(ROW_TILES - 1)
            superpose(ROW_TILES - 1, ROW_TILES - 1, 1, 0)
            units(dve, superpose, 1, ROW_TILES - 2)
            superpose(UNITS - 2, ROW_TILES - 2, 0, 1)
            superpose(UNITS - 1, ROW_TILES - 1, 1, 1, ahead=False)


def top_phase(nc, t, scr, out):
    with ExitStack() as ctx:
        def sb(name, shape, dt=F32):
            return ctx.enter_context(nc.sbuf_tensor(name, shape, dt))

        def sem(name):
            return ctx.enter_context(nc.semaphore(name))

        TILES_HALF = ROW_TILES // 2
        EPS_NORM, EPS_LN = range(2)
        MR, MI, NEG_MI, POST = range(4)
        LOADS = ("Mr", "Mi", "post", "top1", "top2")
        PLACES = (MR, MI, POST, MR, MI)
        TOP2_WIDTH = D // 2
        wts = [sb(f"top_w_{part}", [P, 4, DK, D], F32R) for part in ("hi", "lo")]
        w_stage = sb("top_w_stage", [P, DK, D])
        w3 = sb("w3", [P, 2])
        sup = sb("top_sup", [P, 2, 2, D])
        norm = sb("norm", [P, ROW_TILES])
        unread = sb("unread", [P, 2 * D])
        sup_t = [[sb(f"sup_t{h}_{part}", [P, 2, DK, HALF], F32R) for part in ("hi", "lo")]
                 for h in range(2)]
        amp_0 = [sb(f"amp_0_{part}", [P, DK, HALF], F32R) for part in ("hi", "lo")]
        amp_t = [[x[:] for x in amp_0], [x[:, 0, :, :] for x in sup_t[0]]]
        z_t = [[x[:, 1, :, :] for x in sup_t[0]], [x[:, 0, :, :] for x in sup_t[1]]]
        h1_t = [[x[:, 1, :, :] for x in sup_t[1]], [x[:] for x in amp_0]]
        sq = sb("top_sq", [P, 2, 2, HALF])
        amp = sb("amp", [P, 2, HALF])
        y = sb("y", [P, DK, B])
        y_sum = sb("y_sum", [P, B])
        x_part = sb("x_part", [P, 2, HALF])
        stages = [x[:, :, 0:TOP2_WIDTH if name == "top2" else D] for name, x in
                  zip(LOADS, (w_stage, y[:, :, 0:D], y[:, :, D:2 * D], w_stage, w_stage))]
        h2 = y[:, 0:2, :]
        y_out = y_sum[0:1, :]
        cols = sb("top_cols", [P, 3 * DK + 2])
        consts = sb("top_consts", [P, 2])
        averager = sb("top_averager", [P, P])
        ident = sb("top_ident", [P, P])
        ps_turn = ctx.enter_context(nc.psum_tensor("ps_turn", [P, 2, DK, P], F32))
        banks = ctx.enter_context(nc.psum_tensor("top_banks", [P, 4, HALF], F32))
        ps_sum = ctx.enter_context(nc.psum_tensor("ps_sum", [P, 2, HALF], F32))

        cols_loaded = sem("cols_loaded")
        consts_set = sem("t_consts_set")
        tw_loaded = [sem(f"{name}_loaded") for name in LOADS]
        tw_rounded = sem("tw_rounded")
        tw_split = [sem(f"{name}_split") for name in LOADS]
        neg_rounded = sem("neg_Mi_rounded")
        neg_split = sem("neg_Mi_split")
        sup_loaded = [sem(f"sup_loaded{j}") for j in range(2)]
        norm2_done = sem("norm2_done")
        norm_done = sem("norm_done")
        norm_inverted = sem("norm_inverted")
        scaled = sem("scaled")
        turned = sem("sup_turned")
        sup_rounded = sem("sup_rounded")
        sup_split = sem("sup_split")
        filled = sem("bank_filled")
        act_read = sem("act_read")
        dve_read = sem("dve_read")
        amp2_done = sem("amp2_done")
        amp_done = sem("amp_done")
        amp_rounded = sem("amp_rounded")
        amp_split = sem("amp_split")
        ln_step = sem("t_ln_step")
        summed = sem("summed")
        averaged = sem("averaged")
        less_mean = sem("less_mean")
        squared = sem("t_squared")
        std_done = sem("t_std_done")
        z_done = sem("t_z_done")
        gelu_done = sem("t_gelu_done")
        z_rounded = sem("z_rounded")
        z_split = sem("z_split")
        x_loaded = [sem(f"x_loaded{j}") for j in range(2)]
        h1_rounded = sem("h1_rounded")
        h1_split = sem("h1_split")
        y_done = sem("y_done")
        y_read = sem("y_read")
        y_stored = sem("y_stored")

        block = ctx.enter_context(nc.Block())

        MEAS_FILLS, POST_FILLS, TOP1_FILLS = 4 * DK, 2 * DK, 2 * DK
        AT_POST = MEAS_FILLS
        AT_TOP1 = AT_POST + POST_FILLS
        AT_TOP2 = AT_TOP1 + TOP1_FILLS

        def rows(h):
            return slice(h * HALF, (h + 1) * HALF)

        @block.sync
        def _(sp):
            sp.dma_start(cols[:], t["top_cols"]).then_inc(cols_loaded, 16)
            sp.dma_start(w3[:], t["w_top3"]).then_inc(cols_loaded, 16)

            def load_sup(tile):
                if tile >= 2:
                    sp.wait_ge(turned, tile - 1)
                sp.dma_start(sup[:, tile % 2, :, :], scr["sup"][tile].rearrange("c p e -> p c e")) \
                    .then_inc(sup_loaded[tile % 2], 16)

            def load_w(m):
                if m >= 3:
                    sp.wait_ge(tw_split[(0, 3)[m - 3]], 1)
                sp.dma_start(stages[m], t["w_" + LOADS[m]].rearrange("p (k e) -> p k e", k=DK)) \
                    .then_inc(tw_loaded[m], 16)

            load_sup(0)
            load_w(0)
            load_sup(1)
            load_w(1)
            for tile in range(2, TILES_HALF):
                load_sup(tile)
            load_w(2)
            for tile in range(TILES_HALF, ROW_TILES):
                load_sup(tile)
            load_w(3)
            load_w(4)
            for h in range(2):
                for et in range(DK):
                    x = DK * h + et
                    if x >= 2:
                        sp.wait_ge(dve_read, x - 1)
                    sp.dma_start(x_part[:, x % 2, :], scr["u"][2 * ENC_TILES + et, :, rows(h)]) \
                        .then_inc(x_loaded[x % 2], 16)
            sp.wait_ge(y_read, 2)
            sp.dma_start(out.rearrange("b x -> x b"), y_out).then_inc(y_stored, 16)
            sp.wait_ge(y_stored, 16)

        def low_weights(eng, m):
            eng.wait_ge(tw_rounded, m + 1)
            hi, lo = (x[:, PLACES[m], :, 0:stages[m].shape[2]] for x in wts)
            eng.tensor_tensor(lo, stages[m], hi.bitcast(F32), ALU.subtract).then_inc(tw_split[m], 1)

        @block.gpsimd
        def _(pool):
            pool.memset(averager[:], 1.0 / P).then_inc(consts_set, 1)
            pool.memset(consts[:, EPS_NORM:EPS_NORM + 1], MAG_EPS).then_inc(consts_set, 1)
            pool.memset(consts[:, EPS_LN:EPS_LN + 1], LN_EPS).then_inc(consts_set, 1)
            pool.memset(ident[:], 0.0).then_inc(consts_set, 1)
            pool.wait_ge(consts_set, 4)
            pool.affine_select(out=ident[:], in_=ident[:], compare_op=ALU.not_equal, fill=1.0,
                               base=0, pattern=[[-1, P]], channel_multiplier=1).then_inc(consts_set, 1)
            for m in range(1, len(LOADS)):
                if m == 1:
                    pool.wait_ge(tw_rounded, m + 1)
                    pool.tensor_tensor(wts[1][:, NEG_MI], wts[0][:, MI].bitcast(F32), stages[1],
                                       ALU.subtract).then_inc(neg_split, 1)
                else:
                    low_weights(pool, m)

        @block.tensor
        def _(pe):
            def turn(tile):
                pe.wait_ge(scaled, tile + 1)
                if tile:
                    pe.wait_ge(sup_split, tile)
                for c in range(2):
                    for k in range(DK):
                        last = pe.transpose(ps_turn[:, c, k, :], sup[:, tile % 2, c, k * P:(k + 1) * P],
                                            ident[:])
                last.then_inc(turned, 1)

            def fill(x, terms, et):
                before = x - 4
                if before >= AT_TOP2:
                    pe.wait_ge(act_read, AT_TOP1 + before - AT_TOP2 + 1)
                elif before >= AT_TOP1:
                    pe.wait_ge(dve_read, before - AT_TOP1 + 1)
                elif before >= 0:
                    pe.wait_ge(act_read, before + 1)
                all_mm = [(wts[wp][:, place, k, et * P:(et + 1) * P], mov[mp][:, k, :])
                          for place, mov in terms for k in range(DK) for wp, mp in PARTS]
                for n, (lhs, rhs) in enumerate(all_mm):
                    last = pe.matmul(banks[:, x % 4, :], lhs, rhs, start=n == 0,
                                     stop=n == len(all_mm) - 1)
                last.then_inc(filled, 1)

            def average(h, number):
                pe.wait_ge(summed, number + 1)
                pe.matmul(ps_sum[:, h, :], averager[:], y_sum[:, rows(h)], start=True, stop=True) \
                    .then_inc(averaged, 1)

            pe.wait_ge(consts_set, 5)
            for tile in range(TILES_HALF):
                turn(tile)
            pe.wait_ge(tw_split[0], 1)
            pe.wait_ge(tw_split[1], 1)
            pe.wait_ge(neg_rounded, 1)
            pe.wait_ge(neg_split, 1)
            for h in range(2):
                pe.wait_ge(sup_split, TILES_HALF * (h + 1))
                real, imag = ([x[:, c, :, :] for x in sup_t[h]] for c in range(2))
                for et in range(DK):
                    fill(2 * DK * h + 2 * et, [(MR, real), (NEG_MI, imag)], et)
                    fill(2 * DK * h + 2 * et + 1, [(MI, real), (MR, imag)], et)
                    if h == 0:
                        turn(TILES_HALF + et)
            pe.wait_ge(tw_split[2], 1)
            for h in range(2):
                pe.wait_ge(amp_split, DK * (h + 1))
                for et in range(DK):
                    fill(AT_POST + DK * h + et, [(POST, amp_t[h])], et)
                    if h == 1 and et == 0:
                        average(0, 0)
            for number, h in ((1, 0), (2, 1), (3, 1)):
                average(h, number)
            pe.wait_ge(tw_split[3], 1)
            pe.wait_ge(tw_split[4], 1)
            for h in range(2):
                pe.wait_ge(z_split, h + 1)
                for et in range(DK):
                    fill(AT_TOP1 + DK * h + et, [(MR, z_t[h])], et)
            for h in range(2):
                pe.wait_ge(h1_split, DK * (h + 1))
                for et in range(2):
                    fill(AT_TOP2 + 2 * h + et, [(MI, h1_t[h])], et)
            pe.wait_ge(cols_loaded, 32)
            for h in range(2):
                pe.wait_ge(act_read, AT_TOP1 + 2 * (h + 1))
                for k in range(2):
                    last = pe.matmul(ps_sum[0:1, h, :], w3[:, k:k + 1], h2[:, k, rows(h)],
                                     start=k == 0, stop=k == 1)
                last.then_inc(y_done, 1)

        @block.scalar
        def _(act):
            def norms(tile):
                act.wait_ge(sup_loaded[tile % 2], 16 * (tile // 2 + 1))
                act.activation(unread[:],
                               sup[:, tile % 2, :, :].rearrange("p c e -> p (c e)"), ACT.Square,
                               accum_out=norm[:, tile:tile + 1]).then_inc(norm2_done, 1)
                act.wait_ge(norm2_done, tile + 1)
                act.activation(norm[:, tile:tile + 1], norm[:, tile:tile + 1], ACT.Sqrt,
                               bias=consts[:, EPS_NORM:EPS_NORM + 1]).then_inc(norm_done, 1)

            def round_sup(tile):
                act.wait_ge(turned, tile + 1)
                h, at = tile // TILES_HALF, tile % TILES_HALF * P
                act.activation(sup_t[h][0][:, :, :, at:at + P], ps_turn[:], ACT.Copy) \
                    .then_inc(sup_rounded, 1)

            def squares(x):
                if x >= 4:
                    act.wait_ge(amp2_done, x // 2 - 1)
                act.wait_ge(filled, x + 1)
                act.activation(sq[:, x // 2 % 2, x % 2, :], banks[:, x % 4, :], ACT.Square) \
                    .then_inc(act_read, 1)

            def root(n):
                act.wait_ge(amp2_done, n + 1)
                act.activation(amp[:, n % 2, :], amp[:, n % 2, :], ACT.Sqrt).then_inc(amp_done, 1)

            def round_weights(m):
                act.wait_ge(tw_loaded[m], 16)
                act.activation(wts[0][:, PLACES[m], :, 0:stages[m].shape[2]], stages[m], ACT.Copy) \
                    .then_inc(tw_rounded, 1)

            act.wait_ge(consts_set, 5)
            act.wait_ge(cols_loaded, 32)
            for tile in range(TILES_HALF):
                norms(tile)
                if tile:
                    round_sup(tile - 1)
                if tile < 2:
                    round_weights(tile)
            act.activation(wts[0][:, NEG_MI], stages[1], ACT.Copy, scale=-1.0).then_inc(neg_rounded, 1)
            round_sup(TILES_HALF - 1)
            round_weights(2)
            for n in range(2 * DK):
                if n < TILES_HALF:
                    norms(TILES_HALF + n)
                squares(2 * n)
                squares(2 * n + 1)
                if n:
                    root(n - 1)
                if n < TILES_HALF:
                    round_sup(TILES_HALF + n)
            root(2 * DK - 1)
            round_weights(3)

            def read_post(h, et):
                x = AT_POST + DK * h + et
                act.wait_ge(filled, x + 1)
                act.activation(y[:, et, rows(h)], banks[:, x % 4, :], ACT.Identity,
                               bias=cols[:, et:et + 1]).then_inc(act_read, 1)

            def square(h):
                act.wait_ge(less_mean, h + 1)
                if h:
                    act.wait_ge(summed, 3)
                act.activation(sq[:].rearrange("p a c x -> p (a c) x"), y[:, :, rows(h)],
                               ACT.Square).then_inc(squared, 1)

            def std(h):
                act.wait_ge(averaged, 2 * (h + 1))
                act.activation(amp[:, h, :], ps_sum[:, h, :], ACT.Sqrt, scale=1.0 / DK,
                               bias=consts[:, EPS_LN:EPS_LN + 1]).then_inc(std_done, 1)

            def gelu(h):
                act.wait_ge(z_done, h + 1)
                for et in range(DK):
                    last = act.activation(y[:, et, rows(h)], y[:, et, rows(h)], ACT.Gelu,
                                          scale=cols[:, DK + et:DK + et + 1],
                                          bias=cols[:, 2 * DK + et:2 * DK + et + 1])
                last.then_inc(gelu_done, 1)

            for et in range(DK):
                read_post(0, et)
            round_weights(4)
            for et in range(2):
                read_post(1, et)
            square(0)
            for et in range(2, DK):
                read_post(1, et)
            std(0)
            gelu(0)
            square(1)
            std(1)
            gelu(1)
            for h in range(2):
                for et in range(2):
                    x = AT_TOP2 + 2 * h + et
                    act.wait_ge(filled, x + 1)
                    act.activation(h2[:, et, rows(h)], banks[:, x % 4, :], ACT.Relu,
                                   bias=cols[:, 3 * DK + et:3 * DK + et + 1]).then_inc(act_read, 1)
            for h in range(2):
                act.wait_ge(y_done, h + 1)
                act.activation(y_out[:, rows(h)], ps_sum[0:1, h, :], ACT.Copy).then_inc(y_read, 1)

        @block.vector
        def _(dve):
            def scale(tile):
                dve.wait_ge(norm_done, tile + 1)
                dve.reciprocal(norm[:, tile:tile + 1], norm[:, tile:tile + 1]).then_inc(norm_inverted, 1)
                dve.wait_ge(norm_inverted, tile + 1)
                tile_sup = sup[:, tile % 2, :, :]
                dve.tensor_scalar(tile_sup, tile_sup, norm[:, tile:tile + 1], None, ALU.mult) \
                    .then_inc(scaled, 1)

            def low_sup(tile):
                dve.wait_ge(sup_rounded, tile + 1)
                h, at = tile // TILES_HALF, tile % TILES_HALF * P
                hi, lo = (x[:, :, :, at:at + P] for x in sup_t[h])
                dve.tensor_tensor(lo, ps_turn[:], hi.bitcast(F32), ALU.subtract).then_inc(sup_split, 1)

            def add_squares(n):
                dve.wait_ge(act_read, 2 * n + 2)
                dve.tensor_tensor(amp[:, n % 2, :], sq[:, n % 2, 0, :], sq[:, n % 2, 1, :], ALU.add) \
                    .then_inc(amp2_done, 1)

            def split_amp(n):
                h, et = n // DK, n % DK
                hi, lo = (x[:, et, :] for x in amp_t[h])
                dve.wait_ge(amp_done, n + 1)
                dve.tensor_copy(hi, amp[:, n % 2, :]).then_inc(amp_rounded, 1)
                dve.wait_ge(amp_rounded, n + 1)
                dve.tensor_tensor(lo, amp[:, n % 2, :], hi.bitcast(F32), ALU.subtract) \
                    .then_inc(amp_split, 1)

            for tile in range(TILES_HALF):
                scale(tile)
                if tile:
                    low_sup(tile - 1)
                if tile < 2:
                    low_weights(dve, tile)
            low_sup(TILES_HALF - 1)
            for n in range(2 * DK):
                if n < TILES_HALF:
                    scale(TILES_HALF + n)
                if n >= 2:
                    dve.wait_ge(amp_split, n - 1)
                add_squares(n)
                if n:
                    split_amp(n - 1)
                if n < TILES_HALF:
                    low_sup(TILES_HALF + n)
            split_amp(2 * DK - 1)

            steps = [0]

            def step(instruction):
                steps[0] += 1
                instruction.then_inc(ln_step, 1)
                dve.wait_ge(ln_step, steps[0])

            def over_tiles(x):
                return x.unsqueeze(1).broadcast_to([P, DK, HALF])

            def sum_features(h):
                dve.wait_ge(act_read, AT_POST + DK * (h + 1))
                step(dve.tensor_tensor(sq[:, 0, :, :], y[:, 0:2, rows(h)], y[:, 2:4, rows(h)], ALU.add))
                dve.tensor_tensor(y_sum[:, rows(h)], sq[:, 0, 0, :], sq[:, 0, 1, :], ALU.add) \
                    .then_inc(summed, 1)
                dve.wait_ge(summed, 2 * h + 1)

            def subtract_mean(h):
                dve.wait_ge(averaged, 2 * h + 1)
                step(dve.tensor_scalar(y_sum[:, rows(h)], ps_sum[:, h, :], 1.0 / DK, None, ALU.mult))
                dve.tensor_tensor(y[:, :, rows(h)], y[:, :, rows(h)], over_tiles(y_sum[:, rows(h)]),
                                  ALU.subtract).then_inc(less_mean, 1)

            def sum_squares(h):
                dve.wait_ge(less_mean, h + 1)
                dve.wait_ge(squared, h + 1)
                step(dve.tensor_tensor(sq[:, 0, :, :], sq[:, 0, :, :], sq[:, 1, :, :], ALU.add))
                dve.tensor_tensor(y_sum[:, rows(h)], sq[:, 0, 0, :], sq[:, 0, 1, :], ALU.add) \
                    .then_inc(summed, 1)
                dve.wait_ge(summed, 2 * h + 2)

            def normalise(h):
                dve.wait_ge(std_done, h + 1)
                step(dve.reciprocal(amp[:, h, :], amp[:, h, :]))
                dve.tensor_tensor(y[:, :, rows(h)], y[:, :, rows(h)], over_tiles(amp[:, h, :]),
                                  ALU.mult).then_inc(z_done, 1)

            def split_z(h):
                dve.wait_ge(gelu_done, h + 1)
                dve.tensor_copy(z_t[h][0], y[:, :, rows(h)]).then_inc(z_rounded, 1)
                dve.wait_ge(z_rounded, h + 1)
                dve.tensor_tensor(z_t[h][1], y[:, :, rows(h)], z_t[h][0].bitcast(F32), ALU.subtract) \
                    .then_inc(z_split, 1)

            sum_features(0)
            subtract_mean(0)
            sum_squares(0)
            sum_features(1)
            normalise(0)
            subtract_mean(1)
            split_z(0)
            sum_squares(1)
            normalise(1)
            split_z(1)
            for h in range(2):
                for et in range(DK):
                    n = DK * h + et
                    x = AT_TOP1 + n
                    hi, lo = (v[:, et, :] for v in h1_t[h])
                    added = sq[:, n % 2, 0, :]
                    dve.wait_ge(filled, x + 1)
                    dve.wait_ge(x_loaded[n % 2], 16 * (n // 2 + 1))
                    if n >= 2:
                        dve.wait_ge(h1_split, n - 1)
                    dve.tensor_tensor(added, banks[:, x % 4, :], x_part[:, n % 2, :], ALU.add) \
                        .then_inc(dve_read, 1)
                    dve.wait_ge(dve_read, n + 1)
                    dve.tensor_scalar(hi, added, 0.0, None, ALU.max).then_inc(h1_rounded, 1)
                    dve.wait_ge(h1_rounded, n + 1)
                    dve.scalar_tensor_tensor(lo, added, 0.0, hi.bitcast(F32), ALU.max, ALU.subtract) \
                        .then_inc(h1_split, 1)


def build(nc, t, out):
    scr = {"u": nc.dram_tensor("u_scratch", [ALL_TILES, P, B], F32, kind="Internal").ap(),
           "h": nc.dram_tensor("h_scratch", [2 * ENC_TILES, P, B], F32, kind="Internal").ap()}
    scr["o"] = nc.dram_tensor("o_scratch", [ROW_TILES, HEADS, P, NB], F32, kind="Internal").ap()
    scr["attn"] = nc.dram_tensor("attn_scratch", [ROW_TILES, 2, DK, P, NB], F32, kind="Internal").ap()
    scr["sup"] = nc.dram_tensor("sup_scratch", [ROW_TILES, 2, P, D], F32, kind="Internal").ap()
    encoders_phase(nc, t, scr)
    with nc.sbuf_tensor("strength", [P, ROW_TILES, N, N], F32) as strength:
        attention_phase(nc, t, scr, strength)
        shape = [P, N, DK, 3, EH]
        with nc.sbuf_tensor("int_hi", shape, F32R) as hi, nc.sbuf_tensor("int_lo", shape, F32R) as lo, \
                nc.sbuf_tensor("int_stage", [P, 2, KH, 2, EH], F32) as w_stage:
            output_projection_phase(nc, t, scr, (hi, lo), w_stage)
            interference_phase(nc, t, scr, strength, (hi, lo), w_stage)
    top_phase(nc, t, scr, out)


def _layouts(i):
    f = {k: np.asarray(v) for k, v in i.items()}

    def cols(*vectors):
        return np.concatenate([v.reshape(-1, P).T for v in vectors], axis=1)

    def lhs_tiles(*mats):
        m = np.concatenate(mats, axis=1)
        return m.reshape(m.shape[0] // P, P, -1, P).transpose(2, 1, 0, 3).reshape(-1, P, m.shape[0])

    def rhs(w):
        return w.T.reshape(-1, P, w.shape[0]).transpose(1, 0, 2).reshape(P, -1)

    e = "L0_rec_"
    bq_r, bk_r, bq_i, bk_i = (f[e + b].reshape(DK, P).T for b in ("bq_r", "bk_r", "bq_i", "bk_i"))
    return {
        "qkv": np.stack([rhs(f[e + w]) for w in ("Wq_r", "Wk_r", "Wq_i", "Wk_i", "Wv_r", "Wv_i")]),
        "qk_bias": np.stack([bq_r, bk_r, bq_i, bk_i], axis=1),
        "wo": np.stack([rhs(f[e + w]) for w in ("Wo_r", "Wo_i")]),
        "wo_bias": np.stack([f[e + b].reshape(DK, P).T for b in ("bo_r", "bo_i")], axis=1),
        "int_w": np.stack([f[e + w].reshape(N, 2, EH, DK, P) for w in ("int_Wr", "int_Wi")])
        .transpose(2, 1, 5, 4, 0, 3).reshape(2, N, P, -1),
        "ids": f["ids"].reshape(ROW_TILES, P, N).transpose(1, 0, 2),
        **{f"tbl_{n}": f[f"tbl_{n}"] for n in range(N)},
        "w_Mr": rhs(f[e + "meas_Mr"]),
        "w_Mi": rhs(f[e + "meas_Mi"]),
        "w_post": rhs(f[e + "post_W"]),
        "w_top1": rhs(f["W_top1"][:D].T),
        "w_top2": rhs(f["W_top2"].T),
        "w_top3": f["W_top3"].reshape(2, P).T,
        "top_cols": cols(f[e + "post_b"], f[e + "post_g"], f[e + "post_be"], f["b_top2"]),
        "v_bias": np.concatenate([f[e + "bv_r"].reshape(HEADS, HD).T, f[e + "bv_i"].reshape(HEADS, HD).T]),
        "x_t": f["r_x"].T.reshape(KT, P, B),
        "w_enc": lhs_tiles(f[e + "er_W1"].T, f[e + "ei_W1"].T, f["W_top1"][D:],
                           f[e + "er_W2"].T, f[e + "ei_W2"].T),
        "enc_bias": cols(f[e + "er_b1"], f[e + "ei_b1"], f["b_top1"], f[e + "er_b2"], f[e + "ei_b2"]),
        "ln_g": cols(f[e + "er_g1"], f[e + "ei_g1"]),
        "ln_b": cols(f[e + "er_be1"], f[e + "ei_be1"]),
    }


def kernel(**inputs):
    import concourse.bacc as bacc
    from concourse.bass_utils import run_bass_kernel_spmd

    nc = bacc.Bacc("TRN2", target_bir_lowering=False, num_devices=1)
    arrays, t = {}, {}
    for name, a in _layouts(inputs).items():
        a = np.ascontiguousarray(a)
        arrays[f"in_{name}"] = a
        t[name] = nc.dram_tensor(f"in_{name}", a.shape, mybir.dt.from_np(a.dtype),
                                 kind="ExternalInput").ap()
    out = nc.dram_tensor("out_y", (B, 1), F32, kind="ExternalOutput").ap()
    build(nc, t, out)
    r = run_bass_kernel_spmd(nc, [arrays], core_ids=[0])
    return r.results[0]["out_y"]
```

```python
from contextlib import ExitStack

import numpy as np

import concourse.bass as bass
from concourse import mybir

F32 = mybir.dt.float32
F32R = mybir.dt.float32r
I32 = mybir.dt.int32
ALU = mybir.AluOpType
ACT = mybir.ActivationFunctionType
AX = mybir.AxisListType

P = 128
B = 1024
HID = 2048
D = 512
N = 4
HEADS = 8
HD = D // HEADS
KT = HID // P
KQ = 4
PIECES = KT // KQ
HALF = 512
LN_EPS = 1e-5
ENC_TILES = HID // P
TOP_TILES = D // P
L1_TILES = 2 * ENC_TILES + TOP_TILES
ALL_TILES = L1_TILES + 2 * ENC_TILES
JOBS = 4
PARTS = ((0, 0), (0, 1), (1, 0))


def encoders_phase(nc, t, scr):
    with ExitStack() as ctx:
        def sb(name, shape, dt=F32):
            return ctx.enter_context(nc.sbuf_tensor(name, shape, dt))

        def sem(name):
            return ctx.enter_context(nc.semaphore(name))

        PLACES = 4

        mov = [sb("mov_hi", [P, KT, B], F32R), sb("mov_lo", [P, KT, B], F32R)]
        w_stage = sb("w_stage", [P, PIECES, KQ * P])
        w = [sb("w_hi", [P, PIECES, KQ * P], F32R), sb("w_lo", [P, PIECES, KQ * P], F32R)]
        out_sb = sb("out_sb", [P, 2, B])
        load_sb = sb("load_sb", [P, PLACES, B])
        gelu_sb = load_sb[:, 2:4, :]
        shift = sb("shift", [P, B])
        dev = sb("dev", [P, B])
        dev_sum = sb("dev_sum", [P, B])
        dev_sq = sb("dev_sq", [P, B])
        mean_bc = sb("mean_bc", [P, B])
        rstd_bc = sb("rstd_bc", [P, B])
        bias = sb("bias_cols", [P, ALL_TILES])
        ln_g = sb("ln_g", [P, 2 * ENC_TILES])
        ln_b = sb("ln_b", [P, 2 * ENC_TILES])
        averager = sb("averager", [P, P])
        eps = sb("eps", [P, 1])
        zeros = sb("zeros", [P, KQ * P])
        ps = ctx.enter_context(nc.psum_tensor("ps", [P, 2, B], F32))
        ps_mean = ctx.enter_context(nc.psum_tensor("ps_mean", [P, B], F32))
        ps_var = ctx.enter_context(nc.psum_tensor("ps_var", [P, B], F32))

        consts_loaded = sem("consts_loaded")
        consts_set = sem("consts_set")
        w_loaded = [sem(f"w_loaded{q}") for q in range(PIECES)]
        w_rounded = sem("w_rounded")
        w_split = sem("w_split")
        piece_used = sem("piece_used")
        loaded = [sem(f"loaded{j}") for j in range(PLACES)]
        load_used = [sem(f"load_used{j}") for j in range(PLACES)]
        hi_filled = sem("hi_filled")
        tile_out = sem("tile_out")
        stored = [sem(f"stored{j}") for j in range(2)]
        centred = sem("centred")
        squared = sem("squared")
        tile_summed = sem("tile_summed")
        ln_step = sem("ln_step")
        part_means = sem("part_means")
        mean_done = sem("mean_done")
        part_vars = sem("part_vars")
        var_done = sem("var_done")
        std_done = sem("std_done")
        z_centred = sem("z_centred")
        z_done = sem("z_done")
        gelu_stored = [sem(f"gelu_stored{j}") for j in range(2)]

        block = ctx.enter_context(nc.Block())

        NORM_BASE = tuple(KT // PLACES * (enc + 1) + KT // 2 * enc for enc in range(2))

        def filled_before(f, k):
            return KT // PLACES * f + (KT // 2 * f if k % PLACES < 2 else 0) + k // PLACES

        EARLY = KT - KQ

        ER1, EI1, TOP, ER2, EI2, END = 0, 8, 16, 18, 26, 34
        NORM_PAIRS = (EI1 + 1, ER2 + 1)
        NORM_LEN = KT // JOBS

        @block.sync
        def _(sp):
            def piece(tile, q, first=False):
                if not first:
                    sp.wait_ge(w_split, PIECES * (tile - 1) + q + 1)
                sp.dma_start(w_stage[:, q, :], t["w_enc"][tile, :, q * KQ * P:(q + 1) * KQ * P]) \
                    .then_inc(w_loaded[q], 16)

            def weights(tile):
                for q in range(PIECES):
                    piece(tile, q)

            def load(source, j, before):
                if not (isinstance(before, int) and before == 0):
                    sp.wait_ge(load_used[j], before)
                sp.dma_start(load_sb[:, j, :], source).then_inc(loaded[j], 16)

            def fill(f, pair):
                if f:
                    weights(2 * pair)
                    for j in range(2):
                        sp.wait_ge(gelu_stored[j], 16 * (KT // 2) * f)
                for k in range(KT):
                    if f == 0 and k % KQ == 0:
                        piece(0, k // KQ, first=True)
                    source = t["x_t"][k] if f == 0 else scr["h"][KT * (f - 1) + k]
                    load(source, k % PLACES, filled_before(f, k))
                weights(2 * pair + 1)

            def norm(enc, start):
                for j in range(2):
                    sp.wait_ge(stored[j], 16 * (ENC_TILES // 2) * (enc + 1))
                with sp.Fori(start, start + NORM_LEN) as i:
                    weights(2 * i)
                    weights(2 * i + 1)
                    for c in range(JOBS):
                        load(scr["u"][ENC_TILES * enc + JOBS * (i - start) + c], c % 2,
                             NORM_BASE[enc] + JOBS // 2 * (i - start) + c // 2)

            def plain(start, end):
                with sp.Fori(start, end) as i:
                    weights(2 * i)
                    weights(2 * i + 1)

            fill(0, ER1)
            sp.dma_start(bias[:], t["enc_bias"]).then_inc(consts_loaded, 16)
            sp.dma_start(ln_g[:], t["ln_g"]).then_inc(consts_loaded, 16)
            sp.dma_start(ln_b[:], t["ln_b"]).then_inc(consts_loaded, 16)
            plain(ER1 + 1, NORM_PAIRS[0])
            norm(0, NORM_PAIRS[0])
            plain(NORM_PAIRS[0] + NORM_LEN, ER2)
            fill(1, ER2)
            norm(1, NORM_PAIRS[1])
            plain(NORM_PAIRS[1] + NORM_LEN, EI2)
            fill(2, EI2)
            plain(EI2 + 1, END)

        @block.gpsimd
        def _(pool):
            pool.memset(averager[:], 1.0 / P).then_inc(consts_set, 1)
            pool.memset(eps[:], LN_EPS).then_inc(consts_set, 1)
            pool.memset(zeros[:], 0.0).then_inc(consts_set, 1)
            pool.wait_ge(consts_set, 3)

            def split(tile, first=False):
                for q in range(PIECES):
                    pool.wait_ge(w_loaded[q], 16 * (tile + 1))
                    if not first:
                        pool.wait_ge(piece_used, PIECES * (tile - 1) + q + 1)
                    pool.tensor_tensor(w[0][:, q, :], w_stage[:, q, :], zeros[:], ALU.add) \
                        .then_inc(w_rounded, 1)
                    pool.wait_ge(w_rounded, PIECES * tile + q + 1)
                    pool.tensor_tensor(w[1][:, q, :], w_stage[:, q, :], w[0][:, q, :].bitcast(F32),
                                       ALU.subtract).then_inc(w_split, 1)

            split(0, first=True)
            with pool.Fori(1, ALL_TILES) as tile:
                split(tile)

        @block.tensor
        def _(pe):
            def tile_products(j, tile, fill=None):
                if not (isinstance(tile, int) and tile < 2):
                    pe.wait_ge(tile_out, tile - 1)
                for q in range(PIECES):
                    pe.wait_ge(w_split, PIECES * tile + q + 1)
                    for kk in range(KQ):
                        k = KQ * q + kk
                        if fill is not None:
                            pe.wait_ge(load_used[k % PLACES], filled_before(fill, k) + 1)
                        for wp, mp in PARTS:
                            for half in range(2):
                                last = pe.matmul(ps[:, j, half * HALF:(half + 1) * HALF],
                                                 w[wp][:, q, kk * P:(kk + 1) * P],
                                                 mov[mp][:, k, half * HALF:(half + 1) * HALF],
                                                 start=(k == 0 and (wp, mp) == PARTS[0]),
                                                 stop=(k == KT - 1 and (wp, mp) == PARTS[-1]))
                    last.then_inc(piece_used, 1)

            def pairs(start, end):
                with pe.Fori(start, end) as i:
                    for j in range(2):
                        tile_products(j, 2 * i + j)

            def average(enc, out, source, ready, done):
                pe.wait_ge(ready, enc + 1)
                for half in range(2):
                    cols = slice(half * HALF, (half + 1) * HALF)
                    last = pe.matmul(out[:, cols], averager[:], source[:, cols], start=True, stop=True)
                last.then_inc(done, 1)

            def pair_and_statistics(enc, pair):
                tile_products(0, 2 * pair)
                average(enc, ps_mean, mean_bc, part_means, mean_done)
                tile_products(1, 2 * pair + 1)
                average(enc, ps_var, rstd_bc, part_vars, var_done)

            def pair_filling(fill, pair):
                for j in range(2):
                    tile_products(j, 2 * pair + j, fill if j == 0 else None)

            pe.wait_ge(consts_set, 3)
            pair_filling(0, ER1)
            pairs(ER1 + 1, EI1)
            pair_and_statistics(0, EI1)
            pairs(EI1 + 1, TOP)
            pair_and_statistics(1, TOP)
            pairs(TOP + 1, ER2)
            pair_filling(1, ER2)
            pairs(ER2 + 1, EI2)
            pair_filling(2, EI2)
            pairs(EI2 + 1, END)

        @block.scalar
        def _(act):
            def out(j, tile, pair, first=False, summed=True):
                act.wait_ge(piece_used, PIECES * (tile + 1))
                if not first:
                    act.wait_ge(stored[j], 16 * pair)
                    if summed:
                        act.wait_ge(tile_summed, tile - 1)
                act.activation(out_sb[:, j, :], ps[:, j, :], ACT.Identity,
                               bias=bias[:, bass.ds(tile, 1)]).then_inc(tile_out, 1)
                act.wait_ge(tile_out, tile + 1)
                act.dma_start(scr["u"][tile], out_sb[:, j, :]).then_inc(stored[j], 16)

            def gelu(enc, job, number, half_number, half_job, first=False):
                j = number % 2
                act.wait_ge(z_done, KT * enc + job + 1)
                if not first:
                    act.wait_ge(gelu_stored[j], 16 * (KT // 2 * enc + half_job))
                act.activation(gelu_sb[:, j, :], load_sb[:, j, :], ACT.Gelu,
                               scale=ln_g[:, bass.ds(KT * enc + job, 1)],
                               bias=ln_b[:, bass.ds(KT * enc + job, 1)]).then_inc(load_used[j], 1)
                act.wait_ge(load_used[j], half_number + 1)
                act.dma_start(scr["h"][KT * enc + job], gelu_sb[:, j, :]).then_inc(gelu_stored[j], 16)

            def pairs(start, end, summed=False):
                with act.Fori(start, end) as i:
                    for j in range(2):
                        out(j, 2 * i + j, i, summed=summed)

            def pair_with_jobs(enc, i, start, first=False, summed=False):
                for j in range(2):
                    out(j, 2 * i + j, i, summed=summed)
                    for c in range(j * JOBS // 2, (j + 1) * JOBS // 2):
                        gelu(enc, JOBS * (i - start) + c, c,
                             NORM_BASE[enc] + JOBS // 2 * (i - start) + c // 2,
                             JOBS // 2 * (i - start) + c // 2, first=first and c < 2)

            def fill(f, pair, ks):
                for k in ks:
                    act.wait_ge(loaded[k % PLACES], 16 * (filled_before(f, k) + 1))
                    if f > 0:
                        act.wait_ge(piece_used, PIECES * (2 * pair - 1) + k // KQ + 1)
                    act.activation(mov[0][:, k, :], load_sb[:, k % PLACES, :], ACT.Copy) \
                        .then_inc(hi_filled, 1)

            def refill(f, pair):
                out(0, 2 * pair - 2, pair - 1, summed=False)
                fill(f, pair, range(EARLY))
                out(1, 2 * pair - 1, pair - 1, summed=False)
                fill(f, pair, range(EARLY, KT))
                for j in range(2):
                    out(j, 2 * pair + j, pair, summed=False)

            def std(enc):
                act.wait_ge(var_done, enc + 1)
                act.activation(rstd_bc[:], ps_var[:], ACT.Sqrt, scale=1.0 / ENC_TILES,
                               bias=eps[:]).then_inc(std_done, 1)

            fill(0, ER1, range(KT))
            act.wait_ge(consts_loaded, 48)
            act.wait_ge(consts_set, 3)
            for j in range(2):
                out(j, j, 0, first=True, summed=False)
            pairs(ER1 + 1, EI1, summed=True)
            for j in range(2):
                out(j, 2 * EI1 + j, EI1)
            std(0)
            pair_with_jobs(0, NORM_PAIRS[0], NORM_PAIRS[0], first=True, summed=True)
            with act.Fori(NORM_PAIRS[0] + 1, NORM_PAIRS[0] + NORM_LEN) as i:
                pair_with_jobs(0, i, NORM_PAIRS[0], summed=True)
            pairs(NORM_PAIRS[0] + NORM_LEN, TOP, summed=True)
            for j in range(2):
                out(j, 2 * TOP + j, TOP)
            std(1)
            refill(1, ER2)
            with act.Fori(NORM_PAIRS[1], NORM_PAIRS[1] + NORM_LEN) as i:
                pair_with_jobs(1, i, NORM_PAIRS[1])
            pairs(NORM_PAIRS[1] + NORM_LEN, EI2 - 1)
            refill(2, EI2)
            pairs(EI2 + 1, END)
            for j in range(2):
                act.wait_ge(stored[j], 16 * (ALL_TILES // 2))
                act.wait_ge(gelu_stored[j], 16 * KT)

        @block.vector
        def _(dve):
            def fill(f):
                for k in range(KT):
                    dve.wait_ge(hi_filled, KT * f + k + 1)
                    dve.tensor_tensor(mov[1][:, k, :], load_sb[:, k % PLACES, :],
                                      mov[0][:, k, :].bitcast(F32), ALU.subtract) \
                        .then_inc(load_used[k % PLACES], 1)

            def first_sum(tile, j):
                dve.wait_ge(tile_out, tile + 1)
                dve.tensor_copy(shift[:], out_sb[:, j, :]).then_inc(centred, 1)
                dve.memset(dev_sum[:], 0.0).then_inc(squared, 1)
                dve.memset(dev_sq[:], 0.0).then_inc(tile_summed, 1)

            def add_sum(tile, j):
                dve.wait_ge(tile_out, tile + 1)
                dve.wait_ge(tile_summed, tile)
                dve.tensor_tensor(dev[:], out_sb[:, j, :], shift[:], ALU.subtract).then_inc(centred, 1)
                dve.wait_ge(centred, tile + 1)
                dve.tensor_tensor(dev_sum[:], dev_sum[:], dev[:], ALU.add)
                dve.tensor_tensor(dev[:], dev[:], dev[:], ALU.mult).then_inc(squared, 1)
                dve.wait_ge(squared, tile + 1)
                dve.tensor_tensor(dev_sq[:], dev_sq[:], dev[:], ALU.add).then_inc(tile_summed, 1)

            def pairs(start, end):
                with dve.Fori(start, end) as i:
                    for j in range(2):
                        add_sum(2 * i + j, j)

            steps = [0]

            def step(instruction):
                steps[0] += 1
                instruction.then_inc(ln_step, 1)
                dve.wait_ge(ln_step, steps[0])

            def parts(enc):
                dve.wait_ge(tile_summed, ENC_TILES * (enc + 1))
                step(dve.tensor_scalar(rstd_bc[:], dev_sum[:], 1.0 / ENC_TILES, None, ALU.mult))
                dve.tensor_tensor(mean_bc[:], rstd_bc[:], shift[:], ALU.add).then_inc(part_means, 1)
                step(dve.tensor_tensor(rstd_bc[:], rstd_bc[:], dev_sum[:], ALU.mult))
                step(dve.tensor_tensor(rstd_bc[:], dev_sq[:], rstd_bc[:], ALU.subtract))

            def combine(enc):
                dve.wait_ge(mean_done, enc + 1)
                step(dve.tensor_tensor(dev[:], mean_bc[:], ps_mean[:], ALU.subtract))
                step(dve.tensor_tensor(dev[:], dev[:], dev[:], ALU.mult))
                dve.tensor_copy(mean_bc[:], ps_mean[:])
                dve.scalar_tensor_tensor(rstd_bc[:], dev[:], float(ENC_TILES), rstd_bc[:],
                                         ALU.mult, ALU.add).then_inc(part_vars, 1)

            def rstd(enc):
                dve.wait_ge(std_done, enc + 1)
                step(dve.reciprocal(rstd_bc[:], rstd_bc[:]))

            def normalise(enc, job, number, half_number):
                j = number % 2
                dve.wait_ge(loaded[j], 16 * (half_number + 1))
                dve.tensor_tensor(load_sb[:, j, :], load_sb[:, j, :], mean_bc[:], ALU.subtract) \
                    .then_inc(z_centred, 1)
                dve.wait_ge(z_centred, KT * enc + job + 1)
                dve.tensor_tensor(load_sb[:, j, :], load_sb[:, j, :], rstd_bc[:], ALU.mult) \
                    .then_inc(z_done, 1)

            def jobs(enc, i, start, js, sums):
                for j in js:
                    if sums:
                        add_sum(2 * i + j, j)
                    for c in range(j * JOBS // 2, (j + 1) * JOBS // 2):
                        normalise(enc, JOBS * (i - start) + c, c,
                                  NORM_BASE[enc] + JOBS // 2 * (i - start) + c // 2)

            fill(0)
            first_sum(0, 0)
            add_sum(1, 1)
            pairs(ER1 + 1, EI1)
            parts(0)
            combine(0)
            first_sum(2 * EI1, 0)
            add_sum(2 * EI1 + 1, 1)
            rstd(0)
            with dve.Fori(NORM_PAIRS[0], NORM_PAIRS[0] + NORM_LEN) as i:
                jobs(0, i, NORM_PAIRS[0], (0, 1), True)
            pairs(NORM_PAIRS[0] + NORM_LEN, TOP)
            parts(1)
            combine(1)
            rstd(1)
            fill(1)
            with dve.Fori(NORM_PAIRS[1], NORM_PAIRS[1] + NORM_LEN) as i:
                jobs(1, i, NORM_PAIRS[1], (0, 1), False)
            fill(2)


GROUPS = 4
GR = P // GROUPS
NB = N * P
ROW_TILES = B // P
SCALE = float(HD) ** -0.5
MAG_EPS = 1e-8
DK = D // P


def attention_phase(nc, t, scr, strength):
    with ExitStack() as ctx:
        def sb(name, shape, dt=F32):
            return ctx.enter_context(nc.sbuf_tensor(name, shape, dt))

        def sem(name):
            return ctx.enter_context(nc.semaphore(name))

        wts = [sb("qkv_hi", [P, 6, DK, D], F32R), sb("qkv_lo", [P, 6, DK, D], F32R)]
        s_stage = [sb(f"s{c}_stage", [P, DK, N, P]) for c in "ri"]
        s = [[sb(f"s{c}_{part}", [P, DK, GROUPS, P], F32R) for part in ("hi", "lo")] for c in "ri"]
        q_cat = sb("q_cat", [P, 2, 2, GROUPS, P])
        k_both = sb("k_both", [P, 2, 2, 2, GROUPS, P])
        v_sb = sb("v_sb", [P, GROUPS, HEADS, 2, HD])
        masked = sb("masked", [P, GROUPS, 2 * N, GR])
        scores = sb("scores", [P, HEADS, GROUPS, 2, N])
        mag = sb("mag", [P, HEADS * GROUPS, N])
        top = sb("top", [P, HEADS * GROUPS])
        total = sb("total", [P, HEADS * GROUPS])
        spread = sb("spread", [P, 2, GROUPS, N, GR])
        spread_t = sb("spread_t", [P, 2, GROUPS, P])
        o_sb = sb("o_sb", [P, 2, N, P])
        same_row = sb("same_row", [P, GR])
        ident = sb("ident", [P, P])
        qk_bias = sb("qk_bias", [P, 5, DK])
        v_bias = sb("v_bias", [P, HEADS])
        mag_eps = sb("mag_eps", [P, 1])
        ids = sb("ids", [P, ROW_TILES, N], I32)
        banks = ctx.enter_context(nc.psum_tensor("banks", [P, 4, HALF], F32))
        ps_x = ctx.enter_context(nc.psum_tensor("ps_x", [P, 4, HALF], F32))
        ps_scores = ps_x[:, 0:2, :]
        ps_pt = [ps_x[:, 2, :], ps_x[:, 0, :]]
        ps_o = [ps_x[:, 3, :], ps_x[:, 1, :]]

        consts_loaded = sem("a_consts_loaded")
        consts_set = sem("a_consts_set")
        bias_negated = sem("bias_negated")
        gathered = sem("gathered")
        mat_loaded = [sem(f"mat_loaded{j}") for j in range(4)]
        mat_rounded = sem("mat_rounded")
        mat_split = sem("mat_split")
        s_loaded = [sem(f"s_{c}_loaded") for c in "ri"]
        s_rounded = sem("s_rounded")
        s_split = sem("s_split")
        bank_full = sem("bank_full")
        bank_read = sem("bank_read")
        scores_done = sem("scores_done")
        scores_masked = sem("scores_masked")
        scores_kept = sem("scores_kept")
        soft = sem("soft")
        mag2_done = sem("mag2_done")
        mag_done = sem("mag_done")
        mag_less = sem("mag_less")
        exp_done = sem("exp_done")
        weights_done = sem("weights_done")
        spread_done = sem("spread_done")
        turned = sem("turned")
        turned_out = sem("turned_out")
        o_done = sem("o_done")
        o_out = sem("o_out")
        o_stored = [sem(f"o_stored{j}") for j in range(2)]

        block = ctx.enter_context(nc.Block())

        BANKS = 4
        QK_PLACES = 2 * 2
        FILLS = 4 * DK + 2 * GROUPS
        mat_hi, mat_lo = ([x[:, m, :, :].rearrange("p k e -> p (k e)") for m in range(6)] for x in wts)
        mat_stage = [x.rearrange(pattern)[:, j * DK * D:(j + 1) * DK * D] for x, pattern in
                     ((k_both[:], "p e a k g x -> p (e a k g x)"), (v_sb[:], "p g h c d -> p (g h c d)"))
                     for j in range(2)]
        mat_stage += mat_stage[2:]
        s_src = [scr["u"][L1_TILES + ENC_TILES * c:L1_TILES + ENC_TILES * (c + 1)]
                 .rearrange("(n k) p (t b) -> t p k n b", k=DK, b=P) for c in range(2)]

        @block.sync
        def _(sp):
            sp.dma_start(qk_bias[:, 0:4, :], t["qk_bias"]).then_inc(consts_loaded, 16)
            sp.dma_start(v_bias[:], t["v_bias"]).then_inc(consts_loaded, 16)
            sp.dma_start(ids[:], t["ids"]).then_inc(consts_loaded, 16)

            def load_s(tile, c):
                for k in range(DK):
                    sp.dma_start(s_stage[c][:, k, :, :], s_src[c][tile, :, k, :, :]) \
                        .then_inc(s_loaded[c], 16)

            for j in range(2):
                sp.sem_inc(o_stored[j], 16)
            for m in range(6):
                if m == 0:
                    load_s(0, 0)
                if m == 2:
                    load_s(0, 1)
                if m >= 4:
                    sp.wait_ge(mat_split, m - 1)
                sp.dma_start(mat_stage[m], t["qkv"][m]).then_inc(mat_loaded[m % 4], 16)

            def store_o(tile):
                for h in range(HEADS):
                    sp.wait_ge(o_out, 2 + HEADS * tile + h + 1)
                    sp.dma_start(scr["o"][tile, h], o_sb[:, h % 2, :, :].rearrange("p n b -> p (n b)")) \
                        .then_inc(o_stored[h % 2], 16)

            with sp.Fori(0, ROW_TILES - 1) as tile:
                for c in range(2):
                    sp.wait_ge(s_split, 2 * tile + c + 1)
                    load_s(tile + 1, c)
                store_o(tile)
            store_o(ROW_TILES - 1)
            for j in range(2):
                sp.wait_ge(o_stored[j], 16 * (HEADS // 2 * ROW_TILES + 1))

        @block.gpsimd
        def _(pool):
            pool.memset(mag_eps[:], MAG_EPS).then_inc(consts_set, 1)
            pool.memset(ident[:], 0.0).then_inc(consts_set, 1)
            pool.memset(same_row[:], 0.0).then_inc(consts_set, 1)
            pool.wait_ge(consts_set, 3)
            pool.affine_select(out=ident[:], in_=ident[:], compare_op=ALU.not_equal, fill=1.0,
                               base=0, pattern=[[-1, P]], channel_multiplier=1).then_inc(consts_set, 1)
            for n in range(N):
                pool.wait_ge(consts_set, 4 + n)
                pool.affine_select(out=same_row[:], in_=same_row[:], compare_op=ALU.not_equal,
                                   fill=1.0, base=-GR * n, pattern=[[-1, GR]],
                                   channel_multiplier=1).then_inc(consts_set, 1)
            pool.wait_ge(consts_loaded, 48)
            for tile in range(ROW_TILES):
                for n in range(N):
                    pool.indirect_dma_start(
                        out=strength[:, tile, n, :], out_offset=None, in_=t[f"tbl_{n}"],
                        in_offset=bass.IndirectOffsetOnAxis(ap=ids[:, tile, n:n + 1], axis=0)) \
                        .then_inc(gathered, 16)
            pool.wait_ge(gathered, 16 * N * ROW_TILES)

        CONSTS = 4 + N

        @block.tensor
        def _(pe):
            def fill_bank(tile, x, products):
                pe.wait_ge(bank_read, FILLS * tile + x + 1)
                for n, (lhs, rhs) in enumerate(products):
                    last = pe.matmul(banks[:, x % BANKS, :], lhs, rhs, start=n == 0,
                                     stop=n == len(products) - 1)
                last.then_inc(bank_full, 1)

            def project(tile, et, m):
                c = m // 2
                fill_bank(tile, 4 * et + m,
                          [(wts[wp][:, m, k, et * P:(et + 1) * P], s[c][sp_][:, k, :, :])
                           for k in range(DK) for wp, sp_ in PARTS])

            def values(tile, c, g):
                fill_bank(tile, 4 * DK + GROUPS * c + g,
                          [(s[c][sp_][:, k, g, :], wts[wp][:, 4 + c, k, :])
                           for k in range(DK) for wp, sp_ in PARTS])

            def score(tile, h):
                et, a = h // 2, h % 2
                pe.wait_ge(bank_read, BANKS + FILLS * tile + 4 * (et + 1))
                pe.wait_ge(scores_masked, HEADS * tile + h + 1)
                if h == 0:
                    pe.wait_ge(turned_out, 2 + HEADS * tile)
                    pe.wait_ge(o_out, 2 + HEADS * tile)
                for g in range(GROUPS):
                    last = pe.matmul(ps_scores[:, g // 2, (g % 2) * 2 * P:(g % 2 + 1) * 2 * P],
                                     q_cat[:, et % 2, a, g, :], k_both[:, et % 2, a, :, g, :],
                                     start=True, stop=True)
                last.then_inc(scores_done, 1)

            def turn(tile, h):
                pe.wait_ge(spread_done, HEADS * tile + h + 1)
                pe.wait_ge(turned_out, HEADS * tile + h + 1)
                for g in range(GROUPS):
                    last = pe.transpose(ps_pt[h % 2][:, g * P:(g + 1) * P],
                                        spread[:, h % 2, g, :, :].rearrange("p m b -> p (m b)"),
                                        ident[:])
                last.then_inc(turned, 1)

            def weigh(tile, h):
                if h == 0:
                    pe.wait_ge(bank_read, BANKS + FILLS * (tile + 1))
                pe.wait_ge(turned_out, 2 + HEADS * tile + h + 1)
                pe.wait_ge(o_out, HEADS * tile + h + 1)
                for g in range(GROUPS):
                    last = pe.matmul(ps_o[h % 2][:, g * P:(g + 1) * P],
                                     v_sb[:, g, h, :, :].rearrange("p c d -> p (c d)"),
                                     spread_t[:, h % 2, g, :], start=True, stop=True)
                last.then_inc(o_done, 1)

            pe.sem_inc(scores_done, QK_PLACES)
            pe.sem_inc(bank_full, FILLS)
            pe.sem_inc(turned, 2)
            pe.wait_ge(consts_set, CONSTS)
            with pe.Fori(0, ROW_TILES) as tile:
                for et in range(DK):
                    for m in range(4):
                        if et == 0 and m % 2 == 0:
                            pe.wait_ge(s_split, 2 * tile + m // 2 + 1)
                        if et == 0:
                            pe.wait_ge(mat_split, m + 1)
                        project(tile, et, m)
                        if et and m % 2:
                            score(tile, 2 * (et - 1) + m // 2)
                pe.wait_ge(mat_split, 6)
                for c in range(2):
                    for g in range(GROUPS):
                        values(tile, c, g)
                        if c == 0 and g < 2:
                            score(tile, 2 * (DK - 1) + g)
                turn(tile, 0)
                for h in range(HEADS):
                    if h + 1 < HEADS:
                        turn(tile, h + 1)
                    weigh(tile, h)

        @block.scalar
        def _(act):
            act.sem_inc(bank_read, BANKS)
            act.sem_inc(turned_out, 2)
            act.sem_inc(o_out, 2)
            act.wait_ge(consts_loaded, 48)
            act.mul(qk_bias[:, 4, :], qk_bias[:, 3, :], -1.0).then_inc(bias_negated, 1)
            act.wait_ge(bias_negated, 1)
            act.wait_ge(consts_set, CONSTS)
            for m in range(6):
                act.wait_ge(mat_loaded[m % 4], 16 * (m // 4 + 1))
                act.activation(mat_hi[m], mat_stage[m], ACT.Copy).then_inc(mat_rounded, 1)

            def read_qk(tile, et, m):
                act.wait_ge(bank_full, FILLS * (tile + 1) + 4 * et + m + 1)
                if m == 0:
                    act.wait_ge(scores_done, HEADS * tile + 2 * et + 2)
                imag, par = m // 2, et % 2
                here = slice(imag * HD, (imag + 1) * HD)
                there = slice((1 - imag) * HD, (2 - imag) * HD)
                for a in range(2):
                    src = slice(a * HD, (a + 1) * HD)

                    def put(dst, scale, col):
                        return act.activation(dst.rearrange("p g x -> p (g x)"),
                                              banks[src, (4 * et + m) % BANKS, :], ACT.Identity,
                                              scale=scale, bias=qk_bias[src, col, et:et + 1])
                    if m % 2 == 0:
                        last = put(q_cat[here, par, a, :, :], 1.0, m)
                    else:
                        put(k_both[here, par, a, 0, :, :], 1.0, m)
                        last = put(k_both[there, par, a, 1, :, :], -1.0 if imag else 1.0,
                                   4 if imag else m)
                last.then_inc(bank_read, 1)

            def read_v(tile, c, g):
                x = 4 * DK + GROUPS * c + g
                act.wait_ge(bank_full, FILLS * (tile + 1) + x + 1)
                act.activation(v_sb[:, g, :, c, :],
                               banks[:, x % BANKS, :].rearrange("p (h d) -> p h d", d=HD), ACT.Copy) \
                    .then_inc(bank_read, 1)

            def read_turned(tile, h):
                act.wait_ge(turned, 2 + HEADS * tile + h + 1)
                act.activation(spread_t[:, h % 2, :, :].rearrange("p g q -> p (g q)"), ps_pt[h % 2],
                               ACT.Copy).then_inc(turned_out, 1)

            def read_o(tile, h):
                act.wait_ge(o_done, HEADS * tile + h + 1)
                act.wait_ge(o_stored[h % 2], 16 * (HEADS // 2 * tile + h // 2 + 1))
                act.activation(o_sb[:, h % 2, :, :].rearrange("p n (g b) -> p g n b", b=GR),
                               ps_o[h % 2].rearrange("p (g n b) -> p g n b", n=N, b=GR), ACT.Identity,
                               bias=v_bias[:, h:h + 1]).then_inc(o_out, 1)

            with act.Fori(0, ROW_TILES) as tile:
                for et in range(DK):
                    for m in range(4):
                        read_qk(tile, et, m)
                for g in range(GROUPS):
                    read_v(tile, 0, g)
                act.wait_ge(mag2_done, tile + 1)
                act.activation(mag[:], mag[:], ACT.Sqrt, bias=mag_eps[:]).then_inc(mag_done, 1)
                read_v(tile, 1, 0)
                act.wait_ge(mag_less, tile + 1)
                act.activation(mag[:], mag[:], ACT.Exp, scale=SCALE).then_inc(exp_done, 1)
                for g in range(1, GROUPS):
                    read_v(tile, 1, g)
                read_turned(tile, 0)
                for h in range(HEADS):
                    if h + 1 < HEADS:
                        read_turned(tile, h + 1)
                    read_o(tile, h)

        @block.vector
        def _(dve):
            dve.sem_inc(scores_masked, 1)
            dve.wait_ge(consts_set, CONSTS)

            def low_mat(m):
                dve.wait_ge(mat_rounded, m + 1)
                dve.tensor_tensor(mat_lo[m], mat_stage[m], mat_hi[m].bitcast(F32),
                                  ALU.subtract).then_inc(mat_split, 1)

            def split_s(tile, c):
                dve.wait_ge(s_loaded[c], 16 * DK * (tile + 1))
                dve.wait_ge(bank_full, FILLS * tile + 4 * DK + GROUPS * (c + 1))
                for k in range(DK):
                    stage_k = s_stage[c][:, k, :, :].rearrange("p n (g b) -> p g n b", b=GR)
                    hi_k = s[c][0][:, k, :, :].rearrange("p g (n b) -> p g n b", b=GR)
                    dve.tensor_copy(hi_k, stage_k).then_inc(s_rounded, 1)
                for k in range(DK):
                    stage_k = s_stage[c][:, k, :, :].rearrange("p n (g b) -> p g n b", b=GR)
                    hi_k = s[c][0][:, k, :, :].rearrange("p g (n b) -> p g n b", b=GR)
                    lo_k = s[c][1][:, k, :, :].rearrange("p g (n b) -> p g n b", b=GR)
                    dve.wait_ge(s_rounded, DK * (2 * tile + c) + k + 1)
                    last = dve.tensor_tensor(lo_k, stage_k, hi_k.bitcast(F32), ALU.subtract)
                last.then_inc(s_split, 1)

            def keep_own_row(tile, h):
                dve.wait_ge(scores_done, QK_PLACES + HEADS * tile + h + 1)
                if h > 0:
                    dve.wait_ge(scores_kept, HEADS * tile + h)
                dve.tensor_tensor(masked[:].rearrange("p g m b -> p (g m) b"),
                                  ps_scores.rearrange("p k (x b) -> p (k x) b", b=GR),
                                  same_row[:].unsqueeze(1).broadcast_to([P, GROUPS * 2 * N, GR]),
                                  ALU.mult).then_inc(scores_masked, 1)
                dve.wait_ge(scores_masked, 1 + HEADS * tile + h + 1)
                dve.tensor_reduce(scores[:, h, :, :, :].rearrange("p g c m -> p (g c m)"),
                                  masked[:].rearrange("p g m b -> p (g m) b"), AX.X, ALU.add) \
                    .then_inc(scores_kept, 1)

            HG = HEADS * GROUPS
            SOFT_STEPS = 4

            def softmax(tile):
                def step(n, instruction):
                    instruction.then_inc(soft, 1)
                    dve.wait_ge(soft, SOFT_STEPS * tile + n)

                sc = scores[:].rearrange("p h g c m -> p (h g) c m")
                dve.wait_ge(scores_kept, HEADS * (tile + 1))
                step(1, dve.tensor_tensor(scores[:], scores[:], scores[:], ALU.mult))
                dve.tensor_tensor(mag[:], sc[:, :, 0, :], sc[:, :, 1, :], ALU.add).then_inc(mag2_done, 1)
                dve.wait_ge(mag_done, tile + 1)
                step(2, dve.tensor_reduce(top[:], mag[:], AX.X, ALU.max))
                dve.tensor_tensor(mag[:], mag[:], top[:].unsqueeze(2).broadcast_to([P, HG, N]),
                                  ALU.subtract).then_inc(mag_less, 1)
                dve.wait_ge(exp_done, tile + 1)
                step(3, dve.tensor_reduce(total[:], mag[:], AX.X, ALU.add))
                step(4, dve.reciprocal(total[:], total[:]))
                dve.tensor_tensor(mag[:], mag[:], total[:].unsqueeze(2).broadcast_to([P, HG, N]),
                                  ALU.mult).then_inc(weights_done, 1)

            def spread_weights(tile, h):
                if h == 0:
                    dve.wait_ge(weights_done, tile + 1)
                dve.wait_ge(turned, HEADS * tile + h + 1)
                dve.tensor_tensor(
                    spread[:, h % 2, :, :, :].rearrange("p g m b -> p (g m) b"),
                    mag[:, h * GROUPS:(h + 1) * GROUPS, :].rearrange("p g m -> p (g m)")
                    .unsqueeze(2).broadcast_to([P, GROUPS * N, GR]),
                    same_row[:].unsqueeze(1).broadcast_to([P, GROUPS * N, GR]),
                    ALU.mult).then_inc(spread_done, 1)

            def attend(tile):
                for h in range(HEADS):
                    keep_own_row(tile, h)
                softmax(tile)
                for h in range(HEADS):
                    spread_weights(tile, h)

            split_s(0, 0)
            for m in range(2):
                low_mat(m)
            split_s(0, 1)
            for m in range(2, 6):
                low_mat(m)
            with dve.Fori(0, ROW_TILES - 1) as tile:
                attend(tile)
                for c in range(2):
                    split_s(tile + 1, c)
            attend(ROW_TILES - 1)



EH = D // 2
KH = DK // 2


class InterferenceWeights:

    def __init__(self, ctx, nc):
        self.parts = [ctx.enter_context(nc.sbuf_tensor(f"int_{part}", [P, N, DK, 3, EH], F32R))
                      for part in ("hi", "lo")]
        self.stage = ctx.enter_context(nc.sbuf_tensor("int_stage", [P, 2, KH, 2, EH], F32))
        self.matrix_stage = self.stage[:].rearrange("p j k m e -> p (j k m e)")
        self.rounded = ctx.enter_context(nc.semaphore("int_rounded"))
        self.loaded = [[ctx.enter_context(nc.semaphore(f"int_loaded{half}{kh}")) for kh in range(2)]
                       for half in range(2)]
        self.split = [ctx.enter_context(nc.semaphore(f"int_split{kh}")) for kh in range(2)]

    def load(self, eng, source, half, n, kh):
        if half or n:
            eng.wait_ge(self.split[kh], N * half + n)
        eng.dma_start(self.stage[:, kh, :, :, :].rearrange("p k m e -> p (k m e)"),
                      source[half, n, :, kh * KH * D:(kh + 1) * KH * D]).then_inc(self.loaded[half][kh], 16)

    def round(self, act, half, n):
        for kh in range(2):
            hi = self.parts[0][:, n, KH * kh:KH * (kh + 1), :, :]
            act.wait_ge(self.loaded[half][kh], 16 * (n + 1))
            act.activation(hi[:, :, 1:3, :], self.stage[:, kh, :, :, :], ACT.Copy)
            act.activation(hi[:, :, 0, :], self.stage[:, kh, :, 1, :], ACT.Copy, scale=-1.0) \
                .then_inc(self.rounded, 1)

    def low(self, eng, half, n, kh):
        hi, lo = (x[:, n, KH * kh:KH * (kh + 1), :, :] for x in self.parts)
        eng.wait_ge(self.rounded, 2 * (N * half + n) + kh + 1)
        eng.tensor_tensor(lo[:, :, 1:3, :], self.stage[:, kh, :, :, :], hi[:, :, 1:3, :].bitcast(F32),
                          ALU.subtract)
        eng.tensor_tensor(lo[:, :, 0, :], hi[:, :, 2, :].bitcast(F32), self.stage[:, kh, :, 1, :],
                          ALU.subtract).then_inc(self.split[kh], 1)


class MeasurementInputs:
    PLACES = 4
    MR, MI, NEG_MI, POST = range(PLACES)

    def __init__(self, ctx, nc, int_w):
        flat = [x[:].rearrange("p n k m e -> p (n k m e)") for x in int_w.parts]
        at = self.PLACES * DK * D
        self.wts = [x[:, 0:at].rearrange("p (w k e) -> p w k e", w=self.PLACES, k=DK) for x in flat]
        self.sup_t = [x[:, at:at + 2 * DK * HALF].rearrange("p (c k x) -> p c k x", c=2, k=DK)
                      for x in flat]
        self.ident = ctx.enter_context(nc.sbuf_tensor("m_ident", [P, P], F32))
        self.eps = ctx.enter_context(nc.sbuf_tensor("m_eps", [P, 1], F32))


def output_projection_phase(nc, t, scr, int_w):
    with ExitStack() as ctx:
        def sb(name, shape, dt=F32):
            return ctx.enter_context(nc.sbuf_tensor(name, shape, dt))

        def sem(name):
            return ctx.enter_context(nc.semaphore(name))

        wts = [sb("wo_hi", [P, 2, DK, D], F32R), sb("wo_lo", [P, 2, DK, D], F32R)]
        o_stage = sb("o_stage", [P, 2, DK, NB])
        o = [sb("o_hi", [P, 2, DK, NB], F32R), sb("o_lo", [P, 2, DK, NB], F32R)]
        attn_sb = sb("attn_sb", [P, 2 * DK, NB])
        wo_stage = attn_sb[:].rearrange("p (c k) x -> p c k x", c=2)
        wo_bias = sb("wo_bias", [P, 2, DK])
        banks = ctx.enter_context(nc.psum_tensor("wo_banks", [P, 2 * DK, NB], F32))

        bias_loaded = sem("wo_bias_loaded")
        wo_loaded = [sem(f"wo_loaded{c}") for c in range(2)]
        wo_rounded = sem("wo_rounded")
        wo_split = sem("wo_split")
        o_loaded = [sem(f"o_loaded{c}") for c in range(2)]
        o_rounded = sem("o_rounded")
        o_split = sem("o_split")
        bank_full = sem("wo_bank_full")
        bank_read = sem("wo_bank_read")
        attn_stored = [sem(f"attn_stored{c}") for c in range(2)]

        block = ctx.enter_context(nc.Block())
        FILLS = 2 * DK

        @block.sync
        def _(sp):
            sp.dma_start(wo_bias[:], t["wo_bias"]).then_inc(bias_loaded, 16)

            def load(tile, c, first=False):
                if not first:
                    sp.wait_ge(o_split, 2 * (tile - 1) + c + 1)
                for a in range(2):
                    sp.dma_start(o_stage[a * HD:(a + 1) * HD, c, :, :],
                                 scr["o"][tile, a::2, c * HD:(c + 1) * HD, :].rearrange("k d x -> d k x")) \
                        .then_inc(o_loaded[c], 16)

            for c in range(2):
                sp.dma_start(wo_stage[:, c, :, :].rearrange("p k e -> p (k e)"), t["wo"][c]) \
                    .then_inc(wo_loaded[c], 16)
                load(0, c, first=True)
            with sp.Fori(1, ROW_TILES) as tile:
                for c in range(2):
                    load(tile, c)

        @block.gpsimd
        def _(pool):
            pool.wait_ge(o_split, 1)
            for kh in range(2):
                int_w.load(pool, t["int_w"], 0, 0, kh)
            for n in range(N):
                for kh in range(2):
                    int_w.low(pool, 0, n, kh)
                    if n + 1 < N:
                        int_w.load(pool, t["int_w"], 0, n + 1, kh)

        @block.vector
        def _(dve):
            def split(stage, parts, rounded, done, count):
                dve.tensor_copy(parts[0], stage).then_inc(rounded, 1)
                dve.wait_ge(rounded, count)
                dve.tensor_tensor(parts[1], stage, parts[0].bitcast(F32), ALU.subtract).then_inc(done, 1)

            dve.sem_inc(bank_full, FILLS)
            def split_o(tile, c):
                dve.wait_ge(o_loaded[c], 32 * (tile + 1))
                dve.wait_ge(bank_full, FILLS * tile + DK * (c + 1))
                split(o_stage[:, c, :, :], [x[:, c, :, :] for x in o], o_rounded, o_split,
                      2 * tile + c + 1)

            for c in range(2):
                dve.wait_ge(wo_loaded[c], 16)
                split(wo_stage[:, c, :, :], [w[:, c, :, :] for w in wts], wo_rounded, wo_split, c + 1)
                split_o(0, c)
            with dve.Fori(1, ROW_TILES) as tile:
                for c in range(2):
                    split_o(tile, c)

        @block.tensor
        def _(pe):
            with pe.Fori(0, ROW_TILES) as tile:
                for c in range(2):
                    pe.wait_ge(wo_split, c + 1)
                    pe.wait_ge(o_split, 2 * tile + c + 1)
                    for et in range(DK):
                        pe.wait_ge(bank_read, FILLS * tile + DK * c + et + 1)
                        n = 0
                        for k in range(DK):
                            for wp, op in PARTS:
                                last = pe.matmul(banks[:, DK * c + et, :],
                                                 wts[wp][:, c, k, et * P:(et + 1) * P], o[op][:, c, k, :],
                                                 start=n == 0, stop=n == 3 * DK - 1)
                                n += 1
                        last.then_inc(bank_full, 1)

        @block.scalar
        def _(act):
            act.sem_inc(bank_read, FILLS)
            for c in range(2):
                act.sem_inc(attn_stored[c], 16)
            act.wait_ge(bias_loaded, 16)

            def project(tile, c):
                act.wait_ge(attn_stored[c], 16 * (tile + 1))
                for et in range(DK):
                    x = DK * c + et
                    act.wait_ge(bank_full, FILLS * (tile + 1) + x + 1)
                    act.activation(attn_sb[:, x, :], banks[:, x, :], ACT.Identity,
                                   bias=wo_bias[:, c, et:et + 1]).then_inc(bank_read, 1)
                act.wait_ge(bank_read, FILLS * (tile + 1) + DK * (c + 1))
                act.dma_start(scr["attn"][tile, c].rearrange("k p x -> p k x"),
                              attn_sb[:, DK * c:DK * (c + 1), :]).then_inc(attn_stored[c], 16)

            for n in range(N):
                for c in range(2):
                    project(n, c)
                int_w.round(act, 0, n)
            with act.Fori(N, ROW_TILES) as tile:
                for c in range(2):
                    project(tile, c)
            for c in range(2):
                act.wait_ge(attn_stored[c], 16 * (ROW_TILES + 1))


PAIRS = ((0, 1), (0, 2), (0, 3), (1, 2), (1, 3), (2, 3))


def interference_phase(nc, t, scr, strength, int_w, meas):
    with ExitStack() as ctx:
        def sb(name, shape, dt=F32):
            return ctx.enter_context(nc.sbuf_tensor(name, shape, dt))

        def sem(name):
            return ctx.enter_context(nc.semaphore(name))

        a_stage = sb("a_stage", [P, 2, KH, NB])
        a = [sb("a_hi", [P, 2, DK, NB], F32R), sb("a_lo", [P, 2, DK, NB], F32R)]
        ri = sb("ri", [P, 2, N, 2, EH])
        unit = sb("unit", [P, N, 2, EH])
        sq = sb("ri_squares", [P, N, 2, EH])
        root = sq[:].rearrange("p n c e -> p (n c e)")[:, 0:N * EH]
        newton = sq[:].rearrange("p n c e -> p (n c e)")[:, N * EH:]
        zero = newton.rearrange("p (n e) -> p n e", n=N)
        mag2 = sb("mag2", [P, N, EH])
        mag2_flat = mag2[:].rearrange("p n e -> p (n e)")
        prod = sb("prod", [P, len(PAIRS), 2, EH])
        cos = prod[:, :, 0, :]
        zeros = sb("pair_zeros", [P, len(PAIRS), EH])
        f = zeros[:, 0:N, :]
        sup = sb("sup", [P, 2, 2, EH])
        s_tile = sb("s_tile", [P, 2, N, N])
        EARLY = ROW_TILES // 2
        m_stage = [int_w.matrix_stage, a_stage[:].rearrange("p j k x -> p (j k x)")]
        early = [x[:, i * 2 * D:(i + 1) * 2 * D].rearrange("p (c e) -> p c e", c=2)
                 for x in (int_w.matrix_stage, ri[:, 0, :, :, :].rearrange("p n c e -> p (n c e)"))
                 for i in range(2)]
        early_norm = sb("early_norm", [P, EARLY])
        unread = sq[:].rearrange("p n c e -> p (n c e)")[:, 0:2 * D]
        tiny = sb("tiny", [P, 1])
        one = sb("one", [P, 1])
        banks = ctx.enter_context(nc.psum_tensor("ri_banks", [P, 2, N, 2, EH], F32))

        a_loaded = [sem(f"a_loaded{kh}") for kh in range(2)]
        a_rounded = sem("a_rounded")
        a_split = sem("a_split")
        part_done = sem("part_done")
        ri_out = sem("ri_out")
        mag2_done = sem("mag2_done")
        root_done = sem("root_done")
        root2_done = sem("root2_done")
        t_done = sem("t_done")
        factor_done = sem("factor_done")
        zero_done = sem("zero_done")
        inverse_done = sem("inverse_done")
        unit_done = sem("unit_done")
        zeros_done = sem("zeros_done")
        tiny_set = sem("tiny_set")
        step_done = sem("step_done")
        mr_mi_loaded = [sem(f"{name}_loaded") for name in ("Mr", "Mi")]
        mr_mi_rounded = sem("mr_mi_rounded")
        mr_mi_split = sem("mr_mi_split")
        early_loaded = sem("early_sup_loaded")
        early_norms = sem("early_norms")
        early_inverted = sem("early_inverted")
        early_scaled = sem("early_scaled")
        early_turned = sem("early_turned")
        early_rounded = sem("early_rounded")
        sup_done = sem("sup_done")
        sup_stored = [sem(f"sup_stored{j}") for j in range(2)]

        ps_turn = [banks[:, i // 2, i % 2 * 2:i % 2 * 2 + 2, :, :].rearrange("p n c e -> p (n c e)")
                   .rearrange("p (c k x) -> p c k x", c=2, k=DK) for i in range(EARLY)]

        def early_parts(tile):
            return [x[:, :, :, tile * P:(tile + 1) * P] for x in meas.sup_t]

        block = ctx.enter_context(nc.Block())

        ROOT_SCALE = float(2 ** 15)
        TINY = 1e-26
        UNITS = 2 * ROW_TILES
        PARTS_DONE = 2 * N

        def units(eng, body, half, end=ROW_TILES):
            with eng.Fori(0, end // 2) as i:
                for j in range(2):
                    body(2 * i + (j + ROW_TILES * half), 2 * i + j, j, half)

        @block.sync
        def _(sp):
            def load_a(unit_no, tile, c, first=False):
                for kh in range(2):
                    if not first:
                        sp.wait_ge(a_split, 4 * unit_no + 2 * c + kh - 1)
                    sp.dma_start(a_stage[:, kh, :, :],
                                 scr["attn"][tile, c, KH * kh:KH * (kh + 1)].rearrange("k p x -> p k x")) \
                        .then_inc(a_loaded[kh], 16)

            def store(unit_no, tile, j, half):
                sp.wait_ge(sup_done, unit_no + 3)
                sp.dma_start(scr["sup"][tile, :, :, half * EH:(half + 1) * EH].rearrange("c p e -> p c e"),
                             sup[:, j, :, :]).then_inc(sup_stored[j], 16)

            def load_early(tile):
                sp.dma_start(early[tile], scr["sup"][tile].rearrange("c p e -> p c e")) \
                    .then_inc(early_loaded, 16)

            def load_and_store(half):
                with sp.Fori(0, ROW_TILES // 2 - 2) as i:
                    for j in range(2):
                        tile = 2 * i + j
                        for c in range(2):
                            load_a(tile + (3 + ROW_TILES * half), tile + 3, c)
                        store(tile + ROW_TILES * half, tile, j, half)
                for c in range(2):
                    load_a(ROW_TILES - 1 + ROW_TILES * half, ROW_TILES - 1, c)
                store(ROW_TILES - 4 + ROW_TILES * half, ROW_TILES - 4, 0, half)

            for j in range(2):
                sp.sem_inc(sup_stored[j], 16)
            load_a(0, 0, 0, first=True)
            load_a(0, 0, 1)
            for tile in (1, 2):
                for c in range(2):
                    load_a(tile, tile, c)
            load_and_store(0)
            load_a(ROW_TILES, 0, 0)
            for n in range(N):
                for kh in range(2):
                    int_w.load(sp, t["int_w"], 1, n, kh)
            load_a(ROW_TILES, 0, 1)
            for tile in range(3):
                if tile:
                    for c in range(2):
                        load_a(ROW_TILES + tile, tile, c)
                store(ROW_TILES - 3 + tile, ROW_TILES - 3 + tile, (1 + tile) % 2, 0)
            load_and_store(1)
            for kh in range(2):
                sp.wait_ge(int_w.split[kh], 2 * N)
            sp.wait_ge(a_split, 4 * UNITS)
            for m, name in enumerate(("w_Mr", "w_Mi")):
                sp.dma_start(m_stage[m], t[name]).then_inc(mr_mi_loaded[m], 16)
            for tile in range(ROW_TILES - 3, ROW_TILES):
                store(ROW_TILES + tile, tile, tile % 2, 1)
                if tile == ROW_TILES - 3:
                    for j in range(2):
                        sp.wait_ge(sup_stored[j], 16 * (1 + ROW_TILES // 2 + EARLY // 2))
                    sp.wait_ge(mr_mi_split, 1)
                    for early_tile in range(2):
                        load_early(early_tile)
                if tile == ROW_TILES - 2:
                    for early_tile in range(2, EARLY):
                        load_early(early_tile)
            for j in range(2):
                sp.wait_ge(sup_stored[j], 16 * (UNITS // 2 + 1))

        @block.gpsimd
        def _(pool):
            def low_a(unit_no, c):
                for kh in range(2):
                    hi, lo = (x[:, c, KH * kh:KH * (kh + 1), :] for x in a)
                    pool.wait_ge(a_rounded, 4 * unit_no + 2 * c + kh + 1)
                    pool.tensor_tensor(lo, a_stage[:, kh, :, :], hi.bitcast(F32), ALU.subtract) \
                        .then_inc(a_split, 1)

            def add_squares(unit_no):
                pool.wait_ge(ri_out, 2 * unit_no + 6)
                pool.wait_ge(unit_done, unit_no + 1)
                pool.tensor_tensor(mag2[:], sq[:, :, 0, :], sq[:, :, 1, :], ALU.add) \
                    .then_inc(mag2_done, 1)

            def pair_zeros(unit_no):
                pool.wait_ge(zero_done, unit_no + 1)
                pool.wait_ge(sup_done, unit_no + 2)
                at = 0
                for i in range(N - 1):
                    n = N - 1 - i
                    last = pool.tensor_tensor(zeros[:, at:at + n, :], zero[:, i + 1:N, :],
                                              zero[:, i, :].unsqueeze(1).broadcast_to([P, n, EH]),
                                              ALU.add)
                    at += n
                last.then_inc(zeros_done, 1)

            pool.memset(tiny[:], TINY).then_inc(tiny_set, 1)
            pool.memset(one[:], 1.0).then_inc(tiny_set, 1)
            pool.memset(meas.eps[:], MAG_EPS).then_inc(tiny_set, 1)
            pool.memset(meas.ident[:], 0.0).then_inc(tiny_set, 1)
            pool.wait_ge(tiny_set, 4)
            pool.affine_select(out=meas.ident[:], in_=meas.ident[:], compare_op=ALU.not_equal,
                               fill=1.0, base=0, pattern=[[-1, P]], channel_multiplier=1) \
                .then_inc(tiny_set, 1)
            pool.sem_inc(zeros_done, 1)
            for c in range(2):
                low_a(0, c)
            with pool.Fori(1, ROW_TILES) as unit_no:
                low_a(unit_no, 0)
                add_squares(unit_no - 1)
                low_a(unit_no, 1)
                pair_zeros(unit_no - 1)
            low_a(ROW_TILES, 0)
            int_w.low(pool, 1, 0, 0)
            int_w.low(pool, 1, 0, 1)
            for n in range(1, N):
                int_w.low(pool, 1, n, 0)
            add_squares(ROW_TILES - 1)
            low_a(ROW_TILES, 1)
            pair_zeros(ROW_TILES - 1)
            with pool.Fori(ROW_TILES + 1, UNITS) as unit_no:
                low_a(unit_no, 0)
                add_squares(unit_no - 1)
                low_a(unit_no, 1)
                pair_zeros(unit_no - 1)
            add_squares(UNITS - 1)

            def low_m(place, *operands):
                pool.tensor_tensor(meas.wts[1][:, place].rearrange("p k e -> p (k e)"), *operands,
                                   ALU.subtract).then_inc(mr_mi_split, 1)

            mr_hi, mi_hi = (meas.wts[0][:, place].rearrange("p k e -> p (k e)").bitcast(F32)
                            for place in (meas.MR, meas.MI))
            pool.wait_ge(mr_mi_rounded, 1)
            low_m(meas.MR, m_stage[0], mr_hi)
            pool.wait_ge(mr_mi_rounded, 2)
            low_m(meas.MI, m_stage[1], mi_hi)
            pair_zeros(UNITS - 1)
            low_m(meas.NEG_MI, mi_hi, m_stage[1])

        @block.tensor
        def _(pe):
            pe.sem_inc(part_done, PARTS_DONE)

            def products(unit_no, tile, j, half):
                pe.wait_ge(ri_out, 2 * unit_no + 2)
                for c in range(2):
                    for n in range(N):
                        for k in range(DK):
                            if half and k % KH == 0:
                                pe.wait_ge(int_w.split[k // KH], N + n + 1)
                            if n == 0 and k % KH == 0:
                                pe.wait_ge(a_split, 4 * unit_no + 2 * c + k // KH + 1)
                            for ap, wp in PARTS:
                                cols = slice(1, 3) if c == 0 else slice(0, 2)
                                last = pe.matmul(banks[:, j, n, :, :].rearrange("p c e -> p (c e)"),
                                                 a[ap][:, c, k, n * P:(n + 1) * P],
                                                 int_w.parts[wp][:, n, k, cols, :]
                                                 .rearrange("p m e -> p (m e)"),
                                                 start=c == 0 and k == 0 and (ap, wp) == PARTS[0],
                                                 stop=c == 1 and k == DK - 1 and (ap, wp) == PARTS[-1])
                        last.then_inc(part_done, 1)

            for half in range(2):
                units(pe, products, half)

            pe.wait_ge(ri_out, 2 * UNITS + 4)
            pe.wait_ge(tiny_set, 5)
            for tile in range(EARLY):
                pe.wait_ge(early_scaled, tile + 1)
                for c in range(2):
                    for k in range(DK):
                        last = pe.transpose(ps_turn[tile][:, c, k, :],
                                            early[tile][:, c, k * P:(k + 1) * P], meas.ident[:])
                last.then_inc(early_turned, 1)

        @block.scalar
        def _(act):
            act.sem_inc(ri_out, 4)

            def round_w(n):
                act.wait_ge(part_done, PARTS_DONE * (ROW_TILES + 1) - N + n + 1)
                int_w.round(act, 1, n)

            def round_a(unit_no, c):
                act.wait_ge(part_done, PARTS_DONE * unit_no + N * (c + 1))
                for kh in range(2):
                    act.wait_ge(a_loaded[kh], 16 * (2 * unit_no + c + 1))
                    act.activation(a[0][:, c, KH * kh:KH * (kh + 1), :], a_stage[:, kh, :, :],
                                   ACT.Copy).then_inc(a_rounded, 1)

            def read(unit_no, tile, j, half, ahead=True):
                act.wait_ge(sup_done, unit_no + 1)
                act.activation(s_tile[:, j, :, :].rearrange("p i j -> p (i j)"),
                               strength[:, bass.ds(tile, 1), :, :].rearrange("p t i j -> p (t i j)"),
                               ACT.Copy)
                for pair in range(2):
                    states = slice(2 * pair, 2 * pair + 2)
                    act.wait_ge(part_done, PARTS_DONE * (unit_no + 1) + N + 2 * (pair + 1))
                    act.activation(ri[:, j, states, :, :], banks[:, j, states, :, :], ACT.Copy)
                    if pair == 0:
                        act.wait_ge(inverse_done, unit_no + 1)
                        act.wait_ge(zeros_done, unit_no + 1)
                    act.activation(sq[:, states, :, :], banks[:, j, states, :, :], ACT.Square) \
                        .then_inc(ri_out, 1)
                if ahead:
                    round_a(unit_no + 1, 1)
                else:
                    round_m(0, meas.MR)
                act.wait_ge(mag2_done, unit_no + 1)
                act.activation(root, mag2_flat, ACT.Abs_reciprocal_sqrt, scale=ROOT_SCALE ** 2,
                               bias=tiny[:]).then_inc(root_done, 1)
                act.wait_ge(root_done, unit_no + 1)
                act.activation(newton, root, ACT.Square, scale=ROOT_SCALE).then_inc(root2_done, 1)
                if not ahead:
                    round_m(1, meas.MI)
                act.wait_ge(t_done, unit_no + 1)
                act.activation(mag2_flat, newton, ACT.Copy, scale=-0.5 * ROOT_SCALE,
                               bias=1.5 * ROOT_SCALE).then_inc(factor_done, 1)
                act.wait_ge(factor_done, unit_no + 1)
                act.activation(newton, newton, ACT.Relu, scale=-2.0, bias=one[:]) \
                    .then_inc(zero_done, 1)

            def unit_and_next(unit_no, tile, j, half):
                read(unit_no, tile, j, half)
                round_a(unit_no + 2, 0)

            def round_m(m, place, scale=1.0):
                act.wait_ge(mr_mi_loaded[m], 16)
                act.activation(meas.wts[0][:, place].rearrange("p k e -> p (k e)"), m_stage[m],
                               ACT.Copy, scale=scale).then_inc(mr_mi_rounded, 1)

            act.wait_ge(tiny_set, 3)
            round_a(0, 0)
            round_a(0, 1)
            round_a(1, 0)
            units(act, unit_and_next, 0, ROW_TILES - 2)
            unit_and_next(ROW_TILES - 2, ROW_TILES - 2, 0, 0)
            for n in range(N):
                round_w(n)
            unit_and_next(ROW_TILES - 1, ROW_TILES - 1, 1, 0)
            units(act, unit_and_next, 1, ROW_TILES - 2)
            read(UNITS - 2, ROW_TILES - 2, 0, 1)
            read(UNITS - 1, ROW_TILES - 1, 1, 1, ahead=False)

            round_m(1, meas.NEG_MI, -1.0)
            act.wait_ge(early_loaded, 16 * EARLY)
            act.wait_ge(inverse_done, UNITS + 1)
            for tile in range(EARLY):
                if tile:
                    act.wait_ge(early_norms, tile)
                act.activation(unread, early[tile].rearrange("p c e -> p (c e)"), ACT.Square,
                               accum_out=early_norm[:, tile:tile + 1]).then_inc(early_norms, 1)
            act.wait_ge(early_norms, EARLY)
            act.activation(early_norm[:], early_norm[:], ACT.Sqrt, bias=meas.eps[:]) \
                .then_inc(early_norms, 1)
            act.wait_ge(early_inverted, 1)
            for tile in range(EARLY):
                act.activation(early[tile], early[tile], ACT.Copy,
                               scale=early_norm[:, tile:tile + 1]).then_inc(early_scaled, 1)
            for tile in range(EARLY):
                act.wait_ge(early_turned, tile + 1)
                act.activation(early_parts(tile)[0], ps_turn[tile], ACT.Copy) \
                    .then_inc(early_rounded, 1)

        @block.vector
        def _(dve):
            dve.sem_inc(sup_done, 2)
            dve.sem_inc(inverse_done, 1)
            dve.sem_inc(unit_done, 1)

            def newton_t(unit_no):
                dve.wait_ge(root2_done, unit_no + 1)
                dve.tensor_tensor(newton, newton, mag2_flat, ALU.mult).then_inc(t_done, 1)

            def superpose(unit_no, tile, j, half, ahead=True, last=False):
                STEPS = 8
                count = [0]

                def step(*instructions):
                    instructions[-1].then_inc(step_done, 1)
                    count[0] += 1
                    dve.wait_ge(step_done, STEPS * unit_no + count[0])

                def by_part(x, n):
                    return x.unsqueeze(2).broadcast_to([P, n, 2, EH])

                z = ri[:, j, :, :, :]
                dve.wait_ge(factor_done, unit_no + 1)
                dve.tensor_tensor(mag2_flat, root, mag2_flat, ALU.mult).then_inc(inverse_done, 1)
                dve.wait_ge(inverse_done, unit_no + 2)
                dve.wait_ge(sup_done, unit_no + 2)
                dve.tensor_tensor(unit[:], z, by_part(mag2[:], N), ALU.mult).then_inc(unit_done, 1)
                dve.wait_ge(unit_done, unit_no + 2)
                at, made = 0, []
                for i in range(N - 1):
                    n = N - 1 - i
                    made.append(dve.tensor_tensor(
                        prod[:, at:at + n, :, :], unit[:, i + 1:N, :, :],
                        unit[:, i, :, :].unsqueeze(1).broadcast_to([P, n, 2, EH]), ALU.mult))
                    at += n
                step(*made)
                step(dve.tensor_tensor(cos, cos, prod[:, :, 1, :], ALU.add))
                dve.wait_ge(zeros_done, unit_no + 2)
                step(dve.tensor_tensor(cos, cos, zeros[:], ALU.add))
                others = [[i for i in range(N) if i != m] for m in range(N)]

                def cosine(i, m):
                    return prod[:, PAIRS.index((min(i, m), max(i, m))), 0, :]

                step(*[dve.tensor_scalar(f[:, m, :], cosine(others[m][0], m),
                                         s_tile[:, j, others[m][0], m:m + 1],
                                         s_tile[:, j, m, m:m + 1],
                                         ALU.mult, ALU.add) for m in range(N)])
                for o in (1, 2):
                    step(*[dve.scalar_tensor_tensor(f[:, m, :], cosine(others[m][o], m),
                                                    s_tile[:, j, others[m][o], m:m + 1], f[:, m, :],
                                                    ALU.mult, ALU.add) for m in range(N)])
                    if last and o == 1:
                        dve.wait_ge(early_norms, EARLY + 1)
                        dve.reciprocal(early_norm[:], early_norm[:]).then_inc(early_inverted, 1)
                made = dve.tensor_tensor(unit[:], z, by_part(f, N), ALU.mult)
                if ahead:
                    newton_t(unit_no + 1)
                step(made)
                step(dve.tensor_tensor(unit[:, 0:2, :, :], unit[:, 0:2, :, :], unit[:, 2:4, :, :],
                                       ALU.add))
                assert count[0] == STEPS
                dve.wait_ge(sup_stored[j], 8 * unit_no + 16 - 8 * j)
                dve.tensor_tensor(sup[:, j, :, :], unit[:, 0, :, :], unit[:, 1, :, :], ALU.add) \
                    .then_inc(sup_done, 1)

            newton_t(0)
            units(dve, superpose, 0, ROW_TILES - 2)
            superpose(ROW_TILES - 2, ROW_TILES - 2, 0, 0, ahead=False)
            for n in range(1, N):
                int_w.low(dve, 1, n, 1)
            newton_t(ROW_TILES - 1)
            superpose(ROW_TILES - 1, ROW_TILES - 1, 1, 0)
            units(dve, superpose, 1, ROW_TILES - 2)
            superpose(UNITS - 2, ROW_TILES - 2, 0, 1)
            superpose(UNITS - 1, ROW_TILES - 1, 1, 1, ahead=False, last=True)
            for tile in range(EARLY):
                dve.wait_ge(early_rounded, tile + 1)
                hi, lo = early_parts(tile)
                dve.tensor_tensor(lo, ps_turn[tile], hi.bitcast(F32), ALU.subtract)


def top_phase(nc, t, scr, out, meas, w_stage):
    with ExitStack() as ctx:
        def sb(name, shape, dt=F32):
            return ctx.enter_context(nc.sbuf_tensor(name, shape, dt))

        def sem(name):
            return ctx.enter_context(nc.semaphore(name))

        TILES_HALF = ROW_TILES // 2
        MR, MI, NEG_MI, POST = range(meas.PLACES)
        LOADS = ("post", "top1", "top2")
        PLACES = (POST, MR, MI)
        TOP2_WIDTH = D // 2
        wts = meas.wts
        w3 = sb("w3", [P, 2])
        sup = sb("top_sup", [P, 2, 2, D])
        norm = sb("norm", [P, ROW_TILES])
        unread = sb("unread", [P, 2 * D])
        sup_t = [meas.sup_t, [sb(f"sup_t_{part}", [P, 2, DK, HALF], F32R) for part in ("hi", "lo")]]
        amp_0 = [sb(f"amp_0_{part}", [P, DK, HALF], F32R) for part in ("hi", "lo")]
        amp_t = [[x[:] for x in amp_0], [x[:, 0, :, :] for x in sup_t[0]]]
        z_t = [[x[:, 1, :, :] for x in sup_t[0]], [x[:, 0, :, :] for x in sup_t[1]]]
        h1_t = [[x[:, 1, :, :] for x in sup_t[1]], [x[:] for x in amp_0]]
        sq = sb("top_sq", [P, 2, 2, HALF])
        amp = sb("amp", [P, 2, HALF])
        y = sb("y", [P, DK, B])
        y_sum = sb("y_sum", [P, B])
        x_part = sb("x_part", [P, 2, HALF])
        mats = [[x[:, place, :, 0:TOP2_WIDTH if name == "top2" else D] for x in wts]
                for name, place in zip(LOADS, PLACES)]
        stages = [y[:, :, D:2 * D], w_stage.rearrange("p (k e) -> p k e", k=DK),
                  w_stage[:, 0:DK * TOP2_WIDTH].rearrange("p (k e) -> p k e", k=DK)]
        h2 = y[:, 0:2, :]
        y_out = y_sum[0:1, :]
        cols = sb("top_cols", [P, 3 * DK + 2])
        eps_ln = sb("top_eps", [P, 1])
        averager = sb("top_averager", [P, P])
        ps_turn = ctx.enter_context(nc.psum_tensor("ps_turn", [P, 2, DK, P], F32))
        banks = ctx.enter_context(nc.psum_tensor("top_banks", [P, 4, HALF], F32))
        ps_sum = ctx.enter_context(nc.psum_tensor("ps_sum", [P, 2, HALF], F32))

        cols_loaded = sem("cols_loaded")
        consts_set = sem("t_consts_set")
        tw_loaded = [sem(f"{name}_loaded") for name in LOADS]
        tw_rounded = sem("tw_rounded")
        tw_split = [sem(f"{name}_split") for name in LOADS]
        sup_loaded = [sem(f"sup_loaded{j}") for j in range(2)]
        norm2_done = sem("norm2_done")
        norm_done = sem("norm_done")
        scaled = sem("scaled")
        turned = sem("sup_turned")
        sup_rounded = sem("sup_rounded")
        sup_split = sem("sup_split")
        filled = sem("bank_filled")
        act_read = sem("act_read")
        dve_read = sem("dve_read")
        amp2_done = sem("amp2_done")
        amp_done = sem("amp_done")
        amp_split = sem("amp_split")
        dve_step = sem("dve_step")
        summed = sem("summed")
        averaged = sem("averaged")
        less_mean = sem("less_mean")
        squared = sem("t_squared")
        std_done = sem("t_std_done")
        z_done = sem("t_z_done")
        gelu_done = sem("t_gelu_done")
        z_split = sem("z_split")
        x_loaded = [sem(f"x_loaded{j}") for j in range(2)]
        h1_split = sem("h1_split")
        y_done = sem("y_done")
        y_read = sem("y_read")
        y_stored = sem("y_stored")

        block = ctx.enter_context(nc.Block())

        MEAS_FILLS, POST_FILLS, TOP1_FILLS = 4 * DK, 2 * DK, 2 * DK
        AT_POST = MEAS_FILLS
        AT_TOP1 = AT_POST + POST_FILLS
        AT_TOP2 = AT_TOP1 + TOP1_FILLS

        def rows(h):
            return slice(h * HALF, (h + 1) * HALF)

        @block.sync
        def _(sp):
            sp.dma_start(cols[:], t["top_cols"]).then_inc(cols_loaded, 16)
            sp.dma_start(w3[:], t["w_top3"]).then_inc(cols_loaded, 16)

            def load_sup(tile):
                if tile >= TILES_HALF + 2:
                    sp.wait_ge(turned, tile - TILES_HALF - 1)
                sp.dma_start(sup[:, tile % 2, :, :], scr["sup"][tile].rearrange("c p e -> p c e")) \
                    .then_inc(sup_loaded[tile % 2], 16)

            def load_w(m):
                if m == 2:
                    sp.wait_ge(tw_split[1], 1)
                sp.dma_start(stages[m], t["w_" + LOADS[m]].rearrange("p (k e) -> p k e", k=DK)) \
                    .then_inc(tw_loaded[m], 16)

            load_sup(TILES_HALF)
            load_sup(TILES_HALF + 1)
            load_w(0)
            for tile in range(TILES_HALF + 2, ROW_TILES):
                load_sup(tile)
            load_w(1)
            load_w(2)
            for h in range(2):
                for et in range(DK):
                    x = DK * h + et
                    if x >= 2:
                        sp.wait_ge(dve_read, x - 1)
                    sp.dma_start(x_part[:, x % 2, :], scr["u"][2 * ENC_TILES + et, :, rows(h)]) \
                        .then_inc(x_loaded[x % 2], 16)
            sp.wait_ge(y_read, 2)
            sp.dma_start(out.rearrange("b x -> x b"), y_out).then_inc(y_stored, 16)
            sp.wait_ge(y_stored, 16)

        @block.gpsimd
        def _(pool):
            pool.memset(averager[:], 1.0 / P).then_inc(consts_set, 1)
            pool.memset(eps_ln[:], LN_EPS).then_inc(consts_set, 1)
            for m, (hi, lo) in enumerate(mats):
                pool.wait_ge(tw_rounded, m + 1)
                pool.tensor_tensor(lo, stages[m], hi.bitcast(F32), ALU.subtract) \
                    .then_inc(tw_split[m], 1)

        @block.tensor
        def _(pe):
            def turn(tile):
                n = tile - TILES_HALF
                pe.wait_ge(scaled, n + 1)
                if n:
                    pe.wait_ge(sup_split, n)
                for c in range(2):
                    for k in range(DK):
                        last = pe.transpose(ps_turn[:, c, k, :], sup[:, tile % 2, c, k * P:(k + 1) * P],
                                            meas.ident[:])
                last.then_inc(turned, 1)

            def fill(x, terms, et):
                before = x - 4
                if before >= AT_TOP2:
                    pe.wait_ge(act_read, AT_TOP1 + before - AT_TOP2 + 1)
                elif before >= AT_TOP1:
                    pe.wait_ge(dve_read, before - AT_TOP1 + 1)
                elif before >= 0:
                    pe.wait_ge(act_read, before + 1)
                all_mm = [(wts[wp][:, place, k, et * P:(et + 1) * P], mov[mp][:, k, :])
                          for place, mov in terms for k in range(DK) for wp, mp in PARTS]
                for n, (lhs, rhs) in enumerate(all_mm):
                    last = pe.matmul(banks[:, x % 4, :], lhs, rhs, start=n == 0,
                                     stop=n == len(all_mm) - 1)
                last.then_inc(filled, 1)

            def average(h, number):
                pe.wait_ge(summed, number + 1)
                pe.matmul(ps_sum[:, h, :], averager[:], y_sum[:, rows(h)], start=True, stop=True) \
                    .then_inc(averaged, 1)

            for h in range(2):
                if h:
                    pe.wait_ge(sup_split, TILES_HALF)
                real, imag = ([x[:, c, :, :] for x in sup_t[h]] for c in range(2))
                for et in range(DK):
                    fill(2 * DK * h + 2 * et, [(MR, real), (NEG_MI, imag)], et)
                    fill(2 * DK * h + 2 * et + 1, [(MI, real), (MR, imag)], et)
                    if h == 0:
                        turn(TILES_HALF + et)
            pe.wait_ge(consts_set, 2)
            pe.wait_ge(tw_split[0], 1)
            for h in range(2):
                pe.wait_ge(amp_split, DK * (h + 1))
                for et in range(DK):
                    fill(AT_POST + DK * h + et, [(POST, amp_t[h])], et)
                    if h == 1 and et == 0:
                        average(0, 0)
            for number, h in ((1, 0), (2, 1), (3, 1)):
                average(h, number)
            pe.wait_ge(tw_split[1], 1)
            pe.wait_ge(tw_split[2], 1)
            for h in range(2):
                pe.wait_ge(z_split, h + 1)
                for et in range(DK):
                    fill(AT_TOP1 + DK * h + et, [(MR, z_t[h])], et)
            for h in range(2):
                pe.wait_ge(h1_split, DK * (h + 1))
                for et in range(2):
                    fill(AT_TOP2 + 2 * h + et, [(MI, h1_t[h])], et)
            pe.wait_ge(cols_loaded, 32)
            for h in range(2):
                pe.wait_ge(act_read, AT_TOP1 + 2 * (h + 1))
                for k in range(2):
                    last = pe.matmul(ps_sum[0:1, h, :], w3[:, k:k + 1], h2[:, k, rows(h)],
                                     start=k == 0, stop=k == 1)
                last.then_inc(y_done, 1)

        @block.scalar
        def _(act):
            def norms(tile):
                n = tile - TILES_HALF
                act.wait_ge(sup_loaded[tile % 2], 16 * (n // 2 + 1))
                act.activation(unread[:],
                               sup[:, tile % 2, :, :].rearrange("p c e -> p (c e)"), ACT.Square,
                               accum_out=norm[:, tile:tile + 1]).then_inc(norm2_done, 1)
                act.wait_ge(norm2_done, n + 1)
                act.activation(norm[:, tile:tile + 1], norm[:, tile:tile + 1], ACT.Sqrt,
                               bias=meas.eps[:]).then_inc(norm_done, 1)

            def round_sup(tile):
                act.wait_ge(turned, tile - TILES_HALF + 1)
                h, at = tile // TILES_HALF, tile % TILES_HALF * P
                act.activation(sup_t[h][0][:, :, :, at:at + P], ps_turn[:], ACT.Copy) \
                    .then_inc(sup_rounded, 1)

            def squares(x):
                if x >= 4:
                    act.wait_ge(amp2_done, x // 2 - 1)
                act.wait_ge(filled, x + 1)
                act.activation(sq[:, x // 2 % 2, x % 2, :], banks[:, x % 4, :], ACT.Square) \
                    .then_inc(act_read, 1)

            def root(n):
                act.wait_ge(amp2_done, n + 1)
                act.activation(amp[:, n % 2, :], amp[:, n % 2, :], ACT.Sqrt).then_inc(amp_done, 1)

            def round_weights(m):
                act.wait_ge(tw_loaded[m], 16)
                act.activation(mats[m][0], stages[m], ACT.Copy).then_inc(tw_rounded, 1)

            act.wait_ge(consts_set, 2)
            act.wait_ge(cols_loaded, 32)
            for n in range(2 * DK):
                if n < TILES_HALF:
                    norms(TILES_HALF + n)
                squares(2 * n)
                squares(2 * n + 1)
                if n:
                    root(n - 1)
                if n < TILES_HALF:
                    round_sup(TILES_HALF + n)
                if n == TILES_HALF - 1:
                    round_weights(0)
            root(2 * DK - 1)
            round_weights(1)

            def read_post(h, et):
                x = AT_POST + DK * h + et
                act.wait_ge(filled, x + 1)
                act.activation(y[:, et, rows(h)], banks[:, x % 4, :], ACT.Identity,
                               bias=cols[:, et:et + 1]).then_inc(act_read, 1)

            def square(h):
                act.wait_ge(less_mean, h + 1)
                if h:
                    act.wait_ge(summed, 3)
                act.activation(sq[:].rearrange("p a c x -> p (a c) x"), y[:, :, rows(h)],
                               ACT.Square).then_inc(squared, 1)

            def std(h):
                act.wait_ge(averaged, 2 * (h + 1))
                act.activation(amp[:, h, :], ps_sum[:, h, :], ACT.Sqrt, scale=1.0 / DK,
                               bias=eps_ln[:]).then_inc(std_done, 1)

            def gelu(h):
                act.wait_ge(z_done, h + 1)
                for et in range(DK):
                    last = act.activation(y[:, et, rows(h)], y[:, et, rows(h)], ACT.Gelu,
                                          scale=cols[:, DK + et:DK + et + 1],
                                          bias=cols[:, 2 * DK + et:2 * DK + et + 1])
                last.then_inc(gelu_done, 1)

            for et in range(DK):
                read_post(0, et)
            round_weights(2)
            for et in range(2):
                read_post(1, et)
            square(0)
            for et in range(2, DK):
                read_post(1, et)
            std(0)
            gelu(0)
            square(1)
            std(1)
            gelu(1)
            for h in range(2):
                for et in range(2):
                    x = AT_TOP2 + 2 * h + et
                    act.wait_ge(filled, x + 1)
                    act.activation(h2[:, et, rows(h)], banks[:, x % 4, :], ACT.Relu,
                                   bias=cols[:, 3 * DK + et:3 * DK + et + 1]).then_inc(act_read, 1)
            for h in range(2):
                act.wait_ge(y_done, h + 1)
                act.activation(y_out[:, rows(h)], ps_sum[0:1, h, :], ACT.Copy).then_inc(y_read, 1)

        @block.vector
        def _(dve):
            steps = [0]

            def step(instruction):
                steps[0] += 1
                instruction.then_inc(dve_step, 1)
                dve.wait_ge(dve_step, steps[0])

            def scale(tile):
                dve.wait_ge(norm_done, tile - TILES_HALF + 1)
                step(dve.reciprocal(norm[:, tile:tile + 1], norm[:, tile:tile + 1]))
                tile_sup = sup[:, tile % 2, :, :]
                dve.tensor_scalar(tile_sup, tile_sup, norm[:, tile:tile + 1], None, ALU.mult) \
                    .then_inc(scaled, 1)

            def low_sup(tile):
                dve.wait_ge(sup_rounded, tile - TILES_HALF + 1)
                h, at = tile // TILES_HALF, tile % TILES_HALF * P
                hi, lo = (x[:, :, :, at:at + P] for x in sup_t[h])
                dve.tensor_tensor(lo, ps_turn[:], hi.bitcast(F32), ALU.subtract).then_inc(sup_split, 1)

            def add_squares(n):
                dve.wait_ge(act_read, 2 * n + 2)
                dve.tensor_tensor(amp[:, n % 2, :], sq[:, n % 2, 0, :], sq[:, n % 2, 1, :], ALU.add) \
                    .then_inc(amp2_done, 1)

            def split_amp(n):
                h, et = n // DK, n % DK
                hi, lo = (x[:, et, :] for x in amp_t[h])
                dve.wait_ge(amp_done, n + 1)
                step(dve.tensor_copy(hi, amp[:, n % 2, :]))
                dve.tensor_tensor(lo, amp[:, n % 2, :], hi.bitcast(F32), ALU.subtract) \
                    .then_inc(amp_split, 1)

            for n in range(2 * DK):
                if n < TILES_HALF:
                    scale(TILES_HALF + n)
                if n >= 2:
                    dve.wait_ge(amp_split, n - 1)
                add_squares(n)
                if n:
                    split_amp(n - 1)
                if n < TILES_HALF:
                    low_sup(TILES_HALF + n)
            split_amp(2 * DK - 1)

            def over_tiles(x):
                return x.unsqueeze(1).broadcast_to([P, DK, HALF])

            def sum_features(h):
                dve.wait_ge(act_read, AT_POST + DK * (h + 1))
                step(dve.tensor_tensor(sq[:, 0, :, :], y[:, 0:2, rows(h)], y[:, 2:4, rows(h)], ALU.add))
                dve.tensor_tensor(y_sum[:, rows(h)], sq[:, 0, 0, :], sq[:, 0, 1, :], ALU.add) \
                    .then_inc(summed, 1)
                dve.wait_ge(summed, 2 * h + 1)

            def subtract_mean(h):
                dve.wait_ge(averaged, 2 * h + 1)
                step(dve.tensor_scalar(y_sum[:, rows(h)], ps_sum[:, h, :], 1.0 / DK, None, ALU.mult))
                dve.tensor_tensor(y[:, :, rows(h)], y[:, :, rows(h)], over_tiles(y_sum[:, rows(h)]),
                                  ALU.subtract).then_inc(less_mean, 1)

            def sum_squares(h):
                dve.wait_ge(less_mean, h + 1)
                dve.wait_ge(squared, h + 1)
                step(dve.tensor_tensor(sq[:, 0, :, :], sq[:, 0, :, :], sq[:, 1, :, :], ALU.add))
                dve.tensor_tensor(y_sum[:, rows(h)], sq[:, 0, 0, :], sq[:, 0, 1, :], ALU.add) \
                    .then_inc(summed, 1)
                dve.wait_ge(summed, 2 * h + 2)

            def normalise(h):
                dve.wait_ge(std_done, h + 1)
                step(dve.reciprocal(amp[:, h, :], amp[:, h, :]))
                dve.tensor_tensor(y[:, :, rows(h)], y[:, :, rows(h)], over_tiles(amp[:, h, :]),
                                  ALU.mult).then_inc(z_done, 1)

            def split_z(h):
                dve.wait_ge(gelu_done, h + 1)
                step(dve.tensor_copy(z_t[h][0], y[:, :, rows(h)]))
                dve.tensor_tensor(z_t[h][1], y[:, :, rows(h)], z_t[h][0].bitcast(F32), ALU.subtract) \
                    .then_inc(z_split, 1)

            sum_features(0)
            subtract_mean(0)
            sum_squares(0)
            sum_features(1)
            normalise(0)
            subtract_mean(1)
            split_z(0)
            sum_squares(1)
            normalise(1)
            split_z(1)
            for h in range(2):
                for et in range(DK):
                    n = DK * h + et
                    x = AT_TOP1 + n
                    hi, lo = (v[:, et, :] for v in h1_t[h])
                    added = sq[:, n % 2, 0, :]
                    dve.wait_ge(filled, x + 1)
                    dve.wait_ge(x_loaded[n % 2], 16 * (n // 2 + 1))
                    if n >= 2:
                        dve.wait_ge(h1_split, n - 1)
                    dve.tensor_tensor(added, banks[:, x % 4, :], x_part[:, n % 2, :], ALU.add) \
                        .then_inc(dve_read, 1)
                    dve.wait_ge(dve_read, n + 1)
                    step(dve.tensor_scalar(hi, added, 0.0, None, ALU.max))
                    dve.scalar_tensor_tensor(lo, added, 0.0, hi.bitcast(F32), ALU.max, ALU.subtract) \
                        .then_inc(h1_split, 1)


def build(nc, t, out):
    scr = {"u": nc.dram_tensor("u_scratch", [ALL_TILES, P, B], F32, kind="Internal").ap(),
           "h": nc.dram_tensor("h_scratch", [2 * ENC_TILES, P, B], F32, kind="Internal").ap()}
    scr["o"] = nc.dram_tensor("o_scratch", [ROW_TILES, HEADS, P, NB], F32, kind="Internal").ap()
    scr["attn"] = nc.dram_tensor("attn_scratch", [ROW_TILES, 2, DK, P, NB], F32, kind="Internal").ap()
    scr["sup"] = nc.dram_tensor("sup_scratch", [ROW_TILES, 2, P, D], F32, kind="Internal").ap()
    encoders_phase(nc, t, scr)
    with nc.sbuf_tensor("strength", [P, ROW_TILES, N, N], F32) as strength:
        attention_phase(nc, t, scr, strength)
        with ExitStack() as ctx:
            int_w = InterferenceWeights(ctx, nc)
            output_projection_phase(nc, t, scr, int_w)
            meas = MeasurementInputs(ctx, nc, int_w)
            interference_phase(nc, t, scr, strength, int_w, meas)
            top_phase(nc, t, scr, out, meas, int_w.matrix_stage)


def _layouts(i):
    f = {k: np.asarray(v) for k, v in i.items()}

    def cols(*vectors):
        return np.concatenate([v.reshape(-1, P).T for v in vectors], axis=1)

    def lhs_tiles(*mats):
        m = np.concatenate(mats, axis=1)
        return m.reshape(m.shape[0] // P, P, -1, P).transpose(2, 1, 0, 3).reshape(-1, P, m.shape[0])

    def rhs(w):
        return w.T.reshape(-1, P, w.shape[0]).transpose(1, 0, 2).reshape(P, -1)

    e = "L0_rec_"
    bq_r, bk_r, bq_i, bk_i = (f[e + b].reshape(DK, P).T for b in ("bq_r", "bk_r", "bq_i", "bk_i"))
    return {
        "qkv": np.stack([rhs(f[e + w]) for w in ("Wq_r", "Wk_r", "Wq_i", "Wk_i", "Wv_r", "Wv_i")]),
        "qk_bias": np.stack([bq_r, bk_r, bq_i, bk_i], axis=1),
        "wo": np.stack([rhs(f[e + w]) for w in ("Wo_r", "Wo_i")]),
        "wo_bias": np.stack([f[e + b].reshape(DK, P).T for b in ("bo_r", "bo_i")], axis=1),
        "int_w": np.stack([f[e + w].reshape(N, 2, EH, DK, P) for w in ("int_Wr", "int_Wi")])
        .transpose(2, 1, 5, 4, 0, 3).reshape(2, N, P, -1),
        "ids": f["ids"].reshape(ROW_TILES, P, N).transpose(1, 0, 2),
        **{f"tbl_{n}": f[f"tbl_{n}"] for n in range(N)},
        "w_Mr": rhs(f[e + "meas_Mr"]),
        "w_Mi": rhs(f[e + "meas_Mi"]),
        "w_post": rhs(f[e + "post_W"]),
        "w_top1": rhs(f["W_top1"][:D].T),
        "w_top2": rhs(f["W_top2"].T),
        "w_top3": f["W_top3"].reshape(2, P).T,
        "top_cols": cols(f[e + "post_b"], f[e + "post_g"], f[e + "post_be"], f["b_top2"]),
        "v_bias": np.concatenate([f[e + "bv_r"].reshape(HEADS, HD).T, f[e + "bv_i"].reshape(HEADS, HD).T]),
        "x_t": f["r_x"].T.reshape(KT, P, B),
        "w_enc": lhs_tiles(f[e + "er_W1"].T, f[e + "ei_W1"].T, f["W_top1"][D:],
                           f[e + "er_W2"].T, f[e + "ei_W2"].T),
        "enc_bias": cols(f[e + "er_b1"], f[e + "ei_b1"], f["b_top1"], f[e + "er_b2"], f[e + "ei_b2"]),
        "ln_g": cols(f[e + "er_g1"], f[e + "ei_g1"]),
        "ln_b": cols(f[e + "er_be1"], f[e + "ei_be1"]),
    }


def kernel(**inputs):
    import concourse.bacc as bacc
    from concourse.bass_utils import run_bass_kernel_spmd

    nc = bacc.Bacc("TRN2", target_bir_lowering=False, num_devices=1)
    arrays, t = {}, {}
    for name, a in _layouts(inputs).items():
        a = np.ascontiguousarray(a)
        arrays[f"in_{name}"] = a
        t[name] = nc.dram_tensor(f"in_{name}", a.shape, mybir.dt.from_np(a.dtype),
                                 kind="ExternalInput").ap()
    out = nc.dram_tensor("out_y", (B, 1), F32, kind="ExternalOutput").ap()
    build(nc, t, out)
    r = run_bass_kernel_spmd(nc, [arrays], core_ids=[0])
    return r.results[0]["out_y"]
```
